# Optimizing a Trainium2 kernel written in Bass

```python
import numpy as np
import jax
import jax.numpy as jnp

def _softmax(x, axis=-1):
    return jax.nn.softmax(x, axis=axis)

def _gelu(x):
    return jax.nn.gelu(x, approximate=True)

def _silu(x):
    return jax.nn.silu(x)

def _sigmoid(x):
    return jax.nn.sigmoid(x)

def _layernorm(x, axis=-1, eps=1e-05):
    m = jnp.mean(x, axis=axis, keepdims=True)
    v = jnp.var(x, axis=axis, keepdims=True)
    return (x - m) / jnp.sqrt(v + eps)

def _scatter_add(tgt, idx, src, axis=0):
    return tgt.at[idx].add(src)

def _segment_sum(src, seg, n):
    return jax.ops.segment_sum(src, seg, n)
kernel_name = 'mk_xattn_seq_d2_seqx_r4_cfc19e'

def setup_inputs(seed: int=0):
    np.random.seed(seed)
    _w = jnp.asarray

    def _rec_inputs():
        import jax
        import jax.numpy as jnp
        _rk = jax.random.key(seed)
        x = -0.0003929 + 0.9999 * jax.random.normal(jax.random.fold_in(_rk, 1), (16, 112, 512), jnp.float32)
        _lenS = 112 - jax.random.randint(jax.random.fold_in(_rk, 7), (16,), 0, max(1, 112 // 4) + 1, jnp.int32)
        _lenS2 = 375 - jax.random.randint(jax.random.fold_in(_rk, 8), (16,), 0, max(1, 375 // 4) + 1, jnp.int32)
        _ctx_2048P = jax.random.normal(jax.random.fold_in(_rk, 11), (16, 16, 512), jnp.float32)
        _ctx_2048c = jax.random.dirichlet(jax.random.fold_in(_rk, 511), 0.3 * jnp.ones((16,), jnp.float32), (16, 375))
        _ctx_2048t = jnp.einsum('bsk,bkd->bsd', _ctx_2048c, _ctx_2048P)
        _ctx_2048t = _ctx_2048t * jax.lax.rsqrt(jnp.mean(jnp.square(_ctx_2048t)) + 1e-12) * 0.953939
        ctx_2048 = -8.57375e-05 + 0.999917 * (_ctx_2048t + 0.3 * jax.random.normal(jax.random.fold_in(_rk, 611), (16, 375, 512), jnp.float32))
        _validS = jnp.arange(112)[None, :] < _lenS[:, None]
        _validS2 = jnp.arange(375)[None, :] < _lenS2[:, None]
        _causal = jnp.tril(jnp.ones((112, 112), dtype=bool))
        mask_BxS2_bf1 = jnp.ones((16, 375), dtype=bool)
        return (x, ctx_2048, mask_BxS2_bf1)
    x, ctx_2048, mask_BxS2_bf1 = _rec_inputs()

    def _L0_xattn_setup():
        import jax, jax.numpy as jnp
        import numpy as np
        HIDDEN = 512
        HEADS = 16
        HEAD_DIM = HIDDEN // HEADS
        LN_EPS = 1e-05
        GATE_INIT = 0.5

        def _layer_norm(x, gamma, beta):
            mu = jnp.mean(x, axis=-1, keepdims=True)
            var = jnp.mean(jnp.square(x - mu), axis=-1, keepdims=True)
            return (x - mu) * jax.lax.rsqrt(var + LN_EPS) * gamma + beta
        key = jax.random.key(seed)
        ks = jax.random.split(key, 8)
        B, T_TEXT, T_AUDIO = (4, 512, 375)
        s = 0.02
        return {'hidden_states': jax.random.normal(ks[0], (B, T_TEXT, HIDDEN), jnp.float32), 'audio_kv': jax.random.normal(ks[1], (B, T_AUDIO, HIDDEN), jnp.float32), 'audio_attention_mask': jnp.ones((B, T_AUDIO), dtype=bool), 'Wq': jax.random.normal(ks[2], (HIDDEN, HIDDEN), jnp.float32) * s, 'Wk': jax.random.normal(ks[3], (HIDDEN, HIDDEN), jnp.float32) * s, 'Wv': jax.random.normal(ks[4], (HIDDEN, HIDDEN), jnp.float32) * s, 'Wo': jax.random.normal(ks[5], (HIDDEN, HIDDEN), jnp.float32) * s, 'ln_gamma': jnp.ones((HIDDEN,), jnp.float32), 'ln_beta': jnp.zeros((HIDDEN,), jnp.float32), 'gate': jnp.array([GATE_INIT], jnp.float32)}
    _L0_xattn_all = _L0_xattn_setup()
    _L0_xattn_in = {k: v for k, v in _L0_xattn_all.items() if k in ('Wq', 'Wk', 'Wv', 'Wo', 'ln_gamma', 'ln_beta', 'gate')}
    del _L0_xattn_all

    def _L1_xattn_setup():
        import jax, jax.numpy as jnp
        import numpy as np
        E, H, L, B = (512, 32, 256, 4)
        S = E // H
        DM, DD = (32, 64)

        def _ln(x, w, b, eps=1e-05):
            m = x.mean(-1, keepdims=True)
            v = ((x - m) ** 2).mean(-1, keepdims=True)
            return (x - m) / jnp.sqrt(v + eps) * w + b

        def _block(x, state, ln1_w, ln1_b, ln2_w, ln2_b, maa_x, maa_w1, maa_w2, maa_stack, time_decay, td_w1, td_w2, u, Wr, Wk, Wv, Wg, Wo, gn_w, gn_b, ffn_maa_k, ffn_maa_r, Wfk, Wfr, Wfv):
            b, l, e = x.shape
            h = u.shape[0]
            s_ = e // h
            xa = _ln(x, ln1_w, ln1_b)
            sx = jnp.concatenate([state[:, 1:2] - xa[:, :1], xa[:, :-1] - xa[:, 1:]], axis=1)
            xxx = jnp.tanh((xa + sx * maa_x) @ maa_w1).reshape(b, l, 5, DM)
            xxx = jnp.einsum('blfd,fde->blfe', xxx, maa_w2)
            xm = xa[:, :, None] + sx[:, :, None] * (maa_stack + xxx)
            xk, xw, xv, xr, xg = (xm[:, :, j] for j in range(5))
            w = jnp.exp(-jnp.exp(time_decay + jnp.tanh(xw @ td_w1) @ td_w2)).reshape(b, l, h, s_)
            r = (xr @ Wr.T).reshape(b, l, h, s_)
            k = (xk @ Wk.T).reshape(b, l, h, s_)
            v = (xv @ Wv.T).reshape(b, l, h, s_)
            g = jax.nn.silu(xg @ Wg.T)
            s0 = state[:, 2:2 + s_].reshape(b, h, s_, s_)

            def step(s, rkvw):
                r_t, k_t, v_t, w_t = rkvw
                a = k_t[..., :, None] * v_t[..., None, :]
                out = jnp.einsum('bhi,bhij->bhj', r_t, u * a + s)
                s = a + w_t[..., :, None] * s
                return (s, out)
            rkvw = tuple((jnp.moveaxis(t, 1, 0) for t in (r, k, v, w)))
            _, out = jax.lax.scan(step, s0, rkvw)
            out = jnp.moveaxis(out, 0, 1).reshape(b, l, e)
            og = out.reshape(b, l, h, s_)
            m = og.mean(-1, keepdims=True)
            va = ((og - m) ** 2).mean(-1, keepdims=True)
            og = ((og - m) / jnp.sqrt(va + 1e-05)).reshape(b, l, e) * gn_w + gn_b
            x1 = x + og * g @ Wo.T
            xc = _ln(x1, ln2_w, ln2_b)
            sx2 = jnp.concatenate([state[:, 0:1] - xc[:, :1], xc[:, :-1] - xc[:, 1:]], axis=1)
            xk2 = xc + sx2 * ffn_maa_k
            xr2 = xc + sx2 * ffn_maa_r
            rr = jax.nn.sigmoid(xr2 @ Wfr.T)
            kk = jnp.square(jax.nn.relu(xk2 @ Wfk.T))
            return x1 + rr * (kk @ Wfv.T)
        key = jax.random.key(seed)
        ks = jax.random.split(key, 24)
        sc = 0.02
        d = {'x': jax.random.normal(ks[0], (B, L, E), jnp.float32), 'state': jax.random.normal(ks[1], (B, 2 + S, E), jnp.float32) * 0.1, 'ln1_w': jnp.ones((E,), jnp.float32), 'ln1_b': jnp.zeros((E,), jnp.float32), 'ln2_w': jnp.ones((E,), jnp.float32), 'ln2_b': jnp.zeros((E,), jnp.float32), 'maa_x': jax.random.normal(ks[2], (E,), jnp.float32) * 0.1, 'maa_w1': jax.random.normal(ks[3], (E, 5 * DM), jnp.float32) * sc, 'maa_w2': jax.random.normal(ks[4], (5, DM, E), jnp.float32) * sc, 'maa_stack': jax.random.normal(ks[5], (1, 5, E), jnp.float32) * 0.1, 'time_decay': jax.random.normal(ks[6], (E,), jnp.float32) * 0.5, 'td_w1': jax.random.normal(ks[7], (E, DD), jnp.float32) * sc, 'td_w2': jax.random.normal(ks[8], (DD, E), jnp.float32) * sc, 'u': jax.random.normal(ks[9], (H, S, 1), jnp.float32) * 0.1, 'Wr': jax.random.normal(ks[10], (E, E), jnp.float32) * sc, 'Wk': jax.random.normal(ks[11], (E, E), jnp.float32) * sc, 'Wv': jax.random.normal(ks[12], (E, E), jnp.float32) * sc, 'Wg': jax.random.normal(ks[13], (E, E), jnp.float32) * sc, 'Wo': jax.random.normal(ks[14], (E, E), jnp.float32) * sc, 'gn_w': jnp.ones((E,), jnp.float32), 'gn_b': jnp.zeros((E,), jnp.float32), 'ffn_maa_k': jax.random.normal(ks[15], (E,), jnp.float32) * 0.1, 'ffn_maa_r': jax.random.normal(ks[16], (E,), jnp.float32) * 0.1, 'Wfk': jax.random.normal(ks[17], (E, E), jnp.float32) * sc, 'Wfr': jax.random.normal(ks[18], (E, E), jnp.float32) * sc, 'Wfv': jax.random.normal(ks[19], (E, E), jnp.float32) * sc}
        return d
    _L1_xattn_all = _L1_xattn_setup()
    _L1_xattn_in = {k: v for k, v in _L1_xattn_all.items() if k in ('ln1_w', 'ln1_b', 'ln2_w', 'ln2_b', 'maa_x', 'maa_w1', 'maa_w2', 'maa_stack', 'time_decay', 'td_w1', 'td_w2', 'u', 'Wr', 'Wk', 'Wv', 'Wg', 'Wo', 'gn_w', 'gn_b', 'ffn_maa_k', 'ffn_maa_r', 'Wfk', 'Wfr', 'Wfv')}
    del _L1_xattn_all
    return {'x': x, 'ctx_2048': ctx_2048, 'mask_BxS2_bf1': mask_BxS2_bf1, 'L0_xattn_Wq': _L0_xattn_in['Wq'], 'L0_xattn_Wk': _L0_xattn_in['Wk'], 'L0_xattn_Wv': _L0_xattn_in['Wv'], 'L0_xattn_Wo': _L0_xattn_in['Wo'], 'L0_xattn_ln_gamma': _L0_xattn_in['ln_gamma'], 'L0_xattn_ln_beta': _L0_xattn_in['ln_beta'], 'L0_xattn_gate': _L0_xattn_in['gate'], 'L1_xattn_ln1_w': _L1_xattn_in['ln1_w'], 'L1_xattn_ln1_b': _L1_xattn_in['ln1_b'], 'L1_xattn_ln2_w': _L1_xattn_in['ln2_w'], 'L1_xattn_ln2_b': _L1_xattn_in['ln2_b'], 'L1_xattn_maa_x': _L1_xattn_in['maa_x'], 'L1_xattn_maa_w1': _L1_xattn_in['maa_w1'], 'L1_xattn_maa_w2': _L1_xattn_in['maa_w2'], 'L1_xattn_maa_stack': _L1_xattn_in['maa_stack'], 'L1_xattn_time_decay': _L1_xattn_in['time_decay'], 'L1_xattn_td_w1': _L1_xattn_in['td_w1'], 'L1_xattn_td_w2': _L1_xattn_in['td_w2'], 'L1_xattn_u': _L1_xattn_in['u'], 'L1_xattn_Wr': _L1_xattn_in['Wr'], 'L1_xattn_Wk': _L1_xattn_in['Wk'], 'L1_xattn_Wv': _L1_xattn_in['Wv'], 'L1_xattn_Wg': _L1_xattn_in['Wg'], 'L1_xattn_Wo': _L1_xattn_in['Wo'], 'L1_xattn_gn_w': _L1_xattn_in['gn_w'], 'L1_xattn_gn_b': _L1_xattn_in['gn_b'], 'L1_xattn_ffn_maa_k': _L1_xattn_in['ffn_maa_k'], 'L1_xattn_ffn_maa_r': _L1_xattn_in['ffn_maa_r'], 'L1_xattn_Wfk': _L1_xattn_in['Wfk'], 'L1_xattn_Wfr': _L1_xattn_in['Wfr'], 'L1_xattn_Wfv': _L1_xattn_in['Wfv']}

def reference(x, ctx_2048, mask_BxS2_bf1, L0_xattn_Wq, L0_xattn_Wk, L0_xattn_Wv, L0_xattn_Wo, L0_xattn_ln_gamma, L0_xattn_ln_beta, L0_xattn_gate, L1_xattn_ln1_w, L1_xattn_ln1_b, L1_xattn_ln2_w, L1_xattn_ln2_b, L1_xattn_maa_x, L1_xattn_maa_w1, L1_xattn_maa_w2, L1_xattn_maa_stack, L1_xattn_time_decay, L1_xattn_td_w1, L1_xattn_td_w2, L1_xattn_u, L1_xattn_Wr, L1_xattn_Wk, L1_xattn_Wv, L1_xattn_Wg, L1_xattn_Wo, L1_xattn_gn_w, L1_xattn_gn_b, L1_xattn_ffn_maa_k, L1_xattn_ffn_maa_r, L1_xattn_Wfk, L1_xattn_Wfr, L1_xattn_Wfv):
    import jax
    import jax.numpy as jnp

    def _L0_xattn_ref(hidden_states, audio_kv, audio_attention_mask, Wq, Wk, Wv, Wo, ln_gamma, ln_beta, gate):
        import jax, jax.numpy as jnp
        import numpy as np
        HIDDEN = 512
        HEADS = 16
        HEAD_DIM = HIDDEN // HEADS
        LN_EPS = 1e-05
        GATE_INIT = 0.5

        def _layer_norm(x, gamma, beta):
            mu = jnp.mean(x, axis=-1, keepdims=True)
            var = jnp.mean(jnp.square(x - mu), axis=-1, keepdims=True)
            return (x - mu) * jax.lax.rsqrt(var + LN_EPS) * gamma + beta
        B, Tt, D = hidden_states.shape
        Ta = audio_kv.shape[1]
        scale = HEAD_DIM ** (-0.5)
        a = _layer_norm(audio_kv, ln_gamma, ln_beta)
        Q = (hidden_states @ Wq.T).reshape(B, Tt, HEADS, HEAD_DIM).transpose(0, 2, 1, 3)
        K = (a @ Wk.T).reshape(B, Ta, HEADS, HEAD_DIM).transpose(0, 2, 1, 3)
        V = (a @ Wv.T).reshape(B, Ta, HEADS, HEAD_DIM).transpose(0, 2, 1, 3)
        scores = jnp.einsum('bhtd,bhsd->bhts', Q, K) * scale
        mask = audio_attention_mask[:, None, None, :]
        scores = jnp.where(mask, scores, jnp.float32(-jnp.inf))
        attn = jax.nn.softmax(scores, axis=-1)
        out = jnp.einsum('bhts,bhsd->bhtd', attn, V)
        out = out.transpose(0, 2, 1, 3).reshape(B, Tt, D)
        out = out @ Wo.T
        return hidden_states + jnp.tanh(gate) * out

    def _L1_xattn_ref(x, state, ln1_w, ln1_b, ln2_w, ln2_b, maa_x, maa_w1, maa_w2, maa_stack, time_decay, td_w1, td_w2, u, Wr, Wk, Wv, Wg, Wo, gn_w, gn_b, ffn_maa_k, ffn_maa_r, Wfk, Wfr, Wfv):
        import jax, jax.numpy as jnp
        import numpy as np
        E, H, L, B = (512, 32, 256, 4)
        S = E // H
        DM, DD = (32, 64)

        def _ln(x, w, b, eps=1e-05):
            m = x.mean(-1, keepdims=True)
            v = ((x - m) ** 2).mean(-1, keepdims=True)
            return (x - m) / jnp.sqrt(v + eps) * w + b

        def _block(x, state, ln1_w, ln1_b, ln2_w, ln2_b, maa_x, maa_w1, maa_w2, maa_stack, time_decay, td_w1, td_w2, u, Wr, Wk, Wv, Wg, Wo, gn_w, gn_b, ffn_maa_k, ffn_maa_r, Wfk, Wfr, Wfv):
            b, l, e = x.shape
            h = u.shape[0]
            s_ = e // h
            xa = _ln(x, ln1_w, ln1_b)
            sx = jnp.concatenate([state[:, 1:2] - xa[:, :1], xa[:, :-1] - xa[:, 1:]], axis=1)
            xxx = jnp.tanh((xa + sx * maa_x) @ maa_w1).reshape(b, l, 5, DM)
            xxx = jnp.einsum('blfd,fde->blfe', xxx, maa_w2)
            xm = xa[:, :, None] + sx[:, :, None] * (maa_stack + xxx)
            xk, xw, xv, xr, xg = (xm[:, :, j] for j in range(5))
            w = jnp.exp(-jnp.exp(time_decay + jnp.tanh(xw @ td_w1) @ td_w2)).reshape(b, l, h, s_)
            r = (xr @ Wr.T).reshape(b, l, h, s_)
            k = (xk @ Wk.T).reshape(b, l, h, s_)
            v = (xv @ Wv.T).reshape(b, l, h, s_)
            g = jax.nn.silu(xg @ Wg.T)
            s0 = state[:, 2:2 + s_].reshape(b, h, s_, s_)

            def step(s, rkvw):
                r_t, k_t, v_t, w_t = rkvw
                a = k_t[..., :, None] * v_t[..., None, :]
                out = jnp.einsum('bhi,bhij->bhj', r_t, u * a + s)
                s = a + w_t[..., :, None] * s
                return (s, out)
            rkvw = tuple((jnp.moveaxis(t, 1, 0) for t in (r, k, v, w)))
            _, out = jax.lax.scan(step, s0, rkvw)
            out = jnp.moveaxis(out, 0, 1).reshape(b, l, e)
            og = out.reshape(b, l, h, s_)
            m = og.mean(-1, keepdims=True)
            va = ((og - m) ** 2).mean(-1, keepdims=True)
            og = ((og - m) / jnp.sqrt(va + 1e-05)).reshape(b, l, e) * gn_w + gn_b
            x1 = x + og * g @ Wo.T
            xc = _ln(x1, ln2_w, ln2_b)
            sx2 = jnp.concatenate([state[:, 0:1] - xc[:, :1], xc[:, :-1] - xc[:, 1:]], axis=1)
            xk2 = xc + sx2 * ffn_maa_k
            xr2 = xc + sx2 * ffn_maa_r
            rr = jax.nn.sigmoid(xr2 @ Wfr.T)
            kk = jnp.square(jax.nn.relu(xk2 @ Wfk.T))
            return x1 + rr * (kk @ Wfv.T)
        return _block(x, state, ln1_w, ln1_b, ln2_w, ln2_b, maa_x, maa_w1, maa_w2, maa_stack, time_decay, td_w1, td_w2, u, Wr, Wk, Wv, Wg, Wo, gn_w, gn_b, ffn_maa_k, ffn_maa_r, Wfk, Wfr, Wfv)
    x = _L0_xattn_ref(x, ctx_2048, mask_BxS2_bf1, L0_xattn_Wq, L0_xattn_Wk, L0_xattn_Wv, L0_xattn_Wo, L0_xattn_ln_gamma, L0_xattn_ln_beta, L0_xattn_gate)
    x = _L1_xattn_ref(x, ctx_2048, L1_xattn_ln1_w, L1_xattn_ln1_b, L1_xattn_ln2_w, L1_xattn_ln2_b, L1_xattn_maa_x, L1_xattn_maa_w1, L1_xattn_maa_w2, L1_xattn_maa_stack, L1_xattn_time_decay, L1_xattn_td_w1, L1_xattn_td_w2, L1_xattn_u, L1_xattn_Wr, L1_xattn_Wk, L1_xattn_Wv, L1_xattn_Wg, L1_xattn_Wo, L1_xattn_gn_w, L1_xattn_gn_b, L1_xattn_ffn_maa_k, L1_xattn_ffn_maa_r, L1_xattn_Wfk, L1_xattn_Wfr, L1_xattn_Wfv)
    return x

_drawn_inputs = setup_inputs


def setup_inputs(seed=0):
    import zlib

    import numpy as np

    out = dict(_drawn_inputs(seed))
    spreads = {'L0_xattn_ln_gamma': (1.0, 0.6),
     'L0_xattn_ln_beta': (0.0, 0.8),
     'L1_xattn_ln1_w': (1.0, 0.2),
     'L1_xattn_ln1_b': (0.0, 0.277),
     'L1_xattn_ln2_w': (1.0, 0.6),
     'L1_xattn_ln2_b': (0.0, 0.8),
     'L1_xattn_gn_w': (1.0, 0.6),
     'L1_xattn_gn_b': (0.0, 0.695)}
    factors = {'L0_xattn_Wq': 8.0,
     'L0_xattn_Wk': 8.0,
     'L1_xattn_maa_x': 8.0,
     'L1_xattn_maa_w1': 2.939,
     'L1_xattn_maa_w2': 2.939,
     'L1_xattn_td_w1': 8.0,
     'L1_xattn_td_w2': 8.0,
     'L1_xattn_u': 3.066,
     'L1_xattn_ffn_maa_k': 5.638,
     'L1_xattn_ffn_maa_r': 8.0,
     'L1_xattn_Wfr': 4.071}
    for name, (base, spread) in spreads.items():
        noise = np.random.default_rng([zlib.crc32(name.encode()), seed]).standard_normal(out[name].shape)
        drawn = base * np.exp(spread * noise) if base else spread * noise
        out[name] = jnp.asarray(drawn.astype(out[name].dtype))
    for name, factor in factors.items():
        out[name] = (out[name] * factor).astype(out[name].dtype)
    return out
```

```python
from contextlib import ExitStack

import numpy as np

import concourse.bass as bass
from concourse import mybir

ALU = mybir.AluOpType
ACT = mybir.ActivationFunctionType
AX = mybir.AxisListType
F32 = mybir.dt.float32
F32R = mybir.dt.float32r
U8 = mybir.dt.uint8

P = 128
B, T, D = 16, 112, 512
TC = 375
KT = 3
TK = TC // KT
C = D // P
HEADS, HD = 16, 32
HG = P // HD
SCALE = HD ** -0.5
EPS = 1e-5
BANK = 512
LOWEST = -3.0e38

VECTORS = ["ln_gamma", "ln_beta", "ln1_w", "ln1_b", "ln2_w", "ln2_b", "maa_x", "maa_k", "maa_w", "maa_v", "maa_r",
           "maa_g", "time_decay", "gn_w", "gn_b", "ffn_k", "ffn_r", "u"]
S = 16
MAA, MD, TD = 5, 32, 64
NRING = 4
MIXES = ["maa_w", "maa_v", "maa_k", "maa_r", "maa_g"]
MIX_ROW = [1, 2, 0, 3, 4]
MIX_SLOT = [3, 5, 7, 9, 11]
MIX_USE = [2, 4, 6, 8, 10]
VEC = {name: n for n, name in enumerate(VECTORS)}


def index(b):
    return 2 * b[0] + b[1]


def later(b, steps):
    n = b[1] + steps
    return b[0] + n // 2, n % 2


def count(b, per_batch, done):
    return index(b) * per_batch + done


def at_least(b, n):
    return not isinstance(b[0], int) or index(b) >= n


def is_batch(b, n):
    return isinstance(b[0], int) and index(b) == n


def cross_attention(nc, A, W, w_loaded):
    with ExitStack() as ctx:
        def sb(name, shape, dt=F32):
            return ctx.enter_context(nc.sbuf_tensor(name, shape, dt))

        def sem(name):
            return ctx.enter_context(nc.semaphore(name))

        def sem2(name):
            return [sem(f"{name}_{q}") for q in range(2)]

        bank = [ctx.enter_context(nc.psum_tensor(f"a_bank{n}", [P, BANK], F32)) for n in range(8)]
        score_bank, proj_bank, q_bank, pt_bank, av_bank = bank[0:2], bank[2:4], bank[4], bank[5:7], bank[7]

        wq, wk, wv, wo = (sb(n, [P, C, D]) for n in ("wq_sb", "wk_sb", "wv_sb", "wo_sb"))
        ident = sb("a_ident", [P, P])
        headmask = sb("headmask_sb", [P, HG])
        vec = sb("a_vec", [P, len(VECTORS), C])
        gate = sb("gate_sb", [T, 1])
        tanh_gate = sb("tanh_gate", [T, 1])
        eps_exp = sb("a_eps_exp", [TK, KT])
        to_inf = sb("to_inf", [T, 3])
        mask8 = sb("mask8", [T, B, TC], U8)
        unmask = sb("unmask", [T, 2, TC])
        xT = sb("xT_sb", [P, 2, C, T])
        x_tok = sb("x_tok", [T, 2, D])
        ctx_tok = sb("ctx_tok", [TK, 2, KT, D])
        ctx_norm = sb("ctx_norm", [TK, KT, D])
        stats = sb("ctx_stats", [TK, KT, 6])
        meanvar = sb("ctx_meanvar", [TK, KT, 2])
        var_eps = sb("ctx_var_eps", [TK, KT])
        rstd = sb("ctx_rstd", [TK, KT])
        aT = sb("aT", [P, C, TC])
        keyT = sb("keyT", [P, 2, C, TC])
        value = sb("value", [TK, 2, KT, D])
        qpad = sb("qpad", [P, 2, C, HG, T])
        probs = sb("probs", [T, 2, HG, TC])
        maxes = sb("maxes", [T, 2, HG])
        negmax = sb("negmax", [T, 2, HG])
        sums = sb("sums", [T, 2, HG])
        inv = sb("inv", [T, 2, HG])
        probsT = sb("probsT", [TK, 2, KT, HG * T])
        attnT = sb("attnT", [P, C, T])
        x1 = sb("x1_sb", [T, 2, D])

        s_w = {n: sem(f"a_{n}_loaded") for n in ("wq", "wk", "wv", "wo", "ident", "headmask", "vec", "gate", "mask")}
        s_xT, s_xtok, s_ctx, s_x1st = sem2("xT_loaded"), sem2("xtok_loaded"), sem2("ctx_loaded"), sem2("x1_stored")
        s_gate = sem("gate_ready")
        s_const = sem("a_constants_set")
        s_unmask1 = sem("unmask_steps")
        s_stats, s_mv, s_ve = sem("ctx_stats_done"), sem("ctx_meanvar_done"), sem("ctx_vareps_done")
        s_rstd, s_ctxn = sem("ctx_rstd_done"), sem("ctx_normalised")
        s_proj, s_projev = sem("proj_done"), sem("proj_copied")
        s_q, s_qpad = sem("q_done"), sem("qpad_ready")
        s_score, s_masked, s_negmax = sem("score_done"), sem("score_masked"), sem("negmax_ready")
        s_exp, s_inv, s_probs = sem("exp_done"), sem("inv_ready"), sem("probs_ready")
        s_pt, s_ptev = sem("probs_transposed"), sem("probsT_ready")
        s_av, s_attn, s_wo, s_x1 = sem("av_done"), sem("attnT_ready"), sem("wo_done"), sem("x1_ready")

        FIRST, LOOP, LAST = [(0, 0), (0, 1), (1, 0), (1, 1)], (2, B // 2 - 1), [(B // 2 - 1, 0), (B // 2 - 1, 1), (B // 2, 0)]

        def run(engine, step):
            for n in FIRST:
                step(n, True, not is_batch(n, 0), True)
            with engine.Fori(*LOOP) as k:
                for q in range(2):
                    step((k, q), True, True, True)
            for n in LAST:
                step(n, not is_batch(n, B), True, is_batch(n, B - 2))

        block = ctx.enter_context(nc.Block())

        @block.sync
        def _(sp):
            def load_ctx(b):
                if at_least(b, 2):
                    sp.wait_ge(s_ctxn, count(later(b, -2), 1, 1))
                sp.dma_start(ctx_tok[:, b[1]], A["ctx"][index(b)].rearrange("(k p) d -> p k d", p=TK)).then_inc(s_ctx[b[1]], 16)

            def load_x(b):
                if at_least(b, 2):
                    sp.wait_ge(s_q, count(later(b, -2), C, C))
                sp.dma_start(xT[:, b[1]], A["xT"][index(b)]).then_inc(s_xT[b[1]], 16)

            def load_xtok(b):
                if at_least(b, 2):
                    sp.wait_ge(s_x1, count(later(b, -2), 1, 1))
                sp.dma_start(x_tok[:, b[1]], A["x"][index(b)]).then_inc(s_xtok[b[1]], 16)

            load_ctx((0, 0))
            sp.dma_start(vec[:], A["vec"]).then_inc(s_w["vec"], 16)
            sp.dma_start(ident[:], A["ident"]).then_inc(s_w["ident"], 16)
            load_x((0, 0))
            sp.dma_start(wq[:], A["wq"]).then_inc(s_w["wq"], 16)
            sp.dma_start(wk[:], A["wk"]).then_inc(s_w["wk"], 16)
            load_ctx((0, 1))
            sp.dma_start(wv[:], A["wv"]).then_inc(s_w["wv"], 16)
            sp.dma_start(headmask[:], A["headmask"]).then_inc(s_w["headmask"], 16)
            sp.dma_start(mask8[:], A["mask"].rearrange("(o b) t -> o b t", o=1).broadcast_to([T, B, TC])).then_inc(s_w["mask"], 16)
            sp.dma_start(gate[:], A["gate"].broadcast_to([T, 1])).then_inc(s_w["gate"], 16)
            sp.dma_start(wo[:], A["wo"]).then_inc(s_w["wo"], 16)
            for name in W:
                sp.dma_start(W[name][:], A["b_" + name]).then_inc(w_loaded[name], 16)

            def step(n, project, attend, normalise):
                if project and not is_batch(n, 0):
                    load_x(n)
                if attend:
                    load_xtok(later(n, -1))
                if normalise and not is_batch(n, 0):
                    load_ctx(later(n, 1))
                if attend:
                    m = later(n, -1)
                    sp.wait_ge(s_x1, count(m, 1, 1))
                    sp.dma_start(A["x1"][index(m)], x1[:, m[1]]).then_inc(s_x1st[m[1]], 16)

            run(sp, step)
            for q in range(2):
                sp.wait_ge(s_x1st[q], 16 * (B // 2))

        @block.gpsimd
        def _(pool):
            for i, x in enumerate((1.0, 3.0e38, 10.0)):
                pool.memset(to_inf[:, i:i + 1], x)
            pool.memset(eps_exp[:], -0.5).then_inc(s_const, 1)
            pool.wait_ge(s_w["mask"], 16)

            def step(n, project, attend, normalise):
                if attend:
                    m = later(n, -1)
                    q = m[1]
                    if at_least(m, 2):
                        pool.wait_ge(s_masked, count(later(m, -2), HEADS, HEADS))
                    pool.tensor_copy(unmask[:, q], mask8[:, index(m), :]).then_inc(s_unmask1, 1)
                    for i, op in enumerate((ALU.subtract, ALU.mult, ALU.mult)):
                        pool.wait_ge(s_unmask1, count(m, C, i + 1))
                        last = pool.tensor_tensor(unmask[:, q], unmask[:, q], to_inf[:, i:i + 1].broadcast_to([T, TC]), op)
                        last.then_inc(s_unmask1, 1)
                if normalise:
                    rsqrt(later(n, 1))

            def rsqrt(b):
                pool.wait_ge(s_ve, count(b, 1, 1))
                if at_least(b, 1):
                    pool.wait_ge(s_ctxn, count(later(b, -1), 1, 1))
                pool.tensor_tensor(rstd[:], var_eps[:], eps_exp[:], ALU.pow).then_inc(s_rstd, 1)

            pool.wait_ge(s_const, 1)
            rsqrt((0, 0))
            run(pool, step)

        @block.vector
        def _(dve):
            def ln_stats(b):
                dve.wait_ge(s_ctx[b[1]], 16 * (b[0] + 1))
                for k in range(KT):
                    last = dve.bn_stats(stats[:, k], ctx_tok[:, b[1], k])
                last.then_inc(s_stats, 1)
                dve.wait_ge(s_stats, count(b, 1, 1))
                dve.memset(var_eps[:], 0.0)
                for k in range(KT):
                    last = dve.bn_aggr(meanvar[:, k], stats[:, k])
                last.then_inc(s_mv, 1)
                dve.wait_ge(s_mv, count(b, 1, 1))
                dve.tensor_scalar(var_eps[:], meanvar[:, :, 1], EPS, None, ALU.add).then_inc(s_ve, 1)

            def ln_apply(b):
                dve.wait_ge(s_rstd, count(b, 1, 1))
                if at_least(b, 1):
                    dve.wait_ge(s_proj, count(later(b, -1), 11, C))
                for k in range(KT):
                    last = dve.tensor_scalar(ctx_norm[:, k], ctx_tok[:, b[1], k], meanvar[:, k, 0:1], rstd[:, k:k + 1],
                                             ALU.subtract, ALU.mult)
                last.then_inc(s_ctxn, 1)

            def pad_queries(b, c):
                dve.wait_ge(s_q, count(b, C, c + 1))
                dve.tensor_tensor(qpad[:, b[1], c], q_bank[:, 0:T].unsqueeze(1).broadcast_to([P, HG, T]),
                                  headmask[:].unsqueeze(2).broadcast_to([P, HG, T]), ALU.mult).then_inc(s_qpad, 1)

            def mask_scores(m, g):
                if g == 0:
                    dve.wait_ge(s_unmask1, count(m, C, C))
                if g >= 2 or at_least(m, 1):
                    dve.wait_ge(s_pt, count(m, C * KT, (g - 1) * KT))
                for i in range(HG):
                    h = g * HG + i
                    dve.wait_ge(s_score, count(m, HEADS, h + 1))
                    if i == 0:
                        dve.memset(negmax[:, g % 2, 0:1], 0.0)
                    else:
                        negate_max(m, g, i - 1)
                    dve.tensor_tensor_reduce(out=probs[:, g % 2, i], in0=score_bank[h % 2][0:T, 0:TC], in1=unmask[:, m[1]],
                                             scale=SCALE, scalar=LOWEST, op0=ALU.add, op1=ALU.max,
                                             accum_out=maxes[:, g % 2, i:i + 1]).then_inc(s_masked, 1)
                negate_max(m, g, HG - 1).then_inc(s_negmax, 1)

            def negate_max(m, g, i):
                dve.wait_ge(s_masked, count(m, HEADS, g * HG + i + 1))
                return dve.tensor_scalar(negmax[:, g % 2, i:i + 1], maxes[:, g % 2, i:i + 1], -1.0, None, ALU.mult)

            def normalise_probs(m, g):
                dve.wait_ge(s_exp, count(m, C, g + 1))
                dve.reciprocal(inv[:, g % 2], sums[:, g % 2]).then_inc(s_inv, 1)
                dve.wait_ge(s_inv, count(m, C, g + 1))
                for i in range(HG):
                    last = dve.tensor_scalar(probs[:, g % 2, i], probs[:, g % 2, i], inv[:, g % 2, i:i + 1], None, ALU.mult)
                last.then_inc(s_probs, 1)

            def copy_probsT(m, g):
                for k in range(KT):
                    u = g * KT + k
                    dve.wait_ge(s_pt, count(m, C * KT, u + 1))
                    if k == 0 and (g >= 2 or at_least(m, 1)):
                        dve.wait_ge(s_av, count(m, C, g - 1))
                    dve.tensor_copy(probsT[:, g % 2, k], pt_bank[u % 2][0:TK, 0:HG * T]).then_inc(s_ptev, 1)

            def residual(m):
                if at_least(m, 2):
                    dve.wait_ge(s_x1st[m[1]], 16 * m[0])
                dve.wait_ge(s_xtok[m[1]], 16 * (m[0] + 1))
                dve.wait_ge(s_wo, count(m, 1, 1))
                if is_batch(m, 0):
                    dve.wait_ge(s_gate, 1)
                dve.scalar_tensor_tensor(out=x1[:, m[1]], in0=av_bank[0:T, :], scalar=tanh_gate[:, 0:1], in1=x_tok[:, m[1]],
                                         op0=ALU.mult, op1=ALU.add).then_inc(s_x1, 1)

            def step(n, project, attend, normalise):
                m = later(n, -1)
                if attend:
                    mask_scores(m, 0)
                if project:
                    pad_queries(n, 0)
                if attend:
                    normalise_probs(m, 0)
                if project:
                    pad_queries(n, 1)
                    pad_queries(n, 2)
                if attend:
                    copy_probsT(m, 0)
                if normalise:
                    ln_stats(later(n, 1))
                for g in range(1, C):
                    if attend:
                        mask_scores(m, g)
                    if g == 1 and project:
                        pad_queries(n, 3)
                    if attend:
                        normalise_probs(m, g)
                        copy_probsT(m, g)
                    if g == 1 and normalise:
                        ln_apply(later(n, 1))
                if attend:
                    residual(m)

            dve.wait_ge(s_w["headmask"], 16)
            ln_stats((0, 0))
            ln_apply((0, 0))
            run(dve, step)

        @block.scalar
        def _(act):
            act.wait_ge(s_w["gate"], 16)
            act.activation(tanh_gate[:], gate[:], ACT.Tanh).then_inc(s_gate, 1)
            act.wait_ge(s_w["vec"], 16)

            def copy_aT(b, c):
                act.wait_ge(s_proj, count(b, 11, c + 1))
                act.activation(aT[:, c], proj_bank[(b[1] * 11 + c) % 2][:, 0:TC], ACT.Identity,
                               scale=vec[:, VEC["ln_gamma"], c:c + 1], bias=vec[:, VEC["ln_beta"], c:c + 1]).then_inc(s_projev, 1)

            def copy_key(b, c):
                u = C + c
                act.wait_ge(s_proj, count(b, 11, u + 1))
                act.copy(keyT[:, b[1], c], proj_bank[(b[1] * 11 + u) % 2][:, 0:TC]).then_inc(s_projev, 1)

            def copy_value(b, k):
                u = 2 * C + k
                act.wait_ge(s_proj, count(b, 11, u + 1))
                act.copy(value[:, b[1], k], proj_bank[(b[1] * 11 + u) % 2][0:TK, :]).then_inc(s_projev, 1)

            def exps(m, g, heads):
                act.wait_ge(s_negmax, count(m, C, g + 1))
                for i in heads:
                    last = act.activation(probs[:, g % 2, i], probs[:, g % 2, i], ACT.Exp, bias=negmax[:, g % 2, i:i + 1],
                                          accum_out=sums[:, g % 2, i:i + 1])
                if i == HG - 1:
                    last.then_inc(s_exp, 1)

            def copy_attn(m, g):
                act.wait_ge(s_av, count(m, C, g + 1))
                if g == 0 and at_least(m, 1):
                    act.wait_ge(s_wo, count(later(m, -1), 1, 1))
                act.copy(attnT[:, g], av_bank[:, g * T:(g + 1) * T]).then_inc(s_attn, 1)

            def step(n, project, attend, normalise):
                m = later(n, -1)
                if attend:
                    exps(m, 0, (0, 1))
                if project:
                    copy_aT(n, 0)
                    copy_aT(n, 1)
                if attend:
                    exps(m, 0, (2, 3))
                if project:
                    copy_aT(n, 2)
                    copy_aT(n, 3)
                for g in range(1, C):
                    if attend:
                        exps(m, g, range(HG))
                        copy_attn(m, g - 1)
                    if project:
                        if g < 3:
                            copy_key(n, 2 * g - 2)
                            copy_key(n, 2 * g - 1)
                        else:
                            for k in range(KT):
                                copy_value(n, k)
                if attend:
                    copy_attn(m, C - 1)

            run(act, step)

        @block.tensor
        def _(pe):
            def proj_free(b, u):
                if u >= 2 or at_least(b, 1):
                    pe.wait_ge(s_projev, count(b, 11, u - 1))
                return proj_bank[(b[1] * 11 + u) % 2]

            def transpose_ctx(b, c):
                dst = proj_free(b, c)
                pe.wait_ge(s_ctxn, count(b, 1, 1))
                for k in range(KT):
                    last = pe.transpose(dst[:, k * TK:(k + 1) * TK], ctx_norm[:, k, c * P:(c + 1) * P], ident[0:TK, 0:TK])
                last.then_inc(s_proj, 1)

            def project_key(b, m):
                dst = proj_free(b, C + m)
                pe.wait_ge(s_projev, count(b, 11, C))
                for c in range(C):
                    last = pe.matmul(dst[:, 0:TC], wk[:, c, m * P:(m + 1) * P], aT[:, c], start=(c == 0), stop=(c == C - 1))
                last.then_inc(s_proj, 1)

            def project_value(b, k):
                dst = proj_free(b, 2 * C + k)
                for c in range(C):
                    last = pe.matmul(dst[0:TK, :], aT[:, c, k * TK:(k + 1) * TK], wv[:, c], start=(c == 0), stop=(c == C - 1))
                last.then_inc(s_proj, 1)

            def project_query(b, m):
                if m == 0:
                    pe.wait_ge(s_xT[b[1]], 16 * (b[0] + 1))
                if m > 0 or at_least(b, 1):
                    pe.wait_ge(s_qpad, count(b, C, m))
                for c in range(C):
                    last = pe.matmul(q_bank[:, 0:T], wq[:, c, m * P:(m + 1) * P], xT[:, b[1], c], start=(c == 0), stop=(c == C - 1))
                last.then_inc(s_q, 1)

            def scores(m, g):
                if g == 0:
                    pe.wait_ge(s_qpad, count(m, C, C))
                    pe.wait_ge(s_projev, count(m, 11, 11))
                for i in range(HG):
                    h = g * HG + i
                    if h >= 2 or at_least(m, 1):
                        pe.wait_ge(s_masked, count(m, HEADS, h - 1))
                    pe.matmul(score_bank[h % 2][0:T, 0:TC], qpad[:, m[1], g, i], keyT[:, m[1], g], start=True,
                              stop=True).then_inc(s_score, 1)

            def transpose_probs(m, g):
                pe.wait_ge(s_probs, count(m, C, g + 1))
                for k in range(KT):
                    u = g * KT + k
                    if u >= 2 or at_least(m, 1):
                        pe.wait_ge(s_ptev, count(m, C * KT, u - 1))
                    for i in range(HG):
                        last = pe.transpose(pt_bank[u % 2][0:TK, i * T:(i + 1) * T], probs[:, g % 2, i, k * TK:(k + 1) * TK],
                                            ident[0:T, 0:T])
                    last.then_inc(s_pt, 1)

            def weigh_values(m, g):
                pe.wait_ge(s_ptev, count(m, C * KT, (g + 1) * KT))
                if g > 0:
                    pe.wait_ge(s_attn, count(m, C, g))
                elif at_least(m, 1):
                    pe.wait_ge(s_x1, count(later(m, -1), 1, 1))
                for i in range(HG):
                    h = g * HG + i
                    for k in range(KT):
                        last = pe.matmul(av_bank[i * HD:(i + 1) * HD, g * T:(g + 1) * T], value[:, m[1], k, h * HD:(h + 1) * HD],
                                         probsT[:, g % 2, k, i * T:(i + 1) * T], start=(k == 0), stop=(k == KT - 1))
                last.then_inc(s_av, 1)

            def project_out(m):
                pe.wait_ge(s_attn, count(m, C, C))
                for c in range(C):
                    last = pe.matmul(av_bank[0:T, :], attnT[:, c], wo[:, c], start=(c == 0), stop=(c == C - 1))
                last.then_inc(s_wo, 1)

            def step(n, project, attend, normalise):
                m = later(n, -1)
                if attend:
                    scores(m, 0)
                if project:
                    project_query(n, 0)
                    transpose_ctx(n, 0)
                    transpose_ctx(n, 1)
                    project_query(n, 1)
                    transpose_ctx(n, 2)
                    transpose_ctx(n, 3)
                    project_query(n, 2)
                if attend:
                    transpose_probs(m, 0)
                for g in range(1, C):
                    if attend:
                        scores(m, g)
                        if is_batch(m, 0) and g == 1:
                            pe.wait_ge(s_w["wo"], 16)
                        weigh_values(m, g - 1)
                    if project:
                        if g == 1:
                            project_query(n, 3)
                        if is_batch(n, 0) and g == 1:
                            pe.wait_ge(s_w["wk"], 16)
                        if is_batch(n, 0) and g == 3:
                            pe.wait_ge(s_w["wv"], 16)
                        if g < 3:
                            project_key(n, 2 * g - 2)
                            project_key(n, 2 * g - 1)
                        else:
                            project_value(n, 0)
                            project_value(n, 1)
                    if attend:
                        transpose_probs(m, g)
                    if project and g == 3:
                        project_value(n, 2)
                if attend:
                    weigh_values(m, C - 1)
                    project_out(m)

            pe.wait_ge(s_w["ident"], 16)
            pe.wait_ge(s_w["wq"], 16)
            run(pe, step)


def rwkv_block(nc, A, W, w_loaded):
    with ExitStack() as ctx:
        def sb(name, shape, dt=F32):
            return ctx.enter_context(nc.sbuf_tensor(name, shape, dt))

        def sem(name):
            return ctx.enter_context(nc.semaphore(name))

        def sem2(name):
            return [sem(f"{name}_{q}") for q in range(2)]

        bank = [ctx.enter_context(nc.psum_tensor(f"b_bank{n}", [P, BANK], F32)) for n in range(8)]
        vrep_bank, out_bank, pre_bank, post_bank = bank[0:2], bank[2], bank[3:6], bank[6:8]

        CT = C * T
        ident = sb("b_ident", [P, P])
        vec = sb("b_vec", [P, len(VECTORS), C])
        half_gn = sb("half_gn", [P, 2, C])
        maa1 = sb("maa1_sb", [P, C, MAA * MD])
        maa2 = sb("maa2_sb", [P, MAA, D])
        td1 = sb("td1_sb", [P, C, TD])
        td2 = sb("td2_sb", [P, D])
        headsum = sb("headsum_sb", [P, P])
        headmean = sb("headmean", [P, P])
        bonus_w = sb("bonus_w", [P, C, P])
        collect = sb("collect_sb", [P, S, P])
        spread = sb("spread_r", [P, S, P], F32R)
        s0 = sb("s0_sb", [P, B, C, S])
        rows = sb("rows_sb", [P, B, 2, C])
        neg_half = sb("neg_half", [T, 1])
        ln_eps = sb("b_eps", [P, 1])

        x1 = sb("b_x1", [T, 2, D])
        ln_tok = sb("ln1_tok", [T, D])
        bn6, mv, ve, rs = sb("ln1_bn", [T, 6]), sb("ln1_mv", [T, 2]), sb("ln1_ve", [T, 1]), sb("ln1_rs", [T, 1])
        xa = sb("xa", [P, C, T + 1])
        sx = sb("sx", [P, C, T])
        xin = sb("xin", [P, C, T])
        th = sb("th", [P, 2, T])
        mixed = sb("mixed", [P, 2, C, T])
        xm = sb("xm", [P, 2, C, T])
        ttd = sb("ttd", [P, T])
        etd = sb("etd", [P, C, T])
        wdec = sb("wdec", [P, 2, C, T])
        v = sb("v_sb", [P, 2, C, T])
        vhi = sb("v_hi", [P, 2, C, T], F32R)
        vlo = sb("v_lo", [P, 2, C, T], F32R)
        key = sb("key", [P, 2, C, T])
        rec = sb("rec", [P, 2, C, T])
        tg = sb("tg", [P, C, T])
        gate2 = sb("gate2", [P, 2, C, T])
        rk = sb("rk", [P, C, T])
        bv = sb("bv", [P, C, T])
        kv = sb("kv", [P, NRING, BANK])
        st = sb("st", [P, NRING, CT])
        rst = sb("rst", [P, NRING, CT])
        wkv = sb("wkv", [P, C, T])
        cen = sb("cen", [P, C, T])
        sq = sb("sq", [P, C, T])
        gated = sb("gated", [P, C, T])
        x1p = sb("x1_post", [T, 2, D])
        x2 = sb("x2", [T, D])
        ln2_tok = sb("ln2_tok", [T, D])
        bn6p, mvp, vep, rsp = sb("ln2_bn", [T, 6]), sb("ln2_mv", [T, 2]), sb("ln2_ve", [T, 1]), sb("ln2_rs", [T, 1])
        xc = sb("xc", [P, C, T + 1])
        sx2 = sb("sx2", [P, C, T])
        xk2 = sb("xk2", [P, C, T])
        xr2 = sb("xr2", [P, C, T])
        kk = sb("kk", [P, C, T])
        trr = sb("trr", [T, D])
        fin = sb("fin", [T, 2, D])

        small = ("ident", "vec", "maa1", "td1", "headsum", "collect", "s0", "rows", "maa2", "td2", "spread")
        s_c = {n: sem(f"b_{n}_loaded") for n in small}
        s_x1, s_x1p, s_store = sem2("b_x1_loaded"), sem2("x1_post_loaded"), sem2("out_stored")
        s_zero, s_setup, s_spread = sem("zeros_set"), sem("setup_done"), sem("spread_rounded")
        s_bn, s_mv, s_ve, s_rs, s_ln = (sem(f"ln1_{n}") for n in ("stats", "meanvar", "vareps", "rstd", "normalised"))
        s_bnp, s_mvp, s_vep, s_rsp, s_lnp = (sem(f"ln2_{n}") for n in ("stats", "meanvar", "vareps", "rstd", "normalised"))
        s_t1, s_xa0, s_xa, s_sx, s_xin = sem("x_transposed"), sem("xa_state"), sem("xa_ready"), sem("sx_ready"), sem("xin_ready")
        s_w1, s_th, s_mixmm, s_mixed, s_xm = (sem(n) for n in ("maa1_done", "th_ready", "maa2_done", "mixed_ready", "xm_ready"))
        s_td1, s_ttd, s_td2, s_etd, s_wdec = (sem(n) for n in ("td1_done", "ttd_ready", "td2_done", "etd_ready", "decay_ready"))
        s_vmm, s_v, s_vlo = sem("v_done"), sem("v_ready"), sem("v_lo_ready")
        s_kmm, s_k, s_rmm, s_r = sem("k_done"), sem("k_ready"), sem("r_done"), sem("r_ready")
        s_gmm, s_tg, s_g = sem("g_done"), sem("tg_ready"), sem("gate_ready2")
        s_rk, s_bonus, s_bv = sem("rk_ready"), sem("bonus_done"), sem("bv_ready")
        s_vrep, s_kv0, s_kv, s_st = sem("vrep_done"), sem("kv_state_ready"), sem("kv_ready"), sem("states_ready")
        s_even, s_odd, s_red = sem("even_products"), sem("odd_products"), sem("reduced")
        s_wkv1, s_wkv = sem("wkv_state_part"), sem("wkv_ready")
        s_mean, s_cen, s_sq, s_var, s_ln2, s_grs = (sem(n) for n in ("gn_mean", "gn_centred", "gn_squared", "gn_var", "gn_log", "gn_rstd"))
        s_gnorm, s_gaff, s_gated = sem("gn_normalised"), sem("gn_scaled"), sem("gated_ready")
        s_wo, s_x2, s_t2, s_xc0, s_xc = sem("b_wo_done"), sem("x2_ready"), sem("x2_transposed"), sem("xc_state"), sem("xc_ready")
        s_sx2, s_xk2, s_xr2 = sem("sx2_ready"), sem("xk2_ready"), sem("xr2_ready")
        s_fk, s_relu, s_kk, s_fr, s_rr = (sem(n) for n in ("wfk_done", "relu_ready", "kk_ready", "wfr_done", "rr_ready"))
        s_fv, s_ff, s_fin = sem("wfv_done"), sem("ffn_scaled"), sem("out_ready")

        N_ITER = B + 2
        LOOP = (2, B // 2 - 1)

        def run(engine, step):
            for i in range(2 * LOOP[0]):
                step((i // 2, i % 2), True, i >= 1, i >= 2, i == 0)
            with engine.Fori(*LOOP) as k:
                for q in range(2):
                    step((k, q), True, True, True, False)
            for i in range(2 * LOOP[1], N_ITER):
                step((i // 2, i % 2), i < B, i <= B, True, False)

        block = ctx.enter_context(nc.Block())

        @block.sync
        def _(sp):
            def load_x1(b):
                if at_least(b, 2):
                    sp.wait_ge(s_ln, count(later(b, -2), 1, 1))
                sp.dma_start(x1[:, b[1]], A["x1"][index(b)]).then_inc(s_x1[b[1]], 16)

            sp.dma_start(ident[:], A["ident"]).then_inc(s_c["ident"], 16)
            load_x1((0, 0))
            sp.dma_start(vec[:], A["vec"]).then_inc(s_c["vec"], 16)
            sp.dma_start(rows[:], A["rows"]).then_inc(s_c["rows"], 16)
            load_x1((0, 1))
            sp.dma_start(maa1[:], A["maa1"]).then_inc(s_c["maa1"], 16)
            sp.wait_ge(s_zero, 2)
            for f in range(MAA):
                r = f % HG * MD
                sp.dma_start(maa2[r:r + MD, f], A["maa2"][f]).then_inc(s_c["maa2"], 16)
            sp.dma_start(td1[:], A["td1"]).then_inc(s_c["td1"], 16)
            sp.dma_start(td2[0:TD, :], A["td2"]).then_inc(s_c["td2"], 16)
            sp.dma_start(kv[:].rearrange("p a b -> p (a b)"), A["spread"]).then_inc(s_c["spread"], 16)
            sp.dma_start(headsum[:], A["headsum"]).then_inc(s_c["headsum"], 16)
            sp.dma_start(s0[:], A["s0"]).then_inc(s_c["s0"], 16)
            sp.dma_start(collect[:], A["collect"]).then_inc(s_c["collect"], 16)

            def step(n, pre, scan, post, first):
                if post:
                    l = later(n, -2)
                    if at_least(l, 2):
                        sp.wait_ge(s_x2, count(later(l, -2), 1, 1))
                    sp.dma_start(x1p[:, l[1]], A["x1"][index(l)]).then_inc(s_x1p[l[1]], 16)
                if pre and not first and not is_batch(n, B - 1):
                    load_x1(later(n, 1))
                if post:
                    sp.wait_ge(s_fin, count(l, 1, 1))
                    sp.dma_start(A["out"][index(l)], fin[:, l[1]]).then_inc(s_store[l[1]], 16)

            run(sp, step)
            for q in range(2):
                sp.wait_ge(s_store[q], 16 * (B // 2))

        @block.gpsimd
        def _(pool):
            pool.memset(maa2[:], 0.0).then_inc(s_zero, 1)
            pool.memset(td2[:], 0.0).then_inc(s_zero, 1)
            pool.memset(neg_half[:], -0.5)
            pool.memset(wdec[:], 0.0)
            pool.memset(th[:], 0.0)
            pool.memset(ttd[:], 0.0)
            pool.memset(ln_eps[:], EPS).then_inc(s_zero, 1)
            pool.wait_ge(s_zero, 3)
            pool.wait_ge(s_c["rows"], 16)
            pool.wait_ge(s_c["s0"], 16)
            pool.wait_ge(s_spread, 1)

            def rstd1(b):
                pool.wait_ge(s_ve, count(b, 1, 1))
                pool.tensor_tensor(rs[:], ve[:], neg_half[:], ALU.pow).then_inc(s_rs, 1)

            def xa_state(b):
                if at_least(b, 1):
                    pool.wait_ge(s_xm, count(later(b, -1), MAA, MAA))
                pool.tensor_copy(xa[:, :, 0:1], rows[:, index(b), 1, :].unsqueeze(2)).then_inc(s_xa0, 1)

            def mix(b, f):
                pool.wait_ge(s_mixed, count(b, MAA, f + 1))
                if f == 2:
                    pool.wait_ge(s_td1, count(b, 1, 1))
                if f == 3:
                    pool.wait_ge(s_vmm, count(b, 1, 1))
                if f == 4:
                    pool.wait_ge(s_kmm, count(b, 1, 1))
                if f == 0 and at_least(b, 1):
                    pool.wait_ge(s_gmm, count(later(b, -1), 1, 1))
                pool.tensor_tensor(xm[:, f % 2], mixed[:, f % 2], xa[:, :, 1:T + 1], ALU.add).then_inc(s_xm, 1)

            def kv_state(m, j):
                if j >= NRING:
                    pool.wait_ge(s_st, count(m, S, j - NRING + 1))
                elif at_least(m, 1):
                    pool.wait_ge(s_st, count(later(m, -1), S, S + j - NRING + 1))
                pool.tensor_copy(kv[:, j % NRING, 0:CT].rearrange("p (c t) -> p c t", c=C)[:, :, 0:1],
                                 s0[:, index(m), :, j:j + 1]).then_inc(s_kv0, 1)

            def product(m, j):
                pool.wait_ge(s_st, count(m, S, j + 1))
                if j >= NRING:
                    pool.wait_ge(s_red, count(m, S, j - NRING + 1))
                elif at_least(m, 1):
                    pool.wait_ge(s_red, count(later(m, -1), S, S + j - NRING + 1))
                pool.tensor_tensor(rst[:, j % NRING], st[:, j % NRING], rec[:, m[1]].rearrange("p c t -> p (c t)"),
                                   ALU.mult).then_inc(s_even, 1)

            def step(n, pre, scan, post, first):
                m, l = later(n, -1), later(n, -2)
                if first:
                    rstd1(n)
                if pre:
                    xa_state(n)
                if scan:
                    pool.wait_ge(s_r, count(m, 1, 1))
                    if at_least(m, 1):
                        pool.wait_ge(s_bonus, count(later(m, -1), 1, 1))
                    pool.tensor_tensor(rk[:], rec[:, m[1]], key[:, m[1]], ALU.mult).then_inc(s_rk, 1)
                for s in range(S):
                    if scan:
                        for j in ([0, 1] if s == 0 else [s + 1] if s + 1 < S else []):
                            kv_state(m, j)
                        if s >= 1 and (s - 1) % 2 == 0:
                            product(m, s - 1)
                    if pre and s in MIX_SLOT:
                        mix(n, MIX_SLOT.index(s))
                    if post and s == 5:
                        pool.wait_ge(s_gaff, count(l, 1, 1))
                        pool.wait_ge(s_g, count(l, 1, 1))
                        if at_least(l, 1):
                            pool.wait_ge(s_wo, count(later(l, -1), 1, 1))
                        pool.tensor_tensor(gated[:], sq[:], gate2[:, l[1]], ALU.mult).then_inc(s_gated, 1)
                    if post and s == 8:
                        pool.wait_ge(s_vep, count(l, 1, 1))
                        pool.tensor_tensor(rsp[:], vep[:], neg_half[:], ALU.pow).then_inc(s_rsp, 1)
                        if at_least(l, 1):
                            pool.wait_ge(s_xr2, count(later(l, -1), 1, 1))
                        pool.tensor_copy(xc[:, :, 0:1], rows[:, index(l), 0, :].unsqueeze(2)).then_inc(s_xc0, 1)
                    if pre and s == 14 and not is_batch(n, B - 1):
                        rstd1(later(n, 1))

            run(pool, step)

        @block.vector
        def _(dve):
            dve.wait_ge(s_c["vec"], 16)
            dve.tensor_scalar(half_gn[:, 0], vec[:, VEC["gn_w"]], 0.5, None, ALU.mult)
            dve.tensor_scalar(half_gn[:, 1], vec[:, VEC["gn_b"]], 0.5, None, ALU.mult)
            dve.wait_ge(s_c["headsum"], 16)
            dve.tensor_scalar(headmean[:], headsum[:], 1.0 / S, None, ALU.mult)
            for c in range(C):
                last = dve.tensor_scalar(bonus_w[:, c], headsum[:], vec[:, VEC["u"], c:c + 1], None, ALU.mult)
            last.then_inc(s_setup, 1)
            dve.wait_ge(s_zero, 3)
            dve.wait_ge(s_spread, 1)

            def ln_stats(b, src, loaded, bn6, mv, ve, s_bn, s_mv, s_ve):
                dve.wait_ge(*loaded)
                dve.bn_stats(bn6[:], src).then_inc(s_bn, 1)
                dve.wait_ge(s_bn, count(b, 1, 1))
                dve.memset(ve[:], 0.0)
                dve.bn_aggr(mv[:], bn6[:]).then_inc(s_mv, 1)
                dve.wait_ge(s_mv, count(b, 1, 1))
                dve.tensor_scalar(ve[:], mv[:, 1:2], EPS, None, ALU.add).then_inc(s_ve, 1)

            def stats1(b):
                ln_stats(b, x1[:, b[1]], (s_x1[b[1]], 16 * (b[0] + 1)), bn6, mv, ve, s_bn, s_mv, s_ve)

            def apply1(b):
                dve.wait_ge(s_rs, count(b, 1, 1))
                if at_least(b, 1):
                    dve.wait_ge(s_t1, count(later(b, -1), 1, 1))
                dve.tensor_scalar(ln_tok[:], x1[:, b[1]], mv[:, 0:1], rs[:, 0:1], ALU.subtract, ALU.mult).then_inc(s_ln, 1)

            def token_shift(b):
                dve.wait_ge(s_xa, count(b, 1, 1))
                dve.wait_ge(s_xa0, count(b, 1, 1))
                if at_least(b, 1):
                    dve.wait_ge(s_w1, count(later(b, -1), 1, 1))
                dve.tensor_tensor(sx[:], xa[:, :, 0:T], xa[:, :, 1:T + 1], ALU.subtract).then_inc(s_sx, 1)
                dve.wait_ge(s_sx, count(b, 1, 1))
                for c in range(C):
                    last = dve.scalar_tensor_tensor(out=xin[:, c], in0=sx[:, c], scalar=vec[:, VEC["maa_x"], c:c + 1],
                                                    in1=xa[:, c, 1:T + 1], op0=ALU.mult, op1=ALU.add)
                last.then_inc(s_xin, 1)

            def mix(b, f):
                dve.wait_ge(s_mixmm, count(b, MAA, f + 1))
                if f >= 2 or at_least(b, 1):
                    dve.wait_ge(s_xm, count(b, MAA, max(f - 1, 0)))
                src = pre_bank[MIX_USE[f] % 3]
                for c in range(C):
                    last = dve.scalar_tensor_tensor(out=mixed[:, f % 2, c], in0=src[:, c * T:(c + 1) * T],
                                                    scalar=vec[:, VEC[MIXES[f]], c:c + 1], in1=sx[:, c],
                                                    op0=ALU.add, op1=ALU.mult)
                last.then_inc(s_mixed, 1)

            def value_low(b):
                dve.wait_ge(s_v, count(b, 1, 1))
                if at_least(b, 2):
                    dve.wait_ge(s_vrep, count(later(b, -2), S, S))
                dve.tensor_tensor(vlo[:, b[1]], v[:, b[1]], vhi[:, b[1]].bitcast(F32), ALU.subtract).then_inc(s_vlo, 1)

            def gate(b):
                dve.wait_ge(s_tg, count(b, 1, 1))
                if at_least(b, 2):
                    dve.wait_ge(s_gated, count(later(b, -2), 1, 1))
                dve.scalar_tensor_tensor(out=gate2[:, b[1]].rearrange("p c t -> p (c t)"), in0=tg[:].rearrange("p c t -> p (c t)"),
                                         scalar=1.0, in1=pre_bank[11 % 3][:, 0:CT], op0=ALU.add, op1=ALU.mult).then_inc(s_g, 1)

            def key_value(m, j):
                dve.wait_ge(s_vrep, count(m, S, j + 1))
                if j == 0:
                    dve.wait_ge(s_k, count(m, 1, 1))
                if j >= NRING or at_least(m, 1):
                    dve.wait_ge(s_st, count(m, S, j - NRING + 1))
                src = vrep_bank[j % 2][:, 0:CT].rearrange("p (c t) -> p c t", c=C)
                dst = kv[:, j % NRING, 0:CT].rearrange("p (c t) -> p c t", c=C)
                dve.tensor_tensor(dst[:, :, 1:T], src[:, :, 0:T - 1], key[:, m[1], :, 0:T - 1], ALU.mult).then_inc(s_kv, 1)

            def scan(m, j):
                if j == 0:
                    dve.wait_ge(s_wdec, count(m, 1, 1))
                dve.wait_ge(s_kv, count(m, S, j + 1))
                dve.wait_ge(s_kv0, count(m, S, j + 1))
                if j >= NRING or at_least(m, 1):
                    if j % 2 == 0:
                        dve.wait_ge(s_even, count(m, S // 2, (j - NRING) // 2 + 1))
                    else:
                        dve.wait_ge(s_odd, count(m, S // 2, (j - NRING) // 2 + 1))
                dve.tensor_tensor_scan(st[:, j % NRING], wdec[:, m[1]].rearrange("p c t -> p (c t)"), kv[:, j % NRING, 0:CT], 0.0,
                                       ALU.mult, ALU.add).then_inc(s_st, 1)

            def product(m, j):
                dve.wait_ge(s_st, count(m, S, j + 1))
                if j >= NRING or at_least(m, 1):
                    dve.wait_ge(s_red, count(m, S, j - NRING + 1))
                dve.tensor_tensor(rst[:, j % NRING], st[:, j % NRING], rec[:, m[1]].rearrange("p c t -> p (c t)"),
                                  ALU.mult).then_inc(s_odd, 1)

            def bonus_value(m):
                dve.wait_ge(s_bonus, count(m, 1, 1))
                if at_least(m, 1):
                    dve.wait_ge(s_wkv, count(later(m, -1), 1, 1))
                dve.tensor_tensor(bv[:].rearrange("p c t -> p (c t)"), post_bank[1][:, 0:CT],
                                  v[:, m[1]].rearrange("p c t -> p (c t)"), ALU.mult).then_inc(s_bv, 1)

            def wkv_sum(m):
                dve.wait_ge(s_red, count(m, S, S))
                dve.wait_ge(s_bv, count(m, 1, 1))
                if at_least(m, 1):
                    dve.wait_ge(s_cen, count(later(m, -1), 1, 1))
                dve.tensor_tensor(wkv[:].rearrange("p c t -> p (c t)"), out_bank[:, 0:CT], bv[:].rearrange("p c t -> p (c t)"),
                                  ALU.add).then_inc(s_wkv, 1)

            def centre(l):
                dve.wait_ge(s_mean, count(l, 1, 1))
                if at_least(l, 1):
                    dve.wait_ge(s_gaff, count(later(l, -1), 1, 1))
                dve.tensor_tensor(cen[:].rearrange("p c t -> p (c t)"), wkv[:].rearrange("p c t -> p (c t)"),
                                  post_bank[0][:, 0:CT], ALU.subtract).then_inc(s_cen, 1)

            def group_norm(l):
                dve.wait_ge(s_grs, count(l, 1, 1))
                dve.tensor_tensor(cen[:], cen[:], sq[:], ALU.mult).then_inc(s_gnorm, 1)

            def residual(l):
                dve.wait_ge(s_wo, count(l, 1, 1))
                dve.wait_ge(s_x1p[l[1]], 16 * (l[0] + 1))
                dve.tensor_tensor(x2[:], post_bank[0][0:T, :], x1p[:, l[1]], ALU.add).then_inc(s_x2, 1)
                ln_stats(l, x2[:], (s_x2, count(l, 1, 1)), bn6p, mvp, vep, s_bnp, s_mvp, s_vep)

            def apply2(l):
                dve.wait_ge(s_rsp, count(l, 1, 1))
                dve.tensor_scalar(ln2_tok[:], x2[:], mvp[:, 0:1], rsp[:, 0:1], ALU.subtract, ALU.mult).then_inc(s_lnp, 1)

            def shift2(l):
                dve.wait_ge(s_xc, count(l, 1, 1))
                dve.wait_ge(s_xc0, count(l, 1, 1))
                dve.tensor_tensor(sx2[:], xc[:, :, 0:T], xc[:, :, 1:T + 1], ALU.subtract).then_inc(s_sx2, 1)
                dve.wait_ge(s_sx2, count(l, 1, 1))
                for dst, name, ready in ((xk2, "ffn_k", s_xk2), (xr2, "ffn_r", s_xr2)):
                    for c in range(C):
                        last = dve.scalar_tensor_tensor(out=dst[:, c], in0=sx2[:, c], scalar=vec[:, VEC[name], c:c + 1],
                                                        in1=xc[:, c, 1:T + 1], op0=ALU.mult, op1=ALU.add)
                    last.then_inc(ready, 1)

            def finish(l):
                dve.wait_ge(s_fv, count(l, 1, 1))
                dve.wait_ge(s_rr, count(l, 1, 1))
                if at_least(l, 2):
                    dve.wait_ge(s_store[l[1]], 16 * l[0])
                dve.scalar_tensor_tensor(out=fin[:, l[1]], in0=trr[:], scalar=1.0, in1=post_bank[0][0:T, :], op0=ALU.add,
                                         op1=ALU.mult).then_inc(s_ff, 1)
                dve.wait_ge(s_ff, count(l, 1, 1))
                dve.scalar_tensor_tensor(out=fin[:, l[1]], in0=fin[:, l[1]], scalar=0.5, in1=x2[:], op0=ALU.mult,
                                         op1=ALU.add).then_inc(s_fin, 1)

            def step(n, pre, scans, post, first):
                m, l = later(n, -1), later(n, -2)
                if first:
                    stats1(n)
                    apply1(n)
                for s in range(S):
                    if scans:
                        key_value(m, s)
                        if s >= 1 and (s - 1) % 2 == 1:
                            product(m, s - 1)
                        scan(m, s)
                    if pre and s == 1:
                        token_shift(n)
                    if post and s == 1:
                        centre(l)
                    if scans and s == 2:
                        bonus_value(m)
                    if post and s == 4:
                        group_norm(l)
                    if pre and s in MIX_SLOT:
                        mix(n, MIX_SLOT.index(s))
                    if pre and s == 7:
                        value_low(n)
                    if post and s == 8:
                        residual(l)
                    if post and s == 9:
                        apply2(l)
                    if post and s == 11:
                        shift2(l)
                    if pre and s == 12:
                        gate(n)
                    if pre and not is_batch(n, B - 1):
                        if s == 13:
                            stats1(later(n, 1))
                        if s == 14:
                            apply1(later(n, 1))
                if scans:
                    product(m, S - 1)
                    wkv_sum(m)
                if post:
                    finish(l)

            run(dve, step)

        @block.scalar
        def _(act):
            act.wait_ge(s_c["spread"], 16)
            act.copy(spread[:].rearrange("p j q -> p (j q)"), kv[:].rearrange("p a b -> p (a b)")).then_inc(s_spread, 1)
            act.wait_ge(s_c["vec"], 16)
            act.wait_ge(s_zero, 3)

            def affine(dst, src, scale, bias):
                for c in range(C):
                    last = act.activation(dst(c), src(c), ACT.Identity, scale=scale[:, c:c + 1], bias=bias[:, c:c + 1])
                return last

            def xa_affine(b):
                act.wait_ge(s_t1, count(b, 1, 1))
                if at_least(b, 1):
                    act.wait_ge(s_xm, count(later(b, -1), MAA, MAA))
                affine(lambda c: xa[:, c, 1:T + 1], lambda c: pre_bank[0][:, c * T:(c + 1) * T], vec[:, VEC["ln1_w"]],
                       vec[:, VEC["ln1_b"]]).then_inc(s_xa, 1)

            def tanh_maa(b):
                act.wait_ge(s_w1, count(b, 1, 1))
                if at_least(b, 1):
                    act.wait_ge(s_mixmm, count(later(b, -1), MAA, MAA))
                act.activation(th[:, 0], pre_bank[1][:, 0:T], ACT.Tanh)
                act.activation(th[0:MD, 1], pre_bank[1][0:MD, T:2 * T], ACT.Tanh).then_inc(s_th, 1)

            def tanh_td(b):
                act.wait_ge(s_td1, count(b, 1, 1))
                if at_least(b, 1):
                    act.wait_ge(s_td2, count(later(b, -1), 1, 1))
                act.activation(ttd[0:TD], pre_bank[0][0:TD, 0:T], ACT.Tanh).then_inc(s_ttd, 1)

            def decay(b):
                act.wait_ge(s_td2, count(b, 1, 1))
                if at_least(b, 1):
                    act.wait_ge(s_wdec, count(later(b, -1), 1, 1))
                for c in range(C):
                    last = act.activation(etd[:, c], pre_bank[0][:, c * T:(c + 1) * T], ACT.Exp,
                                          bias=vec[:, VEC["time_decay"], c:c + 1])
                last.then_inc(s_etd, 1)
                act.wait_ge(s_etd, count(b, 1, 1))
                if at_least(b, 2):
                    act.wait_ge(s_st, count(later(b, -2), S, S))
                act.activation(wdec[:, b[1], :, 1:T], etd[:, :, 0:T - 1], ACT.Exp, scale=-1.0).then_inc(s_wdec, 1)

            def copy_value(b):
                act.wait_ge(s_vmm, count(b, 1, 1))
                if at_least(b, 2):
                    act.wait_ge(s_bv, count(later(b, -2), 1, 1))
                    act.wait_ge(s_vlo, count(later(b, -2), 1, 1))
                    act.wait_ge(s_vrep, count(later(b, -2), S, S))
                src = pre_bank[5 % 3][:, 0:CT]
                act.copy(vhi[:, b[1]].rearrange("p c t -> p (c t)"), src)
                act.copy(v[:, b[1]].rearrange("p c t -> p (c t)"), src).then_inc(s_v, 1)

            def copy_key(b):
                act.wait_ge(s_kmm, count(b, 1, 1))
                if at_least(b, 2):
                    act.wait_ge(s_kv, count(later(b, -2), S, S))
                    act.wait_ge(s_rk, count(later(b, -2), 1, 1))
                act.copy(key[:, b[1]].rearrange("p c t -> p (c t)"), pre_bank[7 % 3][:, 0:CT]).then_inc(s_k, 1)

            def copy_rec(b):
                act.wait_ge(s_rmm, count(b, 1, 1))
                if at_least(b, 2):
                    act.wait_ge(s_even, count(later(b, -2), S // 2, S // 2))
                    act.wait_ge(s_odd, count(later(b, -2), S // 2, S // 2))
                act.copy(rec[:, b[1]].rearrange("p c t -> p (c t)"), pre_bank[9 % 3][:, 0:CT]).then_inc(s_r, 1)

            def tanh_gate(b):
                act.wait_ge(s_gmm, count(b, 1, 1))
                if at_least(b, 1):
                    act.wait_ge(s_g, count(later(b, -1), 1, 1))
                act.activation(tg[:].rearrange("p c t -> p (c t)"), pre_bank[11 % 3][:, 0:CT], ACT.Tanh,
                               scale=0.5).then_inc(s_tg, 1)

            def square(l):
                act.wait_ge(s_cen, count(l, 1, 1))
                if at_least(l, 1):
                    act.wait_ge(s_gated, count(later(l, -1), 1, 1))
                act.activation(sq[:], cen[:], ACT.Square).then_inc(s_sq, 1)

            def gn_rstd(l):
                act.wait_ge(s_var, count(l, 1, 1))
                flat = sq[:].rearrange("p c t -> p (c t)")
                act.activation(flat, post_bank[1][:, 0:CT], ACT.Ln, bias=ln_eps[:, 0:1]).then_inc(s_ln2, 1)
                act.wait_ge(s_ln2, count(l, 1, 1))
                act.activation(flat, flat, ACT.Exp, scale=-0.5).then_inc(s_grs, 1)

            def gn_affine(l):
                act.wait_ge(s_gnorm, count(l, 1, 1))
                affine(lambda c: sq[:, c], lambda c: cen[:, c], half_gn[:, 0], half_gn[:, 1]).then_inc(s_gaff, 1)

            def xc_affine(l):
                act.wait_ge(s_t2, count(l, 1, 1))
                if at_least(l, 1):
                    act.wait_ge(s_xr2, count(later(l, -1), 1, 1))
                affine(lambda c: xc[:, c, 1:T + 1], lambda c: post_bank[1][:, c * T:(c + 1) * T], vec[:, VEC["ln2_w"]],
                       vec[:, VEC["ln2_b"]]).then_inc(s_xc, 1)

            def relu_square(l):
                act.wait_ge(s_fk, count(l, 1, 1))
                if at_least(l, 1):
                    act.wait_ge(s_fv, count(later(l, -1), 1, 1))
                flat = kk[:].rearrange("p c t -> p (c t)")
                act.activation(flat, post_bank[0][:, 0:CT], ACT.Relu).then_inc(s_relu, 1)
                act.wait_ge(s_relu, count(l, 1, 1))
                act.activation(flat, flat, ACT.Square).then_inc(s_kk, 1)

            def receptance(l):
                act.wait_ge(s_fr, count(l, 1, 1))
                if at_least(l, 1):
                    act.wait_ge(s_ff, count(later(l, -1), 1, 1))
                act.activation(trr[:], post_bank[1][0:T, :], ACT.Tanh, scale=0.5).then_inc(s_rr, 1)

            def step(n, pre, scans, post, first):
                l = later(n, -2)
                if pre:
                    xa_affine(n)
                if is_batch(l, 0):
                    act.wait_ge(s_setup, 1)
                if post:
                    square(l)
                if pre:
                    tanh_maa(n)
                if post:
                    gn_rstd(l)
                if pre:
                    tanh_td(n)
                if post:
                    gn_affine(l)
                if pre:
                    decay(n)
                    copy_value(n)
                    copy_key(n)
                    copy_rec(n)
                if post:
                    xc_affine(l)
                if pre:
                    tanh_gate(n)
                if post:
                    relu_square(l)
                    receptance(l)

            run(act, step)

        @block.tensor
        def _(pe):
            for name in ("ident", "headsum", "collect", "maa1", "td1", "td2"):
                pe.wait_ge(s_c[name], 16)
            pe.wait_ge(s_c["maa2"], 16 * MAA)
            pe.wait_ge(s_spread, 1)
            pe.wait_ge(s_setup, 1)
            pe.wait_ge(s_zero, 3)
            for s in w_loaded.values():
                pe.wait_ge(s, 16)

            def transposes(dst, src):
                for c in range(C):
                    last = pe.transpose(dst[:, c * T:(c + 1) * T], src[:, c * P:(c + 1) * P], ident[0:T, 0:T])
                return last

            def channel_major(dst, w, src):
                for o in range(C):
                    for c in range(C):
                        last = pe.matmul(dst[:, o * T:(o + 1) * T], w[:, c, o * P:(o + 1) * P], src[:, c], start=(c == 0),
                                         stop=(c == C - 1))
                return last

            def token_major(dst, w, src):
                for c in range(C):
                    last = pe.matmul(dst[0:T, :], src[:, c], w[:, c], start=(c == 0), stop=(c == C - 1))
                return last

            def transpose_x(b):
                pe.wait_ge(s_ln, count(b, 1, 1))
                if at_least(b, 1):
                    pe.wait_ge(s_r, count(later(b, -1), 1, 1))
                transposes(pre_bank[0], ln_tok).then_inc(s_t1, 1)

            def maa_first(b):
                pe.wait_ge(s_xin, count(b, 1, 1))
                if at_least(b, 1):
                    pe.wait_ge(s_mixed, count(later(b, -1), MAA, MAA))
                for o, (a, z) in enumerate(((0, P), (P, MAA * MD))):
                    for c in range(C):
                        last = pe.matmul(pre_bank[1][0:z - a, o * T:(o + 1) * T], maa1[:, c, a:z], xin[:, c], start=(c == 0),
                                         stop=(c == C - 1))
                last.then_inc(s_w1, 1)

            def maa_second(b, f):
                if f == 0:
                    pe.wait_ge(s_th, count(b, 1, 1))
                    if at_least(b, 1):
                        pe.wait_ge(s_g, count(later(b, -1), 1, 1))
                elif f == 1:
                    pe.wait_ge(s_th, count(b, 1, 1))
                elif f == 2:
                    pe.wait_ge(s_etd, count(b, 1, 1))
                elif f == 3:
                    pe.wait_ge(s_v, count(b, 1, 1))
                else:
                    pe.wait_ge(s_k, count(b, 1, 1))
                dst = pre_bank[MIX_USE[f] % 3]
                row = MIX_ROW[f]
                for o in range(C):
                    last = pe.matmul(dst[:, o * T:(o + 1) * T], maa2[:, row, o * P:(o + 1) * P], th[:, row // HG], start=True,
                                     stop=True)
                last.then_inc(s_mixmm, 1)

            def decay_first(b):
                pe.wait_ge(s_xm, count(b, MAA, 1))
                pe.wait_ge(s_xa, count(b, 1, 1))
                for c in range(C):
                    last = pe.matmul(pre_bank[0][0:TD, 0:T], td1[:, c], xm[:, 0, c], start=(c == 0), stop=(c == C - 1))
                last.then_inc(s_td1, 1)

            def decay_second(b):
                pe.wait_ge(s_ttd, count(b, 1, 1))
                for o in range(C):
                    last = pe.matmul(pre_bank[0][:, o * T:(o + 1) * T], td2[:, o * P:(o + 1) * P], ttd[:], start=True, stop=True)
                last.then_inc(s_td2, 1)

            def project(b, f, w, done):
                pe.wait_ge(s_xm, count(b, MAA, f + 1))
                pe.wait_ge(s_mixed, count(b, MAA, f))
                channel_major(pre_bank[(MIX_USE[f] + 1) % 3], W[w], xm[:, f % 2]).then_inc(done, 1)

            def bonus(m):
                pe.wait_ge(s_rk, count(m, 1, 1))
                if at_least(m, 2):
                    pe.wait_ge(s_rr, count(later(m, -2), 1, 1))
                for c in range(C):
                    last = pe.matmul(post_bank[1][:, c * T:(c + 1) * T], bonus_w[:, c], rk[:, c], start=True, stop=True)
                last.then_inc(s_bonus, 1)

            def spread_value(m, j):
                if j == 0:
                    pe.wait_ge(s_vlo, count(m, 1, 1))
                if j >= 2 or at_least(m, 1):
                    pe.wait_ge(s_kv, count(m, S, j - 1))
                for part in (vhi, vlo):
                    last = pe.matmul(vrep_bank[j % 2][:, 0:CT], spread[:, j], part[:, m[1]].rearrange("p c t -> p (c t)"),
                                     start=(part is vhi), stop=(part is vlo))
                last.then_inc(s_vrep, 1)

            def reduce(m, j):
                if j % 2 == 0:
                    pe.wait_ge(s_even, count(m, S // 2, j // 2 + 1))
                else:
                    pe.wait_ge(s_odd, count(m, S // 2, j // 2 + 1))
                if j == 0 and at_least(m, 1):
                    pe.wait_ge(s_wkv, count(later(m, -1), 1, 1))
                pe.matmul(out_bank[:, 0:CT], collect[:, j], rst[:, j % NRING], start=(j == 0), stop=(j == S - 1)).then_inc(s_red, 1)

            def gn_mean(l):
                pe.wait_ge(s_wkv, count(l, 1, 1))
                if at_least(l, 1):
                    pe.wait_ge(s_ff, count(later(l, -1), 1, 1))
                pe.matmul(post_bank[0][:, 0:CT], headmean[:], wkv[:].rearrange("p c t -> p (c t)"), start=True,
                          stop=True).then_inc(s_mean, 1)

            def gn_var(l, scans):
                pe.wait_ge(s_sq, count(l, 1, 1))
                if scans:
                    pe.wait_ge(s_bv, count(later(l, 1), 1, 1))
                pe.matmul(post_bank[1][:, 0:CT], headmean[:], sq[:].rearrange("p c t -> p (c t)"), start=True,
                          stop=True).then_inc(s_var, 1)

            def step(n, pre, scans, post, first):
                m, l = later(n, -1), later(n, -2)
                for s in range(S):
                    if scans:
                        spread_value(m, s)
                    if pre and s == 0:
                        transpose_x(n)
                    if scans and s == 0:
                        bonus(m)
                    if post and s == 0:
                        gn_mean(l)
                    if scans and s >= 2:
                        reduce(m, s - 2)
                    if pre and s == 1:
                        maa_first(n)
                    if post and s == 3:
                        gn_var(l, scans)
                    if pre and s in MIX_SLOT:
                        maa_second(n, MIX_SLOT.index(s))
                    if pre and s == 4:
                        decay_first(n)
                    if pre and s == 5:
                        decay_second(n)
                    if pre and s == 6:
                        project(n, 1, "wv", s_vmm)
                    if post and s == 7:
                        pe.wait_ge(s_gated, count(l, 1, 1))
                        token_major(post_bank[0], W["wo"], gated).then_inc(s_wo, 1)
                    if pre and s == 8:
                        project(n, 2, "wk", s_kmm)
                    if pre and s == 10:
                        project(n, 3, "wr", s_rmm)
                    if post and s == 10:
                        pe.wait_ge(s_lnp, count(l, 1, 1))
                        transposes(post_bank[1], ln2_tok).then_inc(s_t2, 1)
                    if pre and s == 12:
                        project(n, 4, "wg", s_gmm)
                    if post and s == 12:
                        pe.wait_ge(s_xk2, count(l, 1, 1))
                        channel_major(post_bank[0], W["wfk"], xk2).then_inc(s_fk, 1)
                    if post and s == 13:
                        pe.wait_ge(s_xr2, count(l, 1, 1))
                        token_major(post_bank[1], W["wfr"], xr2).then_inc(s_fr, 1)
                    if post and s == 15:
                        pe.wait_ge(s_kk, count(l, 1, 1))
                        token_major(post_bank[0], W["wfv"], kk).then_inc(s_fv, 1)
                if scans:
                    reduce(m, S - 2)
                    reduce(m, S - 1)

            run(pe, step)


BLOCK_WEIGHTS = {"wr": "L1_xattn_Wr", "wk": "L1_xattn_Wk", "wv": "L1_xattn_Wv", "wg": "L1_xattn_Wg", "wo": "L1_xattn_Wo",
                 "wfk": "L1_xattn_Wfk", "wfr": "L1_xattn_Wfr", "wfv": "L1_xattn_Wfv"}


def program(nc, A):
    with ExitStack() as ctx:
        W = {n: ctx.enter_context(nc.sbuf_tensor(f"b_{n}", [P, C, D], F32)) for n in BLOCK_WEIGHTS}
        w_loaded = {n: ctx.enter_context(nc.semaphore(f"b_{n}_loaded")) for n in BLOCK_WEIGHTS}
        cross_attention(nc, A, W, w_loaded)
        rwkv_block(nc, A, W, w_loaded)


def kernel(**inputs):
    import numpy as _np
    import concourse.bacc as _bacc
    from concourse import mybir as _mybir
    from concourse.bass_utils import run_bass_kernel_spmd as _run

    a = {name: _np.asarray(x) for name, x in inputs.items()}

    def channels(x):
        return x.reshape(C, P).T

    def weights(w):
        return w.T.reshape(C, P, -1).transpose(1, 0, 2)

    x, ctx = a["x"], a["ctx_2048"]
    maa = dict(zip(("maa_k", "maa_w", "maa_v", "maa_r", "maa_g"), a["L1_xattn_maa_stack"].reshape(MAA, D)))
    vectors = {"ln_gamma": a["L0_xattn_ln_gamma"], "ln_beta": a["L0_xattn_ln_beta"], "ffn_k": a["L1_xattn_ffn_maa_k"],
               "ffn_r": a["L1_xattn_ffn_maa_r"], "u": a["L1_xattn_u"].reshape(D)} | maa
    p = _np.arange(P)
    same_head = (p[:, None] // S == p[None, :] // S)
    j = _np.arange(S)[None, :, None]
    arrays = {
        "x": x,
        "xT": x.transpose(0, 2, 1).reshape(B, C, P, T).transpose(0, 2, 1, 3),
        "ctx": ctx,
        "mask": a["mask_BxS2_bf1"].view(_np.uint8),
        "vec": _np.stack([channels(vectors.get(n, a.get("L1_xattn_" + n))) for n in VECTORS], 1),
        "gate": a["L0_xattn_gate"].reshape(1, 1),
        "ident": _np.eye(P, dtype=_np.float32),
        "headmask": (p[:, None] // HD == _np.arange(HG)[None, :]).astype(_np.float32),
        "maa1": a["L1_xattn_maa_w1"].reshape(C, P, MAA * MD).transpose(1, 0, 2),
        "maa2": a["L1_xattn_maa_w2"],
        "td1": a["L1_xattn_td_w1"].reshape(C, P, TD).transpose(1, 0, 2),
        "td2": a["L1_xattn_td_w2"],
        "headsum": same_head.astype(_np.float32),
        "collect": (same_head[:, None, :] & (p[None, None, :] % S == j)).astype(_np.float32),
        "spread": (same_head[:, None, :] & (p[:, None, None] % S == j)).astype(_np.float32).reshape(P, S * P),
        "s0": ctx[:, 2:2 + S].reshape(B, C, P, S).transpose(2, 0, 1, 3),
        "rows": ctx[:, 0:2].reshape(B, 2, C, P).transpose(3, 0, 1, 2),
    }
    arrays |= {n: weights(a["L0_xattn_W" + n[1:]]) for n in ("wq", "wk", "wv", "wo")}
    arrays |= {"b_" + n: weights(a[source]) for n, source in BLOCK_WEIGHTS.items()}

    nc = _bacc.Bacc("TRN2", target_bir_lowering=False, num_devices=1)
    fed, A = {}, {}
    for name, array in arrays.items():
        fed[f"in_{name}"] = _np.ascontiguousarray(array)
        A[name] = nc.dram_tensor(f"in_{name}", array.shape, _mybir.dt.from_np(array.dtype), kind="ExternalInput").ap()
    A["x1"] = nc.dram_tensor("x1_between_layers", (B, T, D), F32, kind="Internal").ap()
    A["out"] = nc.dram_tensor("out_dram", (B, T, D), F32, kind="ExternalOutput").ap()
    program(nc, A)
    return _run(nc, [fed], core_ids=[0]).results[0]["out_dram"]
```

```python
from contextlib import ExitStack

import numpy as np

import concourse.bass as bass
from concourse import mybir

ALU = mybir.AluOpType
ACT = mybir.ActivationFunctionType
AX = mybir.AxisListType
F32 = mybir.dt.float32
F32R = mybir.dt.float32r
U8 = mybir.dt.uint8

P = 128
B, T, D = 16, 112, 512
TC = 375
KT = 3
TK = TC // KT
C = D // P
HEADS, HD = 16, 32
HG = P // HD
SCALE = HD ** -0.5
EPS = 1e-5
BANK = 512
LOWEST = -3.0e38

VECTORS = ["ln_gamma", "ln_beta", "ln1_w", "ln1_b", "ln2_w", "ln2_b", "maa_x", "maa_k", "maa_w", "maa_v", "maa_r",
           "maa_g", "time_decay", "gn_w", "gn_b", "ffn_k", "ffn_r", "u"]
S = 16
MAA, MD, TD = 5, 32, 64
NRING = 4
NPROD = 8
QUAD = 4
MIXES = ["maa_w", "maa_v", "maa_k", "maa_r", "maa_g"]
MIX_ROW = [1, 2, 0, 3, 4]
MIX_SLOT = [3, 5, 7, 9, 11]
MIX_BANK = [2, 0, 2, 1, 0]
USE_BANK = {"v": 0, "k": 2, "r": 1, "g": 2}
VEC = {name: n for n, name in enumerate(VECTORS)}


def index(b):
    return 2 * b[0] + b[1]


def later(b, steps):
    n = b[1] + steps
    return b[0] + n // 2, n % 2


def count(b, per_batch, done):
    return index(b) * per_batch + done


def at_least(b, n):
    return not isinstance(b[0], int) or index(b) >= n


def is_batch(b, n):
    return isinstance(b[0], int) and index(b) == n


def cross_attention(nc, A, ident, vec, W, w_loaded):
    with ExitStack() as ctx:
        def sb(name, shape, dt=F32):
            return ctx.enter_context(nc.sbuf_tensor(name, shape, dt))

        def sem(name):
            return ctx.enter_context(nc.semaphore(name))

        def sem2(name):
            return [sem(f"{name}_{q}") for q in range(2)]

        bank = [ctx.enter_context(nc.psum_tensor(f"a_bank{n}", [P, BANK], F32)) for n in range(8)]
        score_bank, proj_bank, q_bank, pt_bank, av_bank = bank[0:2], bank[2:4], bank[4], bank[5:7], bank[7]

        wq, wk, wv, wo = (sb(n, [P, C, D]) for n in ("wq_sb", "wk_sb", "wv_sb", "wo_sb"))
        headmask = sb("headmask_sb", [P, HG])
        gate = sb("gate_sb", [T, 1])
        tanh_gate = sb("tanh_gate", [T, 1])
        eps_exp = sb("a_eps_exp", [TK, KT])
        to_inf = sb("to_inf", [T, 3])
        mask8 = sb("mask8", [T, B, TC], U8)
        unmask = sb("unmask", [T, 2, TC])
        xT = sb("xT_sb", [P, 2, C, T])
        x_tok = sb("x_tok", [T, 2, D])
        ctx_tok = sb("ctx_tok", [TK, 2, KT, D])
        ctx_norm = sb("ctx_norm", [TK, KT, D])
        stats = sb("ctx_stats", [TK, KT, 6])
        meanvar = sb("ctx_meanvar", [TK, KT, 2])
        var_eps = sb("ctx_var_eps", [TK, KT])
        rstd = sb("ctx_rstd", [TK, KT])
        aT = sb("aT", [P, C, TC])
        keyT = sb("keyT", [P, 2, C, TC])
        value = sb("value", [TK, 2, KT, D])
        qpad = sb("qpad", [P, 2, C, HG, T])
        probs = sb("probs", [T, 2, HG, TC])
        maxes = sb("maxes", [T, 2, HG])
        negmax = sb("negmax", [T, 2, HG])
        sums = sb("sums", [T, 2, HG])
        inv = sb("inv", [T, 2, HG])
        probsT = sb("probsT", [TK, 2, KT, HG * T])
        attnT = sb("attnT", [P, C, T])
        x1 = sb("x1_sb", [T, 2, D])

        s_w = {n: sem(f"a_{n}_loaded") for n in ("wq", "wk", "wv", "wo", "ident", "headmask", "vec", "gate", "mask")}
        s_xT, s_xtok, s_ctx, s_x1st = sem2("xT_loaded"), sem2("xtok_loaded"), sem2("ctx_loaded"), sem2("x1_stored")
        s_gate = sem("gate_ready")
        s_const = sem("a_constants_set")
        s_unmask1 = sem("unmask_steps")
        s_stats, s_mv, s_ve = sem("ctx_stats_done"), sem("ctx_meanvar_done"), sem("ctx_vareps_done")
        s_rstd, s_ctxn = sem("ctx_rstd_done"), sem("ctx_normalised")
        s_proj, s_projev = sem("proj_done"), sem("proj_copied")
        s_q, s_qpad = sem("q_done"), sem("qpad_ready")
        s_score, s_masked, s_negmax = sem("score_done"), sem("score_masked"), sem("negmax_ready")
        s_exp, s_inv, s_probs = sem("exp_done"), sem("inv_ready"), sem("probs_ready")
        s_pt, s_ptev = sem("probs_transposed"), sem("probsT_ready")
        s_av, s_attn, s_wo, s_x1 = sem("av_done"), sem("attnT_ready"), sem("wo_done"), sem("x1_ready")

        FIRST, LOOP, LAST = [(0, 0), (0, 1), (1, 0), (1, 1)], (2, B // 2 - 1), [(B // 2 - 1, 0), (B // 2 - 1, 1), (B // 2, 0)]

        def run(engine, step):
            for n in FIRST:
                step(n, True, not is_batch(n, 0), True)
            with engine.Fori(*LOOP) as k:
                for q in range(2):
                    step((k, q), True, True, True)
            for n in LAST:
                step(n, not is_batch(n, B), True, is_batch(n, B - 2))

        block = ctx.enter_context(nc.Block())

        @block.sync
        def _(sp):
            def load_ctx(b):
                if at_least(b, 2):
                    sp.wait_ge(s_ctxn, count(later(b, -2), 1, 1))
                sp.dma_start(ctx_tok[:, b[1]], A["ctx"][index(b)].rearrange("(k p) d -> p k d", p=TK)).then_inc(s_ctx[b[1]], 16)

            def load_x(b):
                if at_least(b, 2):
                    sp.wait_ge(s_q, count(later(b, -2), 1, 1))
                sp.dma_start(xT[:, b[1]], A["xT"][index(b)]).then_inc(s_xT[b[1]], 16)

            def load_xtok(b):
                if at_least(b, 2):
                    sp.wait_ge(s_x1, count(later(b, -2), 1, 1))
                sp.dma_start(x_tok[:, b[1]], A["x"][index(b)]).then_inc(s_xtok[b[1]], 16)

            load_ctx((0, 0))
            sp.dma_start(vec[:], A["vec"]).then_inc(s_w["vec"], 16)
            sp.dma_start(ident[:], A["ident"]).then_inc(s_w["ident"], 16)
            sp.dma_start(headmask[:], A["headmask"]).then_inc(s_w["headmask"], 16)
            load_x((0, 0))
            sp.dma_start(wq[:], A["wq"]).then_inc(s_w["wq"], 16)
            sp.dma_start(wk[:], A["wk"]).then_inc(s_w["wk"], 16)
            load_ctx((0, 1))
            sp.dma_start(wv[:], A["wv"]).then_inc(s_w["wv"], 16)
            sp.dma_start(mask8[:], A["mask"].rearrange("(o b) t -> o b t", o=1).broadcast_to([T, B, TC])).then_inc(s_w["mask"], 16)
            sp.dma_start(gate[:], A["gate"].broadcast_to([T, 1])).then_inc(s_w["gate"], 16)
            sp.dma_start(wo[:], A["wo"]).then_inc(s_w["wo"], 16)

            def step(n, project, attend, normalise):
                if project and not is_batch(n, 0):
                    load_x(n)
                if attend:
                    load_xtok(later(n, -1))
                if normalise and not is_batch(n, 0):
                    load_ctx(later(n, 1))
                if is_batch(n, 1):
                    for name in W:
                        sp.dma_start(W[name][:], A["b_" + name]).then_inc(w_loaded[name], 16)
                if attend:
                    m = later(n, -1)
                    sp.wait_ge(s_x1, count(m, 1, 1))
                    sp.dma_start(A["x1"][index(m)], x1[:, m[1]]).then_inc(s_x1st[m[1]], 16)

            run(sp, step)
            for q in range(2):
                sp.wait_ge(s_x1st[q], 16 * (B // 2))

        @block.gpsimd
        def _(pool):
            for i, x in enumerate((1.0, 3.0e38, 10.0)):
                pool.memset(to_inf[:, i:i + 1], x)
            pool.memset(eps_exp[:], -0.5).then_inc(s_const, 1)

            def step(n, project, attend, normalise):
                if attend:
                    m = later(n, -1)
                    q = m[1]
                    if is_batch(m, 0):
                        pool.wait_ge(s_w["mask"], 16)
                    if at_least(m, 2):
                        pool.wait_ge(s_masked, count(later(m, -2), HEADS, HEADS))
                    pool.tensor_copy(unmask[:, q], mask8[:, index(m), :]).then_inc(s_unmask1, 1)
                    for i, op in enumerate((ALU.subtract, ALU.mult, ALU.mult)):
                        pool.wait_ge(s_unmask1, count(m, C, i + 1))
                        last = pool.tensor_tensor(unmask[:, q], unmask[:, q], to_inf[:, i:i + 1].broadcast_to([T, TC]), op)
                        last.then_inc(s_unmask1, 1)
                if normalise:
                    rsqrt(later(n, 1))

            def rsqrt(b):
                pool.wait_ge(s_ve, count(b, 1, 1))
                if at_least(b, 1):
                    pool.wait_ge(s_ctxn, count(later(b, -1), 1, 1))
                pool.tensor_tensor(rstd[:], var_eps[:], eps_exp[:], ALU.pow).then_inc(s_rstd, 1)

            pool.wait_ge(s_const, 1)
            rsqrt((0, 0))
            run(pool, step)

        @block.vector
        def _(dve):
            def ln_stats(b):
                dve.wait_ge(s_ctx[b[1]], 16 * (b[0] + 1))
                for k in range(KT):
                    last = dve.bn_stats(stats[:, k], ctx_tok[:, b[1], k])
                last.then_inc(s_stats, 1)
                dve.wait_ge(s_stats, count(b, 1, 1))
                dve.memset(var_eps[:], 0.0)
                for k in range(KT):
                    last = dve.bn_aggr(meanvar[:, k], stats[:, k])
                last.then_inc(s_mv, 1)
                dve.wait_ge(s_mv, count(b, 1, 1))
                dve.tensor_scalar(var_eps[:], meanvar[:, :, 1], EPS, None, ALU.add).then_inc(s_ve, 1)

            def ln_apply(b):
                dve.wait_ge(s_rstd, count(b, 1, 1))
                if at_least(b, 1):
                    dve.wait_ge(s_proj, count(later(b, -1), 11, C))
                for k in range(KT):
                    last = dve.tensor_scalar(ctx_norm[:, k], ctx_tok[:, b[1], k], meanvar[:, k, 0:1], rstd[:, k:k + 1],
                                             ALU.subtract, ALU.mult)
                last.then_inc(s_ctxn, 1)

            def pad_queries(b, c):
                if is_batch(b, 0) and c == 0:
                    dve.wait_ge(s_w["headmask"], 16)
                dve.wait_ge(s_q, count(b, 1, 1))
                dve.tensor_tensor(qpad[:, b[1], c], q_bank[:, c * T:(c + 1) * T].unsqueeze(1).broadcast_to([P, HG, T]),
                                  headmask[:].unsqueeze(2).broadcast_to([P, HG, T]), ALU.mult).then_inc(s_qpad, 1)

            def mask_scores(m, g):
                if g == 0:
                    dve.wait_ge(s_unmask1, count(m, C, C))
                if g >= 2 or at_least(m, 1):
                    dve.wait_ge(s_pt, count(m, C * KT, (g - 1) * KT))
                for i in range(HG):
                    h = g * HG + i
                    dve.wait_ge(s_score, count(m, HEADS, h + 1))
                    if i == 0:
                        dve.memset(negmax[:, g % 2, 0:1], 0.0)
                    else:
                        negate_max(m, g, i - 1)
                    dve.tensor_tensor_reduce(out=probs[:, g % 2, i], in0=score_bank[h % 2][0:T, 0:TC], in1=unmask[:, m[1]],
                                             scale=SCALE, scalar=LOWEST, op0=ALU.add, op1=ALU.max,
                                             accum_out=maxes[:, g % 2, i:i + 1]).then_inc(s_masked, 1)
                negate_max(m, g, HG - 1)

            def negate_max(m, g, i):
                dve.wait_ge(s_masked, count(m, HEADS, g * HG + i + 1))
                dve.tensor_scalar(negmax[:, g % 2, i:i + 1], maxes[:, g % 2, i:i + 1], -1.0, None, ALU.mult).then_inc(s_negmax, 1)

            def normalise_probs(m, g):
                for i in range(HG):
                    h = g * HG + i
                    dve.wait_ge(s_exp, count(m, HEADS, h + 1))
                    dve.reciprocal(inv[:, g % 2, i:i + 1], sums[:, g % 2, i:i + 1]).then_inc(s_inv, 1)
                    dve.wait_ge(s_inv, count(m, HEADS, h + 1))
                    last = dve.tensor_scalar(probs[:, g % 2, i], probs[:, g % 2, i], inv[:, g % 2, i:i + 1], None, ALU.mult)
                last.then_inc(s_probs, 1)

            def residual(m):
                if at_least(m, 2):
                    dve.wait_ge(s_x1st[m[1]], 16 * m[0])
                dve.wait_ge(s_xtok[m[1]], 16 * (m[0] + 1))
                dve.wait_ge(s_wo, count(m, 1, 1))
                if is_batch(m, 0):
                    dve.wait_ge(s_gate, 1)
                dve.scalar_tensor_tensor(out=x1[:, m[1]], in0=av_bank[0:T, :], scalar=tanh_gate[:, 0:1], in1=x_tok[:, m[1]],
                                         op0=ALU.mult, op1=ALU.add).then_inc(s_x1, 1)

            def step(n, project, attend, normalise):
                m = later(n, -1)
                for g in range(C):
                    if attend:
                        mask_scores(m, g)
                    if project and g == 1:
                        pad_queries(n, 0)
                        pad_queries(n, 1)
                    if attend:
                        normalise_probs(m, g)
                    if project and g == 2:
                        pad_queries(n, 2)
                        pad_queries(n, 3)
                    if normalise and g == 2:
                        ln_stats(later(n, 1))
                    if normalise and g == 3:
                        ln_apply(later(n, 1))
                if attend:
                    residual(m)

            ln_stats((0, 0))
            ln_apply((0, 0))
            run(dve, step)

        @block.scalar
        def _(act):
            act.wait_ge(s_w["vec"], 16)

            def copy_aT(b, c):
                act.wait_ge(s_proj, count(b, 11, c + 1))
                act.activation(aT[:, c], proj_bank[(b[1] * 11 + c) % 2][:, 0:TC], ACT.Identity,
                               scale=vec[:, VEC["ln_gamma"], c:c + 1], bias=vec[:, VEC["ln_beta"], c:c + 1]).then_inc(s_projev, 1)

            def copy_key(b, c):
                u = C + c
                act.wait_ge(s_proj, count(b, 11, u + 1))
                act.copy(keyT[:, b[1], c], proj_bank[(b[1] * 11 + u) % 2][:, 0:TC]).then_inc(s_projev, 1)

            def copy_value(b, k):
                u = 2 * C + k
                act.wait_ge(s_proj, count(b, 11, u + 1))
                act.copy(value[:, b[1], k], proj_bank[(b[1] * 11 + u) % 2][0:TK, :]).then_inc(s_projev, 1)

            def exps(m, g, heads):
                for i in heads:
                    act.wait_ge(s_negmax, count(m, HEADS, g * HG + i + 1))
                    act.activation(probs[:, g % 2, i], probs[:, g % 2, i], ACT.Exp, bias=negmax[:, g % 2, i:i + 1],
                                   accum_out=sums[:, g % 2, i:i + 1]).then_inc(s_exp, 1)

            def copy_probsT(m, g, tiles):
                for k in tiles:
                    u = g * KT + k
                    act.wait_ge(s_pt, count(m, C * KT, u + 1))
                    if k == 0 and (g >= 2 or at_least(m, 1)):
                        act.wait_ge(s_av, count(m, C, g - 1))
                    act.copy(probsT[:, g % 2, k], pt_bank[u % 2][0:TK, 0:HG * T]).then_inc(s_ptev, 1)

            def copy_attn(m, g):
                act.wait_ge(s_av, count(m, C, g + 1))
                if g == 0 and at_least(m, 1):
                    act.wait_ge(s_wo, count(later(m, -1), 1, 1))
                act.copy(attnT[:, g], av_bank[:, g * T:(g + 1) * T]).then_inc(s_attn, 1)

            def step(n, project, attend, normalise):
                m = later(n, -1)
                if attend:
                    exps(m, 0, (0, 1))
                if project:
                    copy_aT(n, 0)
                    copy_aT(n, 1)
                if attend:
                    exps(m, 0, (2, 3))
                if project:
                    copy_aT(n, 2)
                    copy_aT(n, 3)
                if attend:
                    copy_probsT(m, 0, (0, 1, 2))
                for g in range(1, C):
                    if attend:
                        exps(m, g, range(HG))
                        copy_attn(m, g - 1)
                    if project:
                        if g < 3:
                            copy_key(n, 2 * g - 2)
                        else:
                            copy_value(n, 0)
                    if attend:
                        copy_probsT(m, g, (0, 1))
                    if project:
                        if g < 3:
                            copy_key(n, 2 * g - 1)
                        else:
                            copy_value(n, 1)
                    if attend:
                        copy_probsT(m, g, (2,))
                    if project and g == 3:
                        copy_value(n, 2)
                if is_batch(n, 0):
                    act.wait_ge(s_w["gate"], 16)
                    act.activation(tanh_gate[:], gate[:], ACT.Tanh).then_inc(s_gate, 1)
                if attend:
                    copy_attn(m, C - 1)

            run(act, step)

        @block.tensor
        def _(pe):
            def proj_free(b, u):
                if u >= 2 or at_least(b, 1):
                    pe.wait_ge(s_projev, count(b, 11, u - 1))
                return proj_bank[(b[1] * 11 + u) % 2]

            def transpose_ctx(b, c):
                dst = proj_free(b, c)
                pe.wait_ge(s_ctxn, count(b, 1, 1))
                for k in range(KT):
                    last = pe.transpose(dst[:, k * TK:(k + 1) * TK], ctx_norm[:, k, c * P:(c + 1) * P], ident[0:TK, 0:TK])
                last.then_inc(s_proj, 1)

            def project_key(b, m):
                dst = proj_free(b, C + m)
                pe.wait_ge(s_projev, count(b, 11, C))
                for c in range(C):
                    last = pe.matmul(dst[:, 0:TC], wk[:, c, m * P:(m + 1) * P], aT[:, c], start=(c == 0), stop=(c == C - 1))
                last.then_inc(s_proj, 1)

            def project_value(b, k):
                dst = proj_free(b, 2 * C + k)
                for c in range(C):
                    last = pe.matmul(dst[0:TK, :], aT[:, c, k * TK:(k + 1) * TK], wv[:, c], start=(c == 0), stop=(c == C - 1))
                last.then_inc(s_proj, 1)

            def project_query(b, m):
                if m == 0:
                    pe.wait_ge(s_xT[b[1]], 16 * (b[0] + 1))
                    if at_least(b, 1):
                        pe.wait_ge(s_qpad, count(b, C, 0))
                for c in range(C):
                    last = pe.matmul(q_bank[:, m * T:(m + 1) * T], wq[:, c, m * P:(m + 1) * P], xT[:, b[1], c], start=(c == 0), stop=(c == C - 1))
                if m == C - 1:
                    last.then_inc(s_q, 1)

            def scores(m, g):
                if g == 0:
                    pe.wait_ge(s_qpad, count(m, C, C))
                    pe.wait_ge(s_projev, count(m, 11, 11))
                for i in range(HG):
                    h = g * HG + i
                    if h >= 2 or at_least(m, 1):
                        pe.wait_ge(s_masked, count(m, HEADS, h - 1))
                    pe.matmul(score_bank[h % 2][0:T, 0:TC], qpad[:, m[1], g, i], keyT[:, m[1], g], start=True,
                              stop=True).then_inc(s_score, 1)

            def transpose_probs(m, g, tiles):
                pe.wait_ge(s_probs, count(m, C, g + 1))
                for k in tiles:
                    u = g * KT + k
                    if u >= 2 or at_least(m, 1):
                        pe.wait_ge(s_ptev, count(m, C * KT, u - 1))
                    for i in range(HG):
                        last = pe.transpose(pt_bank[u % 2][0:TK, i * T:(i + 1) * T], probs[:, g % 2, i, k * TK:(k + 1) * TK],
                                            ident[0:T, 0:T])
                    last.then_inc(s_pt, 1)

            def weigh_values(m, g):
                pe.wait_ge(s_ptev, count(m, C * KT, (g + 1) * KT))
                if g > 0:
                    pe.wait_ge(s_attn, count(m, C, g))
                elif at_least(m, 1):
                    pe.wait_ge(s_x1, count(later(m, -1), 1, 1))
                for i in range(HG):
                    h = g * HG + i
                    for k in range(KT):
                        last = pe.matmul(av_bank[i * HD:(i + 1) * HD, g * T:(g + 1) * T], value[:, m[1], k, h * HD:(h + 1) * HD],
                                         probsT[:, g % 2, k, i * T:(i + 1) * T], start=(k == 0), stop=(k == KT - 1))
                last.then_inc(s_av, 1)

            def project_out(m):
                pe.wait_ge(s_attn, count(m, C, C))
                for c in range(C):
                    last = pe.matmul(av_bank[0:T, :], attnT[:, c], wo[:, c], start=(c == 0), stop=(c == C - 1))
                last.then_inc(s_wo, 1)

            def step(n, project, attend, normalise):
                m = later(n, -1)
                if attend:
                    scores(m, 0)
                if project:
                    transpose_ctx(n, 0)
                    transpose_ctx(n, 1)
                    if is_batch(n, 0):
                        pe.wait_ge(s_w["wq"], 16)
                    for c in range(C):
                        project_query(n, c)
                    transpose_ctx(n, 2)
                    transpose_ctx(n, 3)
                if attend:
                    transpose_probs(m, 0, (0, 1, 2))
                for g in range(1, C):
                    if attend:
                        scores(m, g)
                        if is_batch(m, 0) and g == 1:
                            pe.wait_ge(s_w["wo"], 16)
                        weigh_values(m, g - 1)
                    if project:
                        if is_batch(n, 0) and g == 1:
                            pe.wait_ge(s_w["wk"], 16)
                        if is_batch(n, 0) and g == 3:
                            pe.wait_ge(s_w["wv"], 16)
                        if g < 3:
                            project_key(n, 2 * g - 2)
                        else:
                            project_value(n, 0)
                    if attend:
                        transpose_probs(m, g, (0, 1))
                    if project:
                        if g < 3:
                            project_key(n, 2 * g - 1)
                        else:
                            project_value(n, 1)
                    if attend:
                        transpose_probs(m, g, (2,))
                    if project and g == 3:
                        project_value(n, 2)
                if attend:
                    weigh_values(m, C - 1)
                    project_out(m)

            pe.wait_ge(s_w["ident"], 16)
            run(pe, step)


def rwkv_block(nc, A, ident, vec, W, w_loaded):
    with ExitStack() as ctx:
        def sb(name, shape, dt=F32):
            return ctx.enter_context(nc.sbuf_tensor(name, shape, dt))

        def sem(name):
            return ctx.enter_context(nc.semaphore(name))

        def sem2(name):
            return [sem(f"{name}_{q}") for q in range(2)]

        bank = [ctx.enter_context(nc.psum_tensor(f"b_bank{n}", [P, BANK], F32)) for n in range(8)]
        vrep_bank, out_bank, pre_bank, post_bank = bank[0:2], bank[2], bank[3:6], bank[6:8]

        CT = C * T
        half_gn = sb("half_gn", [P, 2, C])
        maa1 = sb("maa1_sb", [P, C, MAA * MD])
        maa2 = sb("maa2_sb", [P, MAA, D])
        td1 = sb("td1_sb", [P, C, TD])
        td2 = sb("td2_sb", [P, D])
        headmean = sb("headmean", [P, P])
        bonus_w = sb("bonus_w", [P, C, P])
        collect = sb("collect_sb", [P, S, P // QUAD])
        spread = sb("spread_r", [P, S, P], F32R)
        s0 = sb("s0_sb", [P, B, C, S])
        rows = sb("rows_sb", [P, B, 2, C])
        neg_half = sb("neg_half", [T, 1])
        ln_eps = sb("b_eps", [P, 1])

        x1 = sb("b_x1", [T, 2, D])
        ln_tok = sb("ln1_tok", [T, D])
        bn6, mv, ve, rs = sb("ln1_bn", [T, 6]), sb("ln1_mv", [T, 2]), sb("ln1_ve", [T, 1]), sb("ln1_rs", [T, 1])
        xa = sb("xa", [P, C, T + 1])
        sx = sb("sx", [P, C, T])
        xin = sb("xin", [P, C, T])
        th = sb("th", [P, 2, T])
        mixed = sb("mixed", [P, 2, C, T])
        xm = sb("xm", [P, 2, C, T])
        ttd = sb("ttd", [P, T])
        etd = sb("etd", [P, C, T])
        wdec = sb("wdec", [P, 2, C, T])
        v = sb("v_sb", [P, 2, C, T])
        vhi = sb("v_hi", [P, 2, C, T], F32R)
        vlo = sb("v_lo", [P, 2, C, T], F32R)
        key = sb("key", [P, 2, C, T])
        rec = sb("rec", [P, 2, C, T])
        tg = sb("tg", [P, C, T])
        gate2 = sb("gate2", [P, 2, C, T])
        rk = sb("rk", [P, C, T])
        bv = sb("bv", [P, C, T])
        kv = sb("kv", [P, NRING, BANK])
        st = sb("st", [P, NRING, CT])
        rst = sb("rst", [P, NPROD, CT])
        same_head = rst[:, 0, 0:P]
        wkv = sb("wkv", [P, C, T])
        cen = sb("cen", [P, C, T])
        sq = sb("sq", [P, C, T])
        gated = sb("gated", [P, C, T])
        x1p = sb("x1_post", [T, 2, D])
        x2 = sb("x2", [T, D])
        ln2_tok = sb("ln2_tok", [T, D])
        bn6p, mvp, vep, rsp = sb("ln2_bn", [T, 6]), sb("ln2_mv", [T, 2]), sb("ln2_ve", [T, 1]), sb("ln2_rs", [T, 1])
        xc = sb("xc", [P, C, T + 1])
        sx2 = sb("sx2", [P, C, T])
        xk2 = sb("xk2", [P, C, T])
        xr2 = sb("xr2", [P, C, T])
        kk = sb("kk", [P, C, T])
        trr = sb("trr", [T, D])
        fin = sb("fin", [T, 2, D])

        small = ("maa1", "td1", "key_value", "value_value", "collect", "s0", "rows", "maa2", "td2", "spread")
        s_c = {n: sem(f"b_{n}_loaded") for n in small}
        s_x1, s_x1p, s_store = sem2("b_x1_loaded"), sem2("x1_post_loaded"), sem2("out_stored")
        s_zero, s_setup, s_spread = sem("zeros_set"), sem("setup_done"), sem("spread_rounded")
        s_bn, s_mv, s_ve, s_rs, s_ln = (sem(f"ln1_{n}") for n in ("stats", "meanvar", "vareps", "rstd", "normalised"))
        s_bnp, s_mvp, s_vep, s_rsp, s_lnp = (sem(f"ln2_{n}") for n in ("stats", "meanvar", "vareps", "rstd", "normalised"))
        s_t1, s_xa0, s_xa, s_sx, s_xin = sem("x_transposed"), sem("xa_state"), sem("xa_ready"), sem("sx_ready"), sem("xin_ready")
        s_w1, s_th, s_mixmm, s_mixed, s_xm = (sem(n) for n in ("maa1_done", "th_ready", "maa2_done", "mixed_ready", "xm_ready"))
        s_td1, s_ttd, s_td2, s_etd, s_wdec = (sem(n) for n in ("td1_done", "ttd_ready", "td2_done", "etd_ready", "decay_ready"))
        s_vmm, s_v, s_vlo = sem("v_done"), sem("v_ready"), sem("v_lo_ready")
        s_kmm, s_k, s_rmm, s_r = sem("k_done"), sem("k_ready"), sem("r_done"), sem("r_ready")
        s_gmm, s_tg, s_g = sem("g_done"), sem("tg_ready"), sem("gate_ready2")
        s_rk, s_bonus, s_bv = sem("rk_ready"), sem("bonus_done"), sem("bv_ready")
        s_vrep, s_kv0, s_kv, s_st = sem("vrep_done"), sem("kv_state_ready"), sem("kv_ready"), sem("states_ready")
        s_even, s_odd, s_red = sem("even_products"), sem("odd_products"), sem("reduced")
        s_wkv1, s_wkv = sem("wkv_state_part"), sem("wkv_ready")
        s_mean, s_cen, s_sq, s_var, s_ln2, s_grs = (sem(n) for n in ("gn_mean", "gn_centred", "gn_squared", "gn_var", "gn_log", "gn_rstd"))
        s_gnorm, s_gaff, s_gated = sem("gn_normalised"), sem("gn_scaled"), sem("gated_ready")
        s_wo, s_x2, s_t2, s_xc0, s_xc = sem("b_wo_done"), sem("x2_ready"), sem("x2_transposed"), sem("xc_state"), sem("xc_ready")
        s_sx2, s_xk2, s_xr2 = sem("sx2_ready"), sem("xk2_ready"), sem("xr2_ready")
        s_fk, s_relu, s_kk, s_fr, s_rr = (sem(n) for n in ("wfk_done", "relu_ready", "kk_ready", "wfr_done", "rr_ready"))
        s_fv, s_ff, s_fin = sem("wfv_done"), sem("ffn_scaled"), sem("out_ready")

        N_ITER = B + 2
        LOOP = (2, B // 2 - 1)

        def run(engine, step):
            for i in range(2 * LOOP[0]):
                step((i // 2, i % 2), True, i >= 1, i >= 2, i == 0)
            with engine.Fori(*LOOP) as k:
                for q in range(2):
                    step((k, q), True, True, True, False)
            for i in range(2 * LOOP[1], N_ITER):
                step((i // 2, i % 2), i < B, i <= B, True, False)

        block = ctx.enter_context(nc.Block())

        @block.sync
        def _(sp):
            def load_x1(b):
                if at_least(b, 2):
                    sp.wait_ge(s_ln, count(later(b, -2), 1, 1))
                sp.dma_start(x1[:, b[1]], A["x1"][index(b)]).then_inc(s_x1[b[1]], 16)

            load_x1((0, 0))
            sp.dma_start(rows[:], A["rows"]).then_inc(s_c["rows"], 16)
            sp.dma_start(maa1[:], A["maa1"]).then_inc(s_c["maa1"], 16)
            sp.dma_start(td1[:], A["td1"]).then_inc(s_c["td1"], 16)
            sp.wait_ge(s_zero, 2)
            for f in range(MAA):
                r = f % HG * MD
                sp.dma_start(maa2[r:r + MD, f], A["maa2"][f]).then_inc(s_c["maa2"], 16)
            sp.dma_start(td2[0:TD, :], A["td2"]).then_inc(s_c["td2"], 16)
            load_x1((0, 1))
            sp.dma_start(kv[:].rearrange("p a b -> p (a b)"), A["spread"]).then_inc(s_c["spread"], 16)
            sp.dma_start(same_head, A["key_value"]).then_inc(s_c["key_value"], 16)
            sp.dma_start(headmean[:], A["value_value"]).then_inc(s_c["value_value"], 16)
            sp.dma_start(s0[:], A["s0"]).then_inc(s_c["s0"], 16)
            sp.dma_start(collect[:], A["collect"]).then_inc(s_c["collect"], 16)

            def step(n, pre, scan, post, first):
                if post:
                    l = later(n, -2)
                    if at_least(l, 2):
                        sp.wait_ge(s_x2, count(later(l, -2), 1, 1))
                    sp.dma_start(x1p[:, l[1]], A["x1"][index(l)]).then_inc(s_x1p[l[1]], 16)
                if pre and not first and not is_batch(n, B - 1):
                    load_x1(later(n, 1))
                if post:
                    sp.wait_ge(s_fin, count(l, 1, 1))
                    sp.dma_start(A["out"][index(l)], fin[:, l[1]]).then_inc(s_store[l[1]], 16)

            run(sp, step)
            for q in range(2):
                sp.wait_ge(s_store[q], 16 * (B // 2))

        @block.gpsimd
        def _(pool):
            pool.memset(maa2[:], 0.0).then_inc(s_zero, 1)
            pool.memset(td2[:], 0.0).then_inc(s_zero, 1)
            pool.memset(neg_half[:], -0.5)
            pool.memset(wdec[:], 0.0)
            pool.memset(th[:], 0.0)
            pool.memset(ttd[:], 0.0)
            pool.memset(ln_eps[:], EPS).then_inc(s_zero, 1)
            pool.wait_ge(s_zero, 3)
            pool.wait_ge(s_c["rows"], 16)

            def rstd1(b):
                pool.wait_ge(s_ve, count(b, 1, 1))
                pool.tensor_tensor(rs[:], ve[:], neg_half[:], ALU.pow).then_inc(s_rs, 1)

            def xa_state(b):
                if at_least(b, 1):
                    pool.wait_ge(s_xm, count(later(b, -1), MAA, MAA))
                pool.tensor_copy(xa[:, :, 0:1], rows[:, index(b), 1, :].unsqueeze(2)).then_inc(s_xa0, 1)

            def mix(b, f):
                pool.wait_ge(s_mixed, count(b, MAA, f + 1))
                if f == 2:
                    pool.wait_ge(s_td1, count(b, 1, 1))
                if f == 3:
                    pool.wait_ge(s_vmm, count(b, 1, 1))
                if f == 4:
                    pool.wait_ge(s_kmm, count(b, 1, 1))
                if f == 0 and at_least(b, 1):
                    pool.wait_ge(s_gmm, count(later(b, -1), 1, 1))
                pool.tensor_tensor(xm[:, f % 2], mixed[:, f % 2], xa[:, :, 1:T + 1], ALU.add).then_inc(s_xm, 1)

            def kv_state(m, j):
                if j >= NRING:
                    pool.wait_ge(s_st, count(m, S, j - NRING + 1))
                elif at_least(m, 1):
                    pool.wait_ge(s_st, count(later(m, -1), S, S + j - NRING + 1))
                pool.tensor_copy(kv[:, j % NRING, 0:CT].rearrange("p (c t) -> p c t", c=C)[:, :, 0:1],
                                 s0[:, index(m), :, j:j + 1]).then_inc(s_kv0, 1)

            def product(m, j):
                pool.wait_ge(s_st, count(m, S, j + 1))
                if j >= NPROD or at_least(m, 1):
                    pool.wait_ge(s_red, count(m, QUAD, (j - NPROD) // QUAD + 1))
                pool.tensor_tensor(rst[:, j % NPROD], st[:, j % NRING], rec[:, m[1]].rearrange("p c t -> p (c t)"),
                                   ALU.mult).then_inc(s_even, 1)

            def step(n, pre, scan, post, first):
                m, l = later(n, -1), later(n, -2)
                if first:
                    rstd1(n)
                    xa_state(n)
                if is_batch(m, 0):
                    pool.wait_ge(s_c["s0"], 16)
                    pool.wait_ge(s_spread, 1)
                if scan:
                    pool.wait_ge(s_r, count(m, 1, 1))
                    if at_least(m, 1):
                        pool.wait_ge(s_bonus, count(later(m, -1), 1, 1))
                    pool.tensor_tensor(rk[:], rec[:, m[1]], key[:, m[1]], ALU.mult).then_inc(s_rk, 1)
                for s in range(S):
                    if scan:
                        for j in ([0, 1] if s == 0 else [s + 1] if s + 1 < S else []):
                            kv_state(m, j)
                        if s >= 1 and (s - 1) % 2 == 0:
                            product(m, s - 1)
                    if pre and s in MIX_SLOT:
                        mix(n, MIX_SLOT.index(s))
                    if post and s == 7:
                        pool.wait_ge(s_gaff, count(l, 1, 1))
                        pool.wait_ge(s_g, count(l, 1, 1))
                        if at_least(l, 1):
                            pool.wait_ge(s_wo, count(later(l, -1), 1, 1))
                        pool.tensor_tensor(gated[:], sq[:], gate2[:, l[1]], ALU.mult).then_inc(s_gated, 1)
                    if post and s == 9:
                        pool.wait_ge(s_vep, count(l, 1, 1))
                        pool.tensor_tensor(rsp[:], vep[:], neg_half[:], ALU.pow).then_inc(s_rsp, 1)
                        if at_least(l, 1):
                            pool.wait_ge(s_xr2, count(later(l, -1), 1, 1))
                        pool.tensor_copy(xc[:, :, 0:1], rows[:, index(l), 0, :].unsqueeze(2)).then_inc(s_xc0, 1)
                    if pre and s == 13 and not is_batch(n, B - 1):
                        rstd1(later(n, 1))
                        xa_state(later(n, 1))

            run(pool, step)

        @block.vector
        def _(dve):
            def setup():
                dve.tensor_scalar(half_gn[:, 0], vec[:, VEC["gn_w"]], 0.5, None, ALU.mult)
                dve.tensor_scalar(half_gn[:, 1], vec[:, VEC["gn_b"]], 0.5, None, ALU.mult)
                dve.wait_ge(s_c["key_value"], 16)
                dve.wait_ge(s_c["value_value"], 16)
                dve.tensor_scalar(headmean[:], headmean[:], 1.0 / S, None, ALU.mult)
                for c in range(C):
                    last = dve.tensor_scalar(bonus_w[:, c], same_head, vec[:, VEC["u"], c:c + 1], None, ALU.mult)
                last.then_inc(s_setup, 1)

            def ln_stats(b, src, loaded, bn6, mv, ve, s_bn, s_mv, s_ve):
                dve.wait_ge(*loaded)
                dve.bn_stats(bn6[:], src).then_inc(s_bn, 1)
                dve.wait_ge(s_bn, count(b, 1, 1))
                dve.memset(ve[:], 0.0)
                dve.bn_aggr(mv[:], bn6[:]).then_inc(s_mv, 1)
                dve.wait_ge(s_mv, count(b, 1, 1))
                dve.tensor_scalar(ve[:], mv[:, 1:2], EPS, None, ALU.add).then_inc(s_ve, 1)

            def stats1(b):
                ln_stats(b, x1[:, b[1]], (s_x1[b[1]], 16 * (b[0] + 1)), bn6, mv, ve, s_bn, s_mv, s_ve)

            def apply1(b):
                dve.wait_ge(s_rs, count(b, 1, 1))
                if at_least(b, 1):
                    dve.wait_ge(s_t1, count(later(b, -1), 1, 1))
                dve.tensor_scalar(ln_tok[:], x1[:, b[1]], mv[:, 0:1], rs[:, 0:1], ALU.subtract, ALU.mult).then_inc(s_ln, 1)

            def token_shift(b):
                dve.wait_ge(s_xa, count(b, 1, 1))
                dve.wait_ge(s_xa0, count(b, 1, 1))
                if at_least(b, 1):
                    dve.wait_ge(s_w1, count(later(b, -1), 1, 1))
                dve.tensor_tensor(sx[:], xa[:, :, 0:T], xa[:, :, 1:T + 1], ALU.subtract).then_inc(s_sx, 1)
                dve.wait_ge(s_sx, count(b, 1, 1))
                for c in range(C):
                    last = dve.scalar_tensor_tensor(out=xin[:, c], in0=sx[:, c], scalar=vec[:, VEC["maa_x"], c:c + 1],
                                                    in1=xa[:, c, 1:T + 1], op0=ALU.mult, op1=ALU.add)
                last.then_inc(s_xin, 1)

            def mix(b, f):
                dve.wait_ge(s_mixmm, count(b, MAA, f + 1))
                if f >= 2 or at_least(b, 1):
                    dve.wait_ge(s_xm, count(b, MAA, max(f - 1, 0)))
                src = pre_bank[MIX_BANK[f]]
                for c in range(C):
                    last = dve.scalar_tensor_tensor(out=mixed[:, f % 2, c], in0=src[:, c * T:(c + 1) * T],
                                                    scalar=vec[:, VEC[MIXES[f]], c:c + 1], in1=sx[:, c],
                                                    op0=ALU.add, op1=ALU.mult)
                last.then_inc(s_mixed, 1)

            def value_low(b):
                dve.wait_ge(s_v, count(b, 1, 1))
                if at_least(b, 2):
                    dve.wait_ge(s_vrep, count(later(b, -2), S, S))
                dve.tensor_tensor(vlo[:, b[1]], v[:, b[1]], vhi[:, b[1]].bitcast(F32), ALU.subtract).then_inc(s_vlo, 1)

            def gate(b):
                dve.wait_ge(s_tg, count(b, 1, 1))
                if at_least(b, 2):
                    dve.wait_ge(s_gated, count(later(b, -2), 1, 1))
                dve.scalar_tensor_tensor(out=gate2[:, b[1]].rearrange("p c t -> p (c t)"), in0=tg[:].rearrange("p c t -> p (c t)"),
                                         scalar=1.0, in1=pre_bank[USE_BANK["g"]][:, 0:CT], op0=ALU.add, op1=ALU.mult).then_inc(s_g, 1)

            def key_value(m, j):
                dve.wait_ge(s_vrep, count(m, S, j + 1))
                if j == 0:
                    dve.wait_ge(s_k, count(m, 1, 1))
                if j >= NRING or at_least(m, 1):
                    dve.wait_ge(s_st, count(m, S, j - NRING + 1))
                src = vrep_bank[j % 2][:, 0:CT].rearrange("p (c t) -> p c t", c=C)
                dst = kv[:, j % NRING, 0:CT].rearrange("p (c t) -> p c t", c=C)
                dve.tensor_tensor(dst[:, :, 1:T], src[:, :, 0:T - 1], key[:, m[1], :, 0:T - 1], ALU.mult).then_inc(s_kv, 1)

            def scan(m, j):
                if j == 0:
                    dve.wait_ge(s_wdec, count(m, 1, 1))
                dve.wait_ge(s_kv, count(m, S, j + 1))
                dve.wait_ge(s_kv0, count(m, S, j + 1))
                if j >= NRING or at_least(m, 1):
                    if j % 2 == 0:
                        dve.wait_ge(s_even, count(m, S // 2, (j - NRING) // 2 + 1))
                    else:
                        dve.wait_ge(s_odd, count(m, S // 2, (j - NRING) // 2 + 1))
                dve.tensor_tensor_scan(st[:, j % NRING], wdec[:, m[1]].rearrange("p c t -> p (c t)"), kv[:, j % NRING, 0:CT], 0.0,
                                       ALU.mult, ALU.add).then_inc(s_st, 1)

            def product(m, j):
                dve.wait_ge(s_st, count(m, S, j + 1))
                if j >= NPROD or at_least(m, 1):
                    dve.wait_ge(s_red, count(m, QUAD, (j - NPROD) // QUAD + 1))
                dve.tensor_tensor(rst[:, j % NPROD], st[:, j % NRING], rec[:, m[1]].rearrange("p c t -> p (c t)"),
                                  ALU.mult).then_inc(s_odd, 1)

            def bonus_value(m):
                dve.wait_ge(s_bonus, count(m, 1, 1))
                if at_least(m, 1):
                    dve.wait_ge(s_wkv, count(later(m, -1), 1, 1))
                dve.tensor_tensor(bv[:].rearrange("p c t -> p (c t)"), post_bank[1][:, 0:CT],
                                  v[:, m[1]].rearrange("p c t -> p (c t)"), ALU.mult).then_inc(s_bv, 1)

            def wkv_sum(m):
                dve.wait_ge(s_red, count(m, QUAD, QUAD))
                dve.wait_ge(s_bv, count(m, 1, 1))
                if at_least(m, 1):
                    dve.wait_ge(s_cen, count(later(m, -1), 1, 1))
                dve.tensor_tensor(wkv[:].rearrange("p c t -> p (c t)"), out_bank[:, 0:CT], bv[:].rearrange("p c t -> p (c t)"),
                                  ALU.add).then_inc(s_wkv, 1)

            def centre(l):
                dve.wait_ge(s_mean, count(l, 1, 1))
                if at_least(l, 1):
                    dve.wait_ge(s_gaff, count(later(l, -1), 1, 1))
                dve.tensor_tensor(cen[:].rearrange("p c t -> p (c t)"), wkv[:].rearrange("p c t -> p (c t)"),
                                  post_bank[0][:, 0:CT], ALU.subtract).then_inc(s_cen, 1)

            def group_norm(l):
                dve.wait_ge(s_grs, count(l, 1, 1))
                dve.tensor_tensor(cen[:], cen[:], sq[:], ALU.mult).then_inc(s_gnorm, 1)

            def residual(l):
                dve.wait_ge(s_wo, count(l, 1, 1))
                dve.wait_ge(s_x1p[l[1]], 16 * (l[0] + 1))
                dve.tensor_tensor(x2[:], post_bank[0][0:T, :], x1p[:, l[1]], ALU.add).then_inc(s_x2, 1)
                ln_stats(l, x2[:], (s_x2, count(l, 1, 1)), bn6p, mvp, vep, s_bnp, s_mvp, s_vep)

            def apply2(l):
                dve.wait_ge(s_rsp, count(l, 1, 1))
                dve.tensor_scalar(ln2_tok[:], x2[:], mvp[:, 0:1], rsp[:, 0:1], ALU.subtract, ALU.mult).then_inc(s_lnp, 1)

            def shift2(l):
                dve.wait_ge(s_xc, count(l, 1, 1))
                dve.wait_ge(s_xc0, count(l, 1, 1))
                dve.tensor_tensor(sx2[:], xc[:, :, 0:T], xc[:, :, 1:T + 1], ALU.subtract).then_inc(s_sx2, 1)
                dve.wait_ge(s_sx2, count(l, 1, 1))
                for dst, name, ready in ((xk2, "ffn_k", s_xk2), (xr2, "ffn_r", s_xr2)):
                    for c in range(C):
                        last = dve.scalar_tensor_tensor(out=dst[:, c], in0=sx2[:, c], scalar=vec[:, VEC[name], c:c + 1],
                                                        in1=xc[:, c, 1:T + 1], op0=ALU.mult, op1=ALU.add)
                    last.then_inc(ready, 1)

            def finish(l):
                dve.wait_ge(s_fv, count(l, 1, 1))
                dve.wait_ge(s_rr, count(l, 1, 1))
                if at_least(l, 2):
                    dve.wait_ge(s_store[l[1]], 16 * l[0])
                dve.scalar_tensor_tensor(out=fin[:, l[1]], in0=trr[:], scalar=1.0, in1=post_bank[0][0:T, :], op0=ALU.add,
                                         op1=ALU.mult).then_inc(s_ff, 1)
                dve.wait_ge(s_ff, count(l, 1, 1))
                dve.scalar_tensor_tensor(out=fin[:, l[1]], in0=fin[:, l[1]], scalar=0.5, in1=x2[:], op0=ALU.mult,
                                         op1=ALU.add).then_inc(s_fin, 1)

            def step(n, pre, scans, post, first):
                m, l = later(n, -1), later(n, -2)
                if first:
                    stats1(n)
                    apply1(n)
                    token_shift(n)
                    setup()
                if is_batch(m, 0):
                    dve.wait_ge(s_zero, 3)
                    dve.wait_ge(s_spread, 1)
                for s in range(S):
                    if scans:
                        key_value(m, s)
                        if s >= 1 and (s - 1) % 2 == 1:
                            product(m, s - 1)
                        scan(m, s)
                    if scans and s == 1:
                        bonus_value(m)
                    if post and s == 1:
                        centre(l)
                    if pre and s in MIX_SLOT:
                        mix(n, MIX_SLOT.index(s))
                    if post and s == 5:
                        group_norm(l)
                    if pre and s == 9:
                        value_low(n)
                    if post and s == 9:
                        residual(l)
                    if post and s == 10:
                        apply2(l)
                    if post and s == 12:
                        shift2(l)
                    if pre and s == 14:
                        gate(n)
                    if pre and not is_batch(n, B - 1):
                        if s == 12:
                            stats1(later(n, 1))
                        if s == 14:
                            apply1(later(n, 1))
                        if s == 15:
                            token_shift(later(n, 1))
                if scans:
                    product(m, S - 1)
                if post:
                    finish(l)
                if scans:
                    wkv_sum(m)

            run(dve, step)

        @block.scalar
        def _(act):
            act.wait_ge(s_zero, 3)

            def affine(dst, src, scale, bias):
                for c in range(C):
                    last = act.activation(dst(c), src(c), ACT.Identity, scale=scale[:, c:c + 1], bias=bias[:, c:c + 1])
                return last

            def xa_affine(b):
                act.wait_ge(s_t1, count(b, 1, 1))
                if at_least(b, 1):
                    act.wait_ge(s_xm, count(later(b, -1), MAA, MAA))
                affine(lambda c: xa[:, c, 1:T + 1], lambda c: pre_bank[0][:, c * T:(c + 1) * T], vec[:, VEC["ln1_w"]],
                       vec[:, VEC["ln1_b"]]).then_inc(s_xa, 1)

            def tanh_maa(b):
                act.wait_ge(s_w1, count(b, 1, 1))
                if at_least(b, 1):
                    act.wait_ge(s_mixmm, count(later(b, -1), MAA, MAA))
                act.activation(th[:, 0], pre_bank[1][:, 0:T], ACT.Tanh)
                act.activation(th[0:MD, 1], pre_bank[1][0:MD, T:2 * T], ACT.Tanh).then_inc(s_th, 1)

            def tanh_td(b):
                act.wait_ge(s_td1, count(b, 1, 1))
                if at_least(b, 1):
                    act.wait_ge(s_td2, count(later(b, -1), 1, 1))
                act.activation(ttd[0:TD], pre_bank[1][0:TD, 0:T], ACT.Tanh).then_inc(s_ttd, 1)

            def decay(b):
                act.wait_ge(s_td2, count(b, 1, 1))
                if at_least(b, 1):
                    act.wait_ge(s_wdec, count(later(b, -1), 1, 1))
                for c in range(C):
                    last = act.activation(etd[:, c], pre_bank[1][:, c * T:(c + 1) * T], ACT.Exp,
                                          bias=vec[:, VEC["time_decay"], c:c + 1])
                last.then_inc(s_etd, 1)
                act.wait_ge(s_etd, count(b, 1, 1))
                if at_least(b, 2):
                    act.wait_ge(s_st, count(later(b, -2), S, S))
                act.activation(wdec[:, b[1], :, 1:T], etd[:, :, 0:T - 1], ACT.Exp, scale=-1.0).then_inc(s_wdec, 1)

            def copy_value(b):
                act.wait_ge(s_vmm, count(b, 1, 1))
                if at_least(b, 2):
                    act.wait_ge(s_bv, count(later(b, -2), 1, 1))
                    act.wait_ge(s_vlo, count(later(b, -2), 1, 1))
                    act.wait_ge(s_vrep, count(later(b, -2), S, S))
                src = pre_bank[USE_BANK["v"]][:, 0:CT]
                act.copy(vhi[:, b[1]].rearrange("p c t -> p (c t)"), src)
                act.copy(v[:, b[1]].rearrange("p c t -> p (c t)"), src).then_inc(s_v, 1)

            def copy_key(b):
                act.wait_ge(s_kmm, count(b, 1, 1))
                if at_least(b, 2):
                    act.wait_ge(s_kv, count(later(b, -2), S, S))
                    act.wait_ge(s_rk, count(later(b, -2), 1, 1))
                act.copy(key[:, b[1]].rearrange("p c t -> p (c t)"), pre_bank[USE_BANK["k"]][:, 0:CT]).then_inc(s_k, 1)

            def copy_rec(b):
                act.wait_ge(s_rmm, count(b, 1, 1))
                if at_least(b, 2):
                    act.wait_ge(s_even, count(later(b, -2), S // 2, S // 2))
                    act.wait_ge(s_odd, count(later(b, -2), S // 2, S // 2))
                act.copy(rec[:, b[1]].rearrange("p c t -> p (c t)"), pre_bank[USE_BANK["r"]][:, 0:CT]).then_inc(s_r, 1)

            def tanh_gate(b):
                act.wait_ge(s_gmm, count(b, 1, 1))
                if at_least(b, 1):
                    act.wait_ge(s_g, count(later(b, -1), 1, 1))
                act.activation(tg[:].rearrange("p c t -> p (c t)"), pre_bank[USE_BANK["g"]][:, 0:CT], ACT.Tanh,
                               scale=0.5).then_inc(s_tg, 1)

            def square(l):
                act.wait_ge(s_cen, count(l, 1, 1))
                if at_least(l, 1):
                    act.wait_ge(s_gated, count(later(l, -1), 1, 1))
                act.activation(sq[:], cen[:], ACT.Square).then_inc(s_sq, 1)

            def gn_rstd(l):
                act.wait_ge(s_var, count(l, 1, 1))
                flat = sq[:].rearrange("p c t -> p (c t)")
                act.activation(flat, post_bank[1][:, 0:CT], ACT.Ln, bias=ln_eps[:, 0:1]).then_inc(s_ln2, 1)
                act.wait_ge(s_ln2, count(l, 1, 1))
                act.activation(flat, flat, ACT.Exp, scale=-0.5).then_inc(s_grs, 1)

            def gn_affine(l):
                act.wait_ge(s_gnorm, count(l, 1, 1))
                affine(lambda c: sq[:, c], lambda c: cen[:, c], half_gn[:, 0], half_gn[:, 1]).then_inc(s_gaff, 1)

            def xc_affine(l):
                act.wait_ge(s_t2, count(l, 1, 1))
                if at_least(l, 1):
                    act.wait_ge(s_xr2, count(later(l, -1), 1, 1))
                affine(lambda c: xc[:, c, 1:T + 1], lambda c: post_bank[1][:, c * T:(c + 1) * T], vec[:, VEC["ln2_w"]],
                       vec[:, VEC["ln2_b"]]).then_inc(s_xc, 1)

            def relu_square(l):
                act.wait_ge(s_fk, count(l, 1, 1))
                if at_least(l, 1):
                    act.wait_ge(s_fv, count(later(l, -1), 1, 1))
                flat = kk[:].rearrange("p c t -> p (c t)")
                act.activation(flat, post_bank[0][:, 0:CT], ACT.Relu).then_inc(s_relu, 1)
                act.wait_ge(s_relu, count(l, 1, 1))
                act.activation(flat, flat, ACT.Square).then_inc(s_kk, 1)

            def receptance(l):
                act.wait_ge(s_fr, count(l, 1, 1))
                if at_least(l, 1):
                    act.wait_ge(s_ff, count(later(l, -1), 1, 1))
                act.activation(trr[:], post_bank[1][0:T, :], ACT.Tanh, scale=0.5).then_inc(s_rr, 1)

            def step(n, pre, scans, post, first):
                l = later(n, -2)
                if first:
                    xa_affine(n)
                if is_batch(l, 0):
                    act.wait_ge(s_setup, 1)
                if pre:
                    tanh_maa(n)
                if post:
                    square(l)
                    gn_rstd(l)
                if pre:
                    tanh_td(n)
                if is_batch(n, 0):
                    act.wait_ge(s_c["spread"], 16)
                    act.copy(spread[:].rearrange("p j q -> p (j q)"), kv[:].rearrange("p a b -> p (a b)")).then_inc(s_spread, 1)
                if post:
                    gn_affine(l)
                if pre:
                    decay(n)
                    copy_value(n)
                    copy_key(n)
                if post:
                    xc_affine(l)
                if pre:
                    copy_rec(n)
                    tanh_gate(n)
                if post:
                    relu_square(l)
                    receptance(l)
                if pre and not is_batch(n, B - 1):
                    xa_affine(later(n, 1))

            run(act, step)

        @block.tensor
        def _(pe):
            def wait_constants(b, *names):
                if is_batch(b, 0):
                    for name in names:
                        pe.wait_ge(s_c[name], 16 * MAA if name == "maa2" else 16)

            def transposes(dst, src):
                for c in range(C):
                    last = pe.transpose(dst[:, c * T:(c + 1) * T], src[:, c * P:(c + 1) * P], ident[0:T, 0:T])
                return last

            def channel_major(dst, w, src):
                for o in range(C):
                    for c in range(C):
                        last = pe.matmul(dst[:, o * T:(o + 1) * T], w[:, c, o * P:(o + 1) * P], src[:, c], start=(c == 0),
                                         stop=(c == C - 1))
                return last

            def token_major(dst, w, src):
                for c in range(C):
                    last = pe.matmul(dst[0:T, :], src[:, c], w[:, c], start=(c == 0), stop=(c == C - 1))
                return last

            def transpose_x(b):
                pe.wait_ge(s_ln, count(b, 1, 1))
                if at_least(b, 1):
                    pe.wait_ge(s_mixed, count(later(b, -1), MAA, MAA))
                transposes(pre_bank[0], ln_tok).then_inc(s_t1, 1)

            def maa_first(b):
                wait_constants(b, "maa1")
                pe.wait_ge(s_xin, count(b, 1, 1))
                if at_least(b, 1):
                    pe.wait_ge(s_r, count(later(b, -1), 1, 1))
                for o, (a, z) in enumerate(((0, P), (P, MAA * MD))):
                    for c in range(C):
                        last = pe.matmul(pre_bank[1][0:z - a, o * T:(o + 1) * T], maa1[:, c, a:z], xin[:, c], start=(c == 0),
                                         stop=(c == C - 1))
                last.then_inc(s_w1, 1)

            def maa_second(b, f):
                if f == 0:
                    if is_batch(b, 0):
                        pe.wait_ge(s_zero, 3)
                    wait_constants(b, "maa2")
                    pe.wait_ge(s_th, count(b, 1, 1))
                    if at_least(b, 1):
                        pe.wait_ge(s_g, count(later(b, -1), 1, 1))
                elif f == 1:
                    pe.wait_ge(s_xa, count(b, 1, 1))
                elif f == 2:
                    pe.wait_ge(s_mixed, count(b, MAA, 1))
                elif f == 3:
                    pe.wait_ge(s_etd, count(b, 1, 1))
                else:
                    pe.wait_ge(s_v, count(b, 1, 1))
                dst = pre_bank[MIX_BANK[f]]
                row = MIX_ROW[f]
                for o in range(C):
                    last = pe.matmul(dst[:, o * T:(o + 1) * T], maa2[:, row, o * P:(o + 1) * P], th[:, row // HG], start=True,
                                     stop=True)
                last.then_inc(s_mixmm, 1)

            def decay_first(b):
                wait_constants(b, "td1", "td2")
                pe.wait_ge(s_xm, count(b, MAA, 1))
                pe.wait_ge(s_th, count(b, 1, 1))
                for c in range(C):
                    last = pe.matmul(pre_bank[1][0:TD, 0:T], td1[:, c], xm[:, 0, c], start=(c == 0), stop=(c == C - 1))
                last.then_inc(s_td1, 1)

            def decay_second(b):
                pe.wait_ge(s_ttd, count(b, 1, 1))
                for o in range(C):
                    last = pe.matmul(pre_bank[1][:, o * T:(o + 1) * T], td2[:, o * P:(o + 1) * P], ttd[:], start=True, stop=True)
                last.then_inc(s_td2, 1)

            def project(b, f, w, done):
                pe.wait_ge(s_xm, count(b, MAA, f + 1))
                if f < 4:
                    pe.wait_ge(s_mixed, count(b, MAA, f + 1))
                else:
                    pe.wait_ge(s_k, count(b, 1, 1))
                channel_major(pre_bank[USE_BANK[w[1]]], W[w], xm[:, f % 2]).then_inc(done, 1)

            def bonus(m):
                if is_batch(m, 0):
                    pe.wait_ge(s_setup, 1)
                pe.wait_ge(s_rk, count(m, 1, 1))
                if at_least(m, 2):
                    pe.wait_ge(s_rr, count(later(m, -2), 1, 1))
                for c in range(C):
                    last = pe.matmul(post_bank[1][:, c * T:(c + 1) * T], bonus_w[:, c], rk[:, c], start=True, stop=True)
                last.then_inc(s_bonus, 1)

            def spread_value(m, j):
                if j == 0:
                    if is_batch(m, 0):
                        pe.wait_ge(s_spread, 1)
                    pe.wait_ge(s_vlo, count(m, 1, 1))
                if j >= 2 or at_least(m, 1):
                    pe.wait_ge(s_kv, count(m, S, j - 1))
                for part in (vhi, vlo):
                    last = pe.matmul(vrep_bank[j % 2][:, 0:CT], spread[:, j], part[:, m[1]].rearrange("p c t -> p (c t)"),
                                     start=(part is vhi), stop=(part is vlo))
                last.then_inc(s_vrep, 1)

            def reduce(m, r):
                if r == 0:
                    wait_constants(m, "collect")
                pe.wait_ge(s_even, count(m, S // 2, 2 * r + 2))
                pe.wait_ge(s_odd, count(m, S // 2, 2 * r + 2))
                if r == 0 and at_least(m, 1):
                    pe.wait_ge(s_wkv, count(later(m, -1), 1, 1))
                for q in range(QUAD):
                    j = QUAD * r + q
                    last = pe.matmul(out_bank[q * (P // QUAD):(q + 1) * (P // QUAD), 0:CT], collect[:, j], rst[:, j % NPROD],
                                     start=(r == 0), stop=(r == QUAD - 1))
                last.then_inc(s_red, 1)

            def gn_mean(l):
                pe.wait_ge(s_wkv, count(l, 1, 1))
                if at_least(l, 1):
                    pe.wait_ge(s_ff, count(later(l, -1), 1, 1))
                pe.matmul(post_bank[0][:, 0:CT], headmean[:], wkv[:].rearrange("p c t -> p (c t)"), start=True,
                          stop=True).then_inc(s_mean, 1)

            def gn_var(l, scans):
                pe.wait_ge(s_sq, count(l, 1, 1))
                if scans:
                    pe.wait_ge(s_bv, count(later(l, 1), 1, 1))
                pe.matmul(post_bank[1][:, 0:CT], headmean[:], sq[:].rearrange("p c t -> p (c t)"), start=True,
                          stop=True).then_inc(s_var, 1)

            def step(n, pre, scans, post, first):
                m, l = later(n, -1), later(n, -2)
                if first:
                    transpose_x(n)
                for s in range(S):
                    if scans:
                        spread_value(m, s)
                        if s == 0:
                            bonus(m)
                        if s >= 6 and (s - 6) % QUAD == 0:
                            reduce(m, (s - 6) // QUAD)
                    if post and s == 1:
                        gn_mean(l)
                    if pre and s == 1:
                        maa_first(n)
                    if pre and s in MIX_SLOT:
                        maa_second(n, MIX_SLOT.index(s))
                    if post and s == 4:
                        gn_var(l, scans)
                    if pre and s == 6:
                        decay_first(n)
                    if pre and s == 7:
                        decay_second(n)
                    if pre and s == 7:
                        project(n, 1, "wv", s_vmm)
                    if post and s == 9:
                        pe.wait_ge(s_gated, count(l, 1, 1))
                        token_major(post_bank[0], W["wo"], gated).then_inc(s_wo, 1)
                    if pre and s == 9:
                        project(n, 2, "wk", s_kmm)
                    if post and s == 12:
                        pe.wait_ge(s_lnp, count(l, 1, 1))
                        transposes(post_bank[1], ln2_tok).then_inc(s_t2, 1)
                    if pre and s == 11:
                        project(n, 3, "wr", s_rmm)
                    if pre and s == 13:
                        project(n, 4, "wg", s_gmm)
                    if post and s == 13:
                        pe.wait_ge(s_xk2, count(l, 1, 1))
                        channel_major(post_bank[0], W["wfk"], xk2).then_inc(s_fk, 1)
                    if post and s == 14:
                        pe.wait_ge(s_xr2, count(l, 1, 1))
                        token_major(post_bank[1], W["wfr"], xr2).then_inc(s_fr, 1)
                    if pre and s == 15 and not is_batch(n, B - 1):
                        transpose_x(later(n, 1))
                    if post and s == 15:
                        pe.wait_ge(s_kk, count(l, 1, 1))
                        token_major(post_bank[0], W["wfv"], kk).then_inc(s_fv, 1)
                if scans:
                    reduce(m, QUAD - 1)

            for s in w_loaded.values():
                pe.wait_ge(s, 16)
            run(pe, step)


BLOCK_WEIGHTS = {"wr": "L1_xattn_Wr", "wk": "L1_xattn_Wk", "wv": "L1_xattn_Wv", "wg": "L1_xattn_Wg", "wo": "L1_xattn_Wo",
                 "wfk": "L1_xattn_Wfk", "wfr": "L1_xattn_Wfr", "wfv": "L1_xattn_Wfv"}


def program(nc, A):
    with ExitStack() as ctx:
        W = {n: ctx.enter_context(nc.sbuf_tensor(f"b_{n}", [P, C, D], F32)) for n in BLOCK_WEIGHTS}
        w_loaded = {n: ctx.enter_context(nc.semaphore(f"b_{n}_loaded")) for n in BLOCK_WEIGHTS}
        ident = ctx.enter_context(nc.sbuf_tensor("ident_sb", [P, P], F32))
        vec = ctx.enter_context(nc.sbuf_tensor("vec_sb", [P, len(VECTORS), C], F32))
        cross_attention(nc, A, ident, vec, W, w_loaded)
        rwkv_block(nc, A, ident, vec, W, w_loaded)


def kernel(**inputs):
    import numpy as _np
    import concourse.bacc as _bacc
    from concourse import mybir as _mybir
    from concourse.bass_utils import run_bass_kernel_spmd as _run

    a = {name: _np.asarray(x) for name, x in inputs.items()}

    def channels(x):
        return x.reshape(C, P).T

    def weights(w):
        return w.T.reshape(C, P, -1).transpose(1, 0, 2)

    x, ctx = a["x"], a["ctx_2048"]
    maa = dict(zip(("maa_k", "maa_w", "maa_v", "maa_r", "maa_g"), a["L1_xattn_maa_stack"].reshape(MAA, D)))
    vectors = {"ln_gamma": a["L0_xattn_ln_gamma"], "ln_beta": a["L0_xattn_ln_beta"], "ffn_k": a["L1_xattn_ffn_maa_k"],
               "ffn_r": a["L1_xattn_ffn_maa_r"], "u": a["L1_xattn_u"].reshape(D)} | maa
    p = _np.arange(P)
    key_head = p // S
    value_head, value_j = p % (P // S), QUAD * (p % (P // QUAD) // (P // S)) + p // (P // QUAD)
    value_order = (_np.arange(C)[:, None] * P + S * value_head + value_j).reshape(D)
    j = _np.arange(S)[None, :, None]
    vectors |= {n: a["L1_xattn_" + n][value_order] for n in ("gn_w", "gn_b")}
    block = {n: a[source] for n, source in BLOCK_WEIGHTS.items()}
    block |= {"wv": block["wv"][value_order], "wg": block["wg"][value_order], "wo": block["wo"][:, value_order]}
    arrays = {
        "x": x,
        "xT": x.transpose(0, 2, 1).reshape(B, C, P, T).transpose(0, 2, 1, 3),
        "ctx": ctx,
        "mask": a["mask_BxS2_bf1"].view(_np.uint8),
        "vec": _np.stack([channels(vectors.get(n, a.get("L1_xattn_" + n))) for n in VECTORS], 1),
        "gate": a["L0_xattn_gate"].reshape(1, 1),
        "ident": _np.eye(P, dtype=_np.float32),
        "headmask": (p[:, None] // HD == _np.arange(HG)[None, :]).astype(_np.float32),
        "maa1": a["L1_xattn_maa_w1"].reshape(C, P, MAA * MD).transpose(1, 0, 2),
        "maa2": a["L1_xattn_maa_w2"],
        "td1": a["L1_xattn_td_w1"].reshape(C, P, TD).transpose(1, 0, 2),
        "td2": a["L1_xattn_td_w2"],
        "key_value": (key_head[:, None] == value_head[None, :]).astype(_np.float32),
        "value_value": (value_head[:, None] == value_head[None, :]).astype(_np.float32),
        "collect": _np.stack([((key_head[:, None] == value_head[None, q]) & (value_j[None, q] == n)).astype(_np.float32)
                              for n in range(S) for q in [slice(n % QUAD * (P // QUAD), (n % QUAD + 1) * (P // QUAD))]], 1),
        "spread": ((value_head[:, None, None] == key_head[None, None, :]) & (value_j[:, None, None] == j)
                   ).astype(_np.float32).reshape(P, S * P),
        "s0": ctx[:, 2:2 + S].reshape(B, C, P, S).transpose(2, 0, 1, 3),
        "rows": ctx[:, 0:2].reshape(B, 2, C, P).transpose(3, 0, 1, 2),
    }
    arrays |= {n: weights(a["L0_xattn_W" + n[1:]]) for n in ("wq", "wk", "wv", "wo")}
    arrays |= {"b_" + n: weights(w) for n, w in block.items()}

    nc = _bacc.Bacc("TRN2", target_bir_lowering=False, num_devices=1)
    fed, A = {}, {}
    for name, array in arrays.items():
        fed[f"in_{name}"] = _np.ascontiguousarray(array)
        A[name] = nc.dram_tensor(f"in_{name}", array.shape, _mybir.dt.from_np(array.dtype), kind="ExternalInput").ap()
    A["x1"] = nc.dram_tensor("x1_between_layers", (B, T, D), F32, kind="Internal").ap()
    A["out"] = nc.dram_tensor("out_dram", (B, T, D), F32, kind="ExternalOutput").ap()
    program(nc, A)
    return _run(nc, [fed], core_ids=[0]).results[0]["out_dram"]
```

```python
from contextlib import ExitStack

import numpy as np

import concourse.bass as bass
from concourse import mybir

ALU = mybir.AluOpType
ACT = mybir.ActivationFunctionType
AX = mybir.AxisListType
F32 = mybir.dt.float32
F32R = mybir.dt.float32r
U8 = mybir.dt.uint8

P = 128
B, T, D = 16, 112, 512
TC = 375
KT = 3
TK = TC // KT
TE = TC + TC % 2
C = D // P
HEADS, HD = 16, 32
HG = P // HD
SCALE = HD ** -0.5
EPS = 1e-5
BANK = 512
LOWEST = -3.0e38

VECTORS = ["ln_gamma", "ln_beta", "ln1_w", "ln1_b", "ln2_w", "ln2_b", "maa_x", "maa_k", "maa_w", "maa_v", "maa_r",
           "maa_g", "time_decay", "gn_w", "gn_b", "ffn_k", "ffn_r", "u"]
S = 16
MAA, MD, TD = 5, 32, 64
NRING = 4
NREP = 8
NPROD = 8
QUAD = 4
MIXES = ["maa_w", "maa_v", "maa_k", "maa_r", "maa_g"]
MIX_ROW = [1, 2, 0, 3, 4]
MIX_SLOT = [2, 4, 7, 9, 11]
REDUCE_SLOT = [7, 10, 13]
MIX_BANK = [2, 0, 2, 1, 0]
USE_BANK = {"v": 0, "k": 2, "r": 1, "g": 2}
VEC = {name: n for n, name in enumerate(VECTORS)}


def index(b):
    return 2 * b[0] + b[1]


def later(b, steps):
    n = b[1] + steps
    return b[0] + n // 2, n % 2


def count(b, per_batch, done):
    return index(b) * per_batch + done


def at_least(b, n):
    return not isinstance(b[0], int) or index(b) >= n


def on_pool(j):
    return j % QUAD != QUAD - 1


def products(j):
    quads, more = divmod(j + 1, QUAD)
    return (QUAD - 1) * quads + more, quads


POOL_PRODUCTS, DVE_PRODUCTS = products(S - 1)


def is_batch(b, n):
    return isinstance(b[0], int) and index(b) == n


def cross_attention(nc, A, ident, vec, W, w_loaded):
    with ExitStack() as ctx:
        def sb(name, shape, dt=F32):
            return ctx.enter_context(nc.sbuf_tensor(name, shape, dt))

        def sem(name):
            return ctx.enter_context(nc.semaphore(name))

        def sem2(name):
            return [sem(f"{name}_{q}") for q in range(2)]

        bank = [ctx.enter_context(nc.psum_tensor(f"a_bank{n}", [P, BANK], F32)) for n in range(8)]
        score_bank, proj_bank, q_bank, pt_bank, av_bank = bank[0:2], bank[2:4], bank[4], bank[5:7], bank[7]

        wq, wo = sb("wq_sb", [P, C, D]), sb("wo_sb", [P, C, D])
        headmask = sb("headmask_sb", [P, HG])
        gate = sb("gate_sb", [T, 1])
        tanh_gate = sb("tanh_gate", [T, 1])
        eps_exp = sb("a_eps_exp", [TK, KT])
        to_inf = sb("to_inf", [T, 3])
        mask8 = sb("mask8", [T, B, TC], U8)
        unmask = sb("unmask", [T, 2, TC])
        xT = sb("xT_sb", [P, 2, C, T])
        x_tok = sb("x_tok", [T, 2, D])
        ctx_tok = sb("ctx_tok", [TK, 2, KT, D])
        ctx_norm = sb("ctx_norm", [TK, KT, D])
        stats = sb("ctx_stats", [TK, KT, 6])
        meanvar = sb("ctx_meanvar", [TK, KT, 2])
        var_eps = sb("ctx_var_eps", [TK, KT])
        rstd = sb("ctx_rstd", [TK, KT])
        wk_hi, wk_lo, wv_hi, wv_lo = (sb(n, [P, C, D], F32R) for n in ("wk_hi", "wk_lo", "wv_hi", "wv_lo"))
        whole = sb("whole", [P, 2, TE])
        aT_hi, aT_lo = sb("aT_hi", [P, C, TE], F32R), sb("aT_lo", [P, C, TE], F32R)
        keyT_hi, keyT_lo = sb("keyT_hi", [P, 2, C, TE], F32R), sb("keyT_lo", [P, 2, C, TE], F32R)
        query, query_hi = sb("query", [P, C, T]), sb("query_hi", [P, C, T], F32R)
        value = sb("value", [TK, 2, KT, D])
        qpad_hi = sb("qpad_hi", [P, 2, C, HG, T], F32R)
        qpad_lo = sb("qpad_lo", [P, 2, C, HG, T], F32R)
        probs = sb("probs", [T, 2, HG, TC])
        maxes = sb("maxes", [T, 2, HG])
        negmax = sb("negmax", [T, 2, HG])
        sums = sb("sums", [T, 2, HG])
        inv = sb("inv", [T, 2, HG])
        probsT = sb("probsT", [TK, 2, KT, HG * T])
        attnT = sb("attnT", [P, C, T])
        x1 = sb("x1_sb", [T, D])

        s_w = {n: sem(f"a_{n}_loaded") for n in ("wq", "wk", "wv", "wo", "ident", "headmask", "vec", "gate", "mask")}
        s_xT, s_xtok, s_ctx, s_x1st = sem2("xT_loaded"), sem2("xtok_loaded"), sem2("ctx_loaded"), sem("x1_stored")
        s_gate = sem("gate_ready")
        s_const = sem("a_constants_set")
        s_unmask1 = sem("unmask_steps")
        s_stats, s_mv, s_ve = sem("ctx_stats_done"), sem("ctx_meanvar_done"), sem("ctx_vareps_done")
        s_rstd, s_ctxn = sem("ctx_rstd_done"), sem("ctx_normalised")
        s_proj, s_projev = sem("proj_done"), sem("proj_copied")
        s_whi, s_wlo = sem("weights_rounded"), sem("weights_split")
        s_zero = sem("aT_ends_set")
        s_split = sem("low_part_ready")
        s_q, s_qhi, s_qlo = sem("q_done"), sem("query_copied"), sem("query_split")
        s_qpad, s_qpadlo = sem("qpad_hi_ready"), sem("qpad_lo_ready")
        s_score, s_masked, s_negmax = sem("score_done"), sem("score_masked"), sem("negmax_ready")
        s_exp, s_inv, s_probs = sem("exp_done"), sem("inv_ready"), sem("probs_ready")
        s_pt, s_ptev = sem("probs_transposed"), sem("probsT_ready")
        s_av, s_attn, s_wo, s_x1 = sem("av_done"), sem("attnT_ready"), sem("wo_done"), sem("x1_ready")

        FIRST, LOOP, LAST = [(0, 0), (0, 1), (1, 0), (1, 1)], (2, B // 2 - 1), [(B // 2 - 1, 0), (B // 2 - 1, 1), (B // 2, 0)]

        def run(engine, step):
            for n in FIRST:
                step(n, True, not is_batch(n, 0), True)
            with engine.Fori(*LOOP) as k:
                for q in range(2):
                    step((k, q), True, True, True)
            for n in LAST:
                step(n, not is_batch(n, B), True, is_batch(n, B - 2))

        block = ctx.enter_context(nc.Block())

        @block.sync
        def _(sp):
            def load_ctx(b):
                if at_least(b, 2):
                    sp.wait_ge(s_ctxn, count(later(b, -2), 1, 1))
                sp.dma_start(ctx_tok[:, b[1]], A["ctx"][index(b)].rearrange("(k p) d -> p k d", p=TK)).then_inc(s_ctx[b[1]], 16)

            def load_x(b):
                if at_least(b, 2):
                    sp.wait_ge(s_q, count(later(b, -2), 1, 1))
                sp.dma_start(xT[:, b[1]], A["xT"][index(b)]).then_inc(s_xT[b[1]], 16)

            def load_xtok(b):
                if at_least(b, 2):
                    sp.wait_ge(s_x1, count(later(b, -2), 1, 1))
                sp.dma_start(x_tok[:, b[1]], A["x"][index(b)]).then_inc(s_xtok[b[1]], 16)

            load_ctx((0, 0))
            sp.dma_start(vec[:], A["vec"]).then_inc(s_w["vec"], 16)
            sp.dma_start(ident[:], A["ident"]).then_inc(s_w["ident"], 16)
            sp.dma_start(headmask[:], A["headmask"]).then_inc(s_w["headmask"], 16)
            load_x((0, 0))
            sp.dma_start(wq[:], A["wq"]).then_inc(s_w["wq"], 16)
            sp.dma_start(W["wk"][:], A["wk"]).then_inc(s_w["wk"], 16)
            load_ctx((0, 1))
            load_x((0, 1))
            sp.dma_start(W["wv"][:], A["wv"]).then_inc(s_w["wv"], 16)
            sp.dma_start(mask8[:], A["mask"].rearrange("(o b) t -> o b t", o=1).broadcast_to([T, B, TC])).then_inc(s_w["mask"], 16)
            sp.dma_start(gate[:], A["gate"].broadcast_to([T, 1])).then_inc(s_w["gate"], 16)
            sp.dma_start(wo[:], A["wo"]).then_inc(s_w["wo"], 16)

            def step(n, project, attend, normalise):
                if normalise and not is_batch(n, 0):
                    load_ctx(later(n, 1))
                    load_x(later(n, 1))
                if attend:
                    load_xtok(later(n, -1))
                if is_batch(n, 1):
                    sp.wait_ge(s_wlo, 2 * C)
                    for name in EARLY:
                        sp.dma_start(W[name][:], A["b_" + name]).then_inc(w_loaded[name], 16)
                if attend:
                    m = later(n, -1)
                    sp.wait_ge(s_x1, count(m, 1, 1))
                    sp.dma_start(A["x1"][index(m)], x1[:]).then_inc(s_x1st, 16)

            run(sp, step)
            sp.wait_ge(s_x1st, 16 * B)

        @block.gpsimd
        def _(pool):
            for i, x in enumerate((1.0, 3.0e38, 10.0)):
                pool.memset(to_inf[:, i:i + 1], x)
            pool.memset(eps_exp[:], -0.5).then_inc(s_const, 1)

            def step(n, project, attend, normalise):
                if attend:
                    m = later(n, -1)
                    q = m[1]
                    if is_batch(m, 0):
                        pool.wait_ge(s_w["mask"], 16)
                    if at_least(m, 2):
                        pool.wait_ge(s_masked, count(later(m, -2), HEADS, HEADS))
                    pool.tensor_copy(unmask[:, q], mask8[:, index(m), :]).then_inc(s_unmask1, 1)
                    for i, op in enumerate((ALU.subtract, ALU.mult, ALU.mult)):
                        pool.wait_ge(s_unmask1, count(m, C, i + 1))
                        last = pool.tensor_tensor(unmask[:, q], unmask[:, q], to_inf[:, i:i + 1].broadcast_to([T, TC]), op)
                        last.then_inc(s_unmask1, 1)
                if project:
                    split_aT(n)
                    if is_batch(n, 0):
                        pool.wait_ge(s_w["headmask"], 16)
                    split_query(n)
                    split_key(n, 0)
                    split_key(n, 1)
                    split_key(n, 2)
                if normalise:
                    rsqrt(later(n, 1))
                if project:
                    split_key(n, 3)

            def split_aT(b):
                for c in range(C):
                    pool.wait_ge(s_projev, count(b, 11, c + 1))
                    pool.tensor_tensor(aT_lo[:, c, 0:TC], whole[:, c % 2, 0:TC], aT_hi[:, c, 0:TC].bitcast(F32),
                                       ALU.subtract).then_inc(s_split, 1)

            def split_key(b, c):
                pool.wait_ge(s_projev, count(b, 11, C + c + 1))
                pool.tensor_tensor(keyT_lo[:, b[1], c], whole[:, c % 2], keyT_hi[:, b[1], c].bitcast(F32),
                                   ALU.subtract).then_inc(s_split, 1)

            def split_query(b):
                pool.wait_ge(s_qhi, count(b, 1, 1))
                pool.tensor_tensor(query[:], query[:], query_hi[:].bitcast(F32), ALU.subtract).then_inc(s_qlo, 1)
                pool.wait_ge(s_qlo, count(b, 1, 1))
                for c in range(C):
                    last = pool.tensor_tensor(qpad_lo[:, b[1], c], query[:, c].unsqueeze(1).broadcast_to([P, HG, T]),
                                              headmask[:].unsqueeze(2).broadcast_to([P, HG, T]), ALU.mult)
                last.then_inc(s_qpadlo, 1)

            def rsqrt(b):
                pool.wait_ge(s_ve, count(b, 1, 1))
                if at_least(b, 1):
                    pool.wait_ge(s_ctxn, count(later(b, -1), 1, 1))
                pool.tensor_tensor(rstd[:], var_eps[:], eps_exp[:], ALU.pow).then_inc(s_rstd, 1)

            pool.wait_ge(s_const, 1)
            rsqrt((0, 0))
            run(pool, step)

        @block.vector
        def _(dve):
            def ln_stats(b):
                dve.wait_ge(s_ctx[b[1]], 16 * (b[0] + 1))
                for k in range(KT):
                    last = dve.bn_stats(stats[:, k], ctx_tok[:, b[1], k])
                last.then_inc(s_stats, 1)
                dve.wait_ge(s_stats, count(b, 1, 1))
                dve.memset(var_eps[:], 0.0)
                for k in range(KT):
                    last = dve.bn_aggr(meanvar[:, k], stats[:, k])
                last.then_inc(s_mv, 1)
                dve.wait_ge(s_mv, count(b, 1, 1))
                dve.tensor_scalar(var_eps[:], meanvar[:, :, 1], EPS, None, ALU.add).then_inc(s_ve, 1)

            def ln_apply(b):
                dve.wait_ge(s_rstd, count(b, 1, 1))
                if at_least(b, 1):
                    dve.wait_ge(s_proj, count(later(b, -1), 11, C))
                for k in range(KT):
                    last = dve.tensor_scalar(ctx_norm[:, k], ctx_tok[:, b[1], k], meanvar[:, k, 0:1], rstd[:, k:k + 1],
                                             ALU.subtract, ALU.mult)
                last.then_inc(s_ctxn, 1)

            def split_weight(low, w, high, n, c):
                dve.wait_ge(s_whi, n * C + c + 1)
                dve.tensor_tensor(low[:, c], w[:, c], high[:, c].bitcast(F32), ALU.subtract).then_inc(s_wlo, 1)

            def pad_queries(b, c):
                if is_batch(b, 0) and c == 0:
                    dve.wait_ge(s_w["headmask"], 16)
                dve.wait_ge(s_qhi, count(b, 1, 1))
                dve.tensor_tensor(qpad_hi[:, b[1], c], query_hi[:, c].bitcast(F32).unsqueeze(1).broadcast_to([P, HG, T]),
                                  headmask[:].unsqueeze(2).broadcast_to([P, HG, T]), ALU.mult).then_inc(s_qpad, 1)

            def mask_scores(m, g, heads):
                if g == 0 and heads[0] == 0:
                    dve.wait_ge(s_unmask1, count(m, C, C))
                if heads[0] == 0 and (g >= 2 or at_least(m, 1)):
                    dve.wait_ge(s_pt, count(m, C * KT, (g - 1) * KT))
                for i in heads:
                    h = g * HG + i
                    dve.wait_ge(s_score, count(m, HEADS, h + 1))
                    if i == heads[0]:
                        dve.memset(negmax[:, g % 2, i:i + 1], 0.0)
                    else:
                        negate_max(m, g, i - 1)
                    dve.tensor_tensor_reduce(out=probs[:, g % 2, i], in0=score_bank[h % 2][0:T, 0:TC], in1=unmask[:, m[1]],
                                             scale=SCALE, scalar=LOWEST, op0=ALU.add, op1=ALU.max,
                                             accum_out=maxes[:, g % 2, i:i + 1]).then_inc(s_masked, 1)
                negate_max(m, g, heads[-1])

            def negate_max(m, g, i):
                dve.wait_ge(s_masked, count(m, HEADS, g * HG + i + 1))
                dve.tensor_scalar(negmax[:, g % 2, i:i + 1], maxes[:, g % 2, i:i + 1], -1.0, None, ALU.mult).then_inc(s_negmax, 1)

            def normalise_probs(m, g, heads):
                for i in heads:
                    h = g * HG + i
                    dve.wait_ge(s_exp, count(m, HEADS, h + 1))
                    dve.reciprocal(inv[:, g % 2, i:i + 1], sums[:, g % 2, i:i + 1]).then_inc(s_inv, 1)
                    dve.wait_ge(s_inv, count(m, HEADS, h + 1))
                    last = dve.tensor_scalar(probs[:, g % 2, i], probs[:, g % 2, i], inv[:, g % 2, i:i + 1], None, ALU.mult)
                if heads[-1] == HG - 1:
                    last.then_inc(s_probs, 1)

            def residual(m):
                if at_least(m, 1):
                    dve.wait_ge(s_x1st, 16 * index(m))
                dve.wait_ge(s_xtok[m[1]], 16 * (m[0] + 1))
                dve.wait_ge(s_wo, count(m, 1, 1))
                if is_batch(m, 0):
                    dve.wait_ge(s_gate, 1)
                dve.scalar_tensor_tensor(out=x1[:], in0=av_bank[0:T, :], scalar=tanh_gate[:, 0:1], in1=x_tok[:, m[1]],
                                         op0=ALU.mult, op1=ALU.add).then_inc(s_x1, 1)

            def step(n, project, attend, normalise):
                m = later(n, -1)
                for g in range(C):
                    if attend:
                        mask_scores(m, g, (0, 1))
                        normalise_probs(m, g, (0, 1))
                    if project and g in (1, 2):
                        pad_queries(n, 2 * g - 2)
                    if is_batch(n, 0) and g < 2:
                        for c in range(C):
                            split_weight((wk_lo, wv_lo)[g], W[("wk", "wv")[g]], (wk_hi, wv_hi)[g], g, c)
                    if attend:
                        mask_scores(m, g, (2, 3))
                        normalise_probs(m, g, (2, 3))
                    if project and g in (1, 2):
                        pad_queries(n, 2 * g - 1)
                    if normalise and g == 0:
                        ln_stats(later(n, 1))
                    if normalise and g == 3:
                        ln_apply(later(n, 1))
                if attend:
                    residual(m)

            ln_stats((0, 0))
            ln_apply((0, 0))
            run(dve, step)

        @block.scalar
        def _(act):

            def round_weight(w, high, name):
                act.wait_ge(s_w[name], 16)
                for c in range(C):
                    act.copy(high[:, c], w[:, c]).then_inc(s_whi, 1)

            act.wait_ge(s_w["vec"], 16)
            for dst in (aT_hi, aT_lo):
                last = act.activation(dst[:, :, TC:TE], vec[:, 0, :].unsqueeze(2), ACT.Identity, scale=0.0)
            last.then_inc(s_zero, 1)

            def whole_free(b, u):
                if u >= 2 or at_least(b, 1):
                    act.wait_ge(s_split, count(b, 2 * C, u - 1))
                return whole[:, u % 2]

            def copy_aT(b, c):
                act.wait_ge(s_proj, count(b, 11, c + 1))
                for dst in (aT_hi[:, c, 0:TC], whole_free(b, c)[:, 0:TC]):
                    last = act.activation(dst, proj_bank[(b[1] * 11 + c) % 2][:, 0:TC], ACT.Identity,
                                          scale=vec[:, VEC["ln_gamma"], c:c + 1], bias=vec[:, VEC["ln_beta"], c:c + 1])
                last.then_inc(s_projev, 1)

            def copy_key(b, c):
                u = C + c
                act.wait_ge(s_proj, count(b, 11, u + 1))
                for dst in (keyT_hi[:, b[1], c], whole_free(b, u)):
                    last = act.copy(dst, proj_bank[(b[1] * 11 + u) % 2][:, 0:TE])
                last.then_inc(s_projev, 1)

            def copy_query(b):
                act.wait_ge(s_q, count(b, 1, 1))
                if at_least(b, 1):
                    act.wait_ge(s_qpad, count(b, C, 0))
                    act.wait_ge(s_qpadlo, count(b, 1, 0))
                for dst in (query_hi, query):
                    last = act.copy(dst[:].rearrange("p c t -> p (c t)"), q_bank[:, 0:C * T])
                last.then_inc(s_qhi, 1)

            def copy_value(b, k):
                u = 2 * C + k
                act.wait_ge(s_proj, count(b, 11, u + 1))
                act.copy(value[:, b[1], k], proj_bank[(b[1] * 11 + u) % 2][0:TK, :]).then_inc(s_projev, 1)

            def exps(m, g, heads):
                for i in heads:
                    act.wait_ge(s_negmax, count(m, HEADS, g * HG + i + 1))
                    act.activation(probs[:, g % 2, i], probs[:, g % 2, i], ACT.Exp, bias=negmax[:, g % 2, i:i + 1],
                                   accum_out=sums[:, g % 2, i:i + 1]).then_inc(s_exp, 1)

            def copy_probsT(m, g, tiles):
                for k in tiles:
                    u = g * KT + k
                    act.wait_ge(s_pt, count(m, C * KT, u + 1))
                    if k == 0 and (g >= 2 or at_least(m, 1)):
                        act.wait_ge(s_av, count(m, C, g - 1))
                    act.copy(probsT[:, g % 2, k], pt_bank[u % 2][0:TK, 0:HG * T]).then_inc(s_ptev, 1)

            def copy_attn(m, g):
                act.wait_ge(s_av, count(m, C, g + 1))
                if g == 0 and at_least(m, 1):
                    act.wait_ge(s_wo, count(later(m, -1), 1, 1))
                act.copy(attnT[:, g], av_bank[:, g * T:(g + 1) * T]).then_inc(s_attn, 1)

            def step(n, project, attend, normalise):
                m = later(n, -1)
                if attend:
                    exps(m, 0, (0, 1))
                if project:
                    copy_aT(n, 0)
                    copy_aT(n, 1)
                if attend:
                    exps(m, 0, (2, 3))
                if project:
                    copy_aT(n, 2)
                    copy_aT(n, 3)
                if is_batch(n, 0):
                    round_weight(W["wk"], wk_hi, "wk")
                    round_weight(W["wv"], wv_hi, "wv")
                if attend:
                    copy_probsT(m, 0, (0, 1))
                if project:
                    copy_query(n)
                for g in range(1, C):
                    if attend:
                        exps(m, g, (0, 1))
                        copy_probsT(m, g - 1, (2,))
                    if project:
                        if g < 3:
                            copy_key(n, 2 * g - 2)
                        else:
                            copy_value(n, 0)
                    if attend:
                        exps(m, g, (2, 3))
                        copy_attn(m, g - 1)
                    if project:
                        if g < 3:
                            copy_key(n, 2 * g - 1)
                        else:
                            copy_value(n, 1)
                    if attend:
                        copy_probsT(m, g, (0, 1))
                if attend:
                    copy_probsT(m, C - 1, (2,))
                if project:
                    copy_value(n, 2)
                if is_batch(n, 0):
                    act.wait_ge(s_w["gate"], 16)
                    act.activation(tanh_gate[:], gate[:], ACT.Tanh).then_inc(s_gate, 1)
                if attend:
                    copy_attn(m, C - 1)

            run(act, step)

        @block.tensor
        def _(pe):
            def proj_free(b, u):
                if u >= 2 or at_least(b, 1):
                    pe.wait_ge(s_projev, count(b, 11, u - 1))
                return proj_bank[(b[1] * 11 + u) % 2]

            def transpose_ctx(b, c):
                dst = proj_free(b, c)
                pe.wait_ge(s_ctxn, count(b, 1, 1))
                for k in range(KT):
                    last = pe.transpose(dst[:, k * TK:(k + 1) * TK], ctx_norm[:, k, c * P:(c + 1) * P], ident[0:TK, 0:TK])
                last.then_inc(s_proj, 1)

            def by_parts(dst, left, right, start, stop):
                (lh, ll), (rh, rl) = left, right
                pe.matmul(dst, ll, rh, start=start, stop=False)
                pe.matmul(dst, lh, rl, start=False, stop=False)
                return pe.matmul(dst, lh, rh, start=False, stop=stop)

            def project_key(b, m):
                dst = proj_free(b, C + m)
                pe.wait_ge(s_split, count(b, 2 * C, C))
                if is_batch(b, 0):
                    pe.wait_ge(s_zero, 1)
                for c in range(C):
                    o = slice(m * P, (m + 1) * P)
                    last = by_parts(dst[:, 0:TE], (wk_hi[:, c, o], wk_lo[:, c, o]), (aT_hi[:, c], aT_lo[:, c]), c == 0, c == C - 1)
                last.then_inc(s_proj, 1)

            def project_value(b, k, inner=range(C)):
                dst = proj_bank[(b[1] * 11 + 2 * C + k) % 2]
                if inner[0] == 0:
                    proj_free(b, 2 * C + k)
                for c in inner:
                    t = slice(k * TK, k * TK + TE - TC + TK)
                    last = by_parts(dst[0:TE - TC + TK, :], (aT_hi[:, c, t], aT_lo[:, c, t]), (wv_hi[:, c], wv_lo[:, c]),
                                    c == 0, c == C - 1)
                if inner[-1] == C - 1:
                    last.then_inc(s_proj, 1)

            def project_query(b, m):
                if m == 0:
                    pe.wait_ge(s_xT[b[1]], 16 * (b[0] + 1))
                    if at_least(b, 1):
                        pe.wait_ge(s_qhi, count(b, 1, 0))
                for c in range(C):
                    last = pe.matmul(q_bank[:, m * T:(m + 1) * T], wq[:, c, m * P:(m + 1) * P], xT[:, b[1], c], start=(c == 0), stop=(c == C - 1))
                if m == C - 1:
                    last.then_inc(s_q, 1)

            def scores(m, g, heads):
                if g == 0 and heads[0] == 0:
                    pe.wait_ge(s_qpad, count(m, C, C))
                    pe.wait_ge(s_qpadlo, count(m, 1, 1))
                    pe.wait_ge(s_split, count(m, 2 * C, 2 * C))
                    pe.wait_ge(s_projev, count(m, 11, 11))
                for i in heads:
                    h = g * HG + i
                    if h >= 2 or at_least(m, 1):
                        pe.wait_ge(s_masked, count(m, HEADS, h - 1))
                    q = m[1]
                    by_parts(score_bank[h % 2][0:T, 0:TE], (qpad_hi[:, q, g, i], qpad_lo[:, q, g, i]),
                             (keyT_hi[:, q, g], keyT_lo[:, q, g]), True, True).then_inc(s_score, 1)

            def transpose_probs(m, g, tiles):
                pe.wait_ge(s_probs, count(m, C, g + 1))
                for k in tiles:
                    u = g * KT + k
                    if u >= 2 or at_least(m, 1):
                        pe.wait_ge(s_ptev, count(m, C * KT, u - 1))
                    for i in range(HG):
                        last = pe.transpose(pt_bank[u % 2][0:TK, i * T:(i + 1) * T], probs[:, g % 2, i, k * TK:(k + 1) * TK],
                                            ident[0:T, 0:T])
                    last.then_inc(s_pt, 1)

            def weigh_values(m, g):
                pe.wait_ge(s_ptev, count(m, C * KT, (g + 1) * KT))
                if g > 0:
                    pe.wait_ge(s_attn, count(m, C, g))
                elif at_least(m, 1):
                    pe.wait_ge(s_x1, count(later(m, -1), 1, 1))
                for i in range(HG):
                    h = g * HG + i
                    for k in range(KT):
                        last = pe.matmul(av_bank[i * HD:(i + 1) * HD, g * T:(g + 1) * T], value[:, m[1], k, h * HD:(h + 1) * HD],
                                         probsT[:, g % 2, k, i * T:(i + 1) * T], start=(k == 0), stop=(k == KT - 1))
                last.then_inc(s_av, 1)

            def project_out(m):
                pe.wait_ge(s_attn, count(m, C, C))
                for c in range(C):
                    last = pe.matmul(av_bank[0:T, :], attnT[:, c], wo[:, c], start=(c == 0), stop=(c == C - 1))
                last.then_inc(s_wo, 1)

            def step(n, project, attend, normalise):
                m = later(n, -1)
                if attend:
                    scores(m, 0, (0, 1))
                if project:
                    transpose_ctx(n, 0)
                    transpose_ctx(n, 1)
                    if is_batch(n, 0):
                        pe.wait_ge(s_w["wq"], 16)
                    project_query(n, 0)
                    project_query(n, 1)
                if attend:
                    scores(m, 0, (2, 3))
                if project:
                    transpose_ctx(n, 2)
                    transpose_ctx(n, 3)
                    project_query(n, 2)
                    project_query(n, 3)
                if attend:
                    transpose_probs(m, 0, (0, 1))
                for g in range(1, C):
                    if attend:
                        scores(m, g, (0, 1))
                        transpose_probs(m, g - 1, (2,))
                    if project:
                        if g < 3:
                            if is_batch(n, 0) and g == 1:
                                pe.wait_ge(s_wlo, C)
                            project_key(n, 2 * g - 2)
                        else:
                            if is_batch(n, 0):
                                pe.wait_ge(s_wlo, 2 * C)
                            project_value(n, 0)
                    if attend:
                        scores(m, g, (2, 3))
                        weigh_values(m, g - 1)
                    if project:
                        if g < 3:
                            project_key(n, 2 * g - 1)
                        else:
                            project_value(n, 1)
                    if attend:
                        transpose_probs(m, g, (0, 1))
                if project:
                    project_value(n, 2, (0, 1))
                if attend:
                    transpose_probs(m, C - 1, (2,))
                if project:
                    project_value(n, 2, (2, 3))
                if attend:
                    weigh_values(m, C - 1)
                    if is_batch(m, 0):
                        pe.wait_ge(s_w["wo"], 16)
                    project_out(m)

            pe.wait_ge(s_w["ident"], 16)
            run(pe, step)


def rwkv_block(nc, A, ident, vec, W, w_loaded):
    with ExitStack() as ctx:
        def sb(name, shape, dt=F32):
            return ctx.enter_context(nc.sbuf_tensor(name, shape, dt))

        def sem(name):
            return ctx.enter_context(nc.semaphore(name))

        def sem2(name):
            return [sem(f"{name}_{q}") for q in range(2)]

        bank = [ctx.enter_context(nc.psum_tensor(f"b_bank{n}", [P, BANK], F32)) for n in range(8)]
        out_bank, pre_bank, post_bank = bank[2], bank[3:6], bank[6:8]

        CT = C * T
        half_gn = sb("half_gn", [P, 2, C])
        maa1 = sb("maa1_sb", [P, C, MAA * MD])
        maa2 = sb("maa2_sb", [P, MAA, D])
        td1 = sb("td1_sb", [P, C, TD])
        td2 = sb("td2_sb", [P, D])
        headmean = sb("headmean", [P, P])
        bonus_w = sb("bonus_w", [P, C, P])
        collect = sb("collect_sb", [P, S, P // QUAD])
        s0 = sb("s0_sb", [P, B, C, S])
        rows = sb("rows_sb", [P, B, 2, C])
        neg_half = sb("neg_half", [T, 1])
        ln_eps = sb("b_eps", [P, 1])

        W = dict(W) | {n: sb(f"b_{n}", [P, C, D]) for n in BLOCK_WEIGHTS if n not in EARLY}
        x1 = sb("b_x1", [T, 2, D])
        ln_tok = sb("ln1_tok", [T, D])
        bn6, mv, ve, rs = sb("ln1_bn", [T, 6]), sb("ln1_mv", [T, 2]), sb("ln1_ve", [T, 1]), sb("ln1_rs", [T, 1])
        xa = sb("xa", [P, C, T + 1])
        sx = sb("sx", [P, C, T])
        xin = sb("xin", [P, C, T])
        th = sb("th", [P, 2, T])
        mixed = sb("mixed", [P, 2, C, T])
        xm = sb("xm", [P, 2, C, T])
        ttd = sb("ttd", [P, T])
        etd = sb("etd", [P, C, T])
        wdec = sb("wdec", [P, 2, C, T])
        v = sb("v_sb", [P, 2, C, T])
        vrep = sb("vrep", [P, NREP, CT])
        key = sb("key", [P, 2, C, T])
        rec = sb("rec", [P, 2, C, T])
        tg = sb("tg", [P, C, T])
        gate2 = sb("gate2", [P, 2, C, T])
        rk = sb("rk", [P, C, T])
        bv = sb("bv", [P, C, T])
        kv = sb("kv", [P, NRING, BANK])
        st = sb("st", [P, NRING, CT])
        rst = sb("rst", [P, NPROD, CT])
        same_head = rst[:, 0, 0:P]
        wkv = sb("wkv", [P, C, T])
        cen = sb("cen", [P, C, T])
        sq = sb("sq", [P, C, T])
        gated = sb("gated", [P, C, T])
        x1p = sb("x1_post", [T, 2, D])
        x2 = sb("x2", [T, D])
        ln2_tok = sb("ln2_tok", [T, D])
        bn6p, mvp, vep, rsp = sb("ln2_bn", [T, 6]), sb("ln2_mv", [T, 2]), sb("ln2_ve", [T, 1]), sb("ln2_rs", [T, 1])
        xc = sb("xc", [P, C, T + 1])
        sx2 = sb("sx2", [P, C, T])
        xk2 = sb("xk2", [P, C, T])
        xr2 = sb("xr2", [P, C, T])
        kk = sb("kk", [P, C, T])
        trr = sb("trr", [T, D])
        fin = sb("fin", [T, 2, D])

        small = ("maa1", "td1", "key_value", "value_value", "collect", "s0", "rows", "maa2", "td2")
        s_c = {n: sem(f"b_{n}_loaded") for n in small}
        s_x1, s_x1p, s_store = sem2("b_x1_loaded"), sem2("x1_post_loaded"), sem2("out_stored")
        s_zero, s_setup = sem("zeros_set"), sem("setup_done")
        s_bn, s_mv, s_ve, s_rs, s_ln = (sem(f"ln1_{n}") for n in ("stats", "meanvar", "vareps", "rstd", "normalised"))
        s_bnp, s_mvp, s_vep, s_rsp, s_lnp = (sem(f"ln2_{n}") for n in ("stats", "meanvar", "vareps", "rstd", "normalised"))
        s_t1, s_xa0, s_xa, s_sx, s_xin = sem("x_transposed"), sem("xa_state"), sem("xa_ready"), sem("sx_ready"), sem("xin_ready")
        s_w1, s_th, s_mixmm, s_mixed, s_xm = (sem(n) for n in ("maa1_done", "th_ready", "maa2_done", "mixed_ready", "xm_ready"))
        s_td1, s_ttd, s_td2, s_etd, s_wdec = (sem(n) for n in ("td1_done", "ttd_ready", "td2_done", "etd_ready", "decay_ready"))
        s_vmm, s_v, s_vst, s_vrep = sem("v_done"), sem("v_ready"), sem2("v_stored"), sem2("vrep_loaded")
        s_kmm, s_k, s_rmm, s_r = sem("k_done"), sem("k_ready"), sem("r_done"), sem("r_ready")
        s_gmm, s_tg, s_g = sem("g_done"), sem("tg_ready"), sem("gate_ready2")
        s_rk, s_bonus, s_bv = sem("rk_ready"), sem("bonus_done"), sem("bv_ready")
        s_kv0, s_kv, s_st = sem("kv_state_ready"), sem("kv_ready"), sem("states_ready")
        s_pprod, s_vprod, s_red = sem("pool_products"), sem("vector_products"), sem("reduced")
        s_wkv1, s_wkv = sem("wkv_state_part"), sem("wkv_ready")
        s_mean, s_cen, s_sq, s_var, s_ln2, s_grs = (sem(n) for n in ("gn_mean", "gn_centred", "gn_squared", "gn_var", "gn_log", "gn_rstd"))
        s_gnorm, s_gaff, s_gated = sem("gn_normalised"), sem("gn_scaled"), sem("gated_ready")
        s_wo, s_x2, s_t2, s_xc0, s_xc = sem("b_wo_done"), sem("x2_ready"), sem("x2_transposed"), sem("xc_state"), sem("xc_ready")
        s_sx2, s_xk2, s_xr2 = sem("sx2_ready"), sem("xk2_ready"), sem("xr2_ready")
        s_fk, s_relu, s_kk, s_fr, s_rr = (sem(n) for n in ("wfk_done", "relu_ready", "kk_ready", "wfr_done", "rr_ready"))
        s_fv, s_ff, s_fin = sem("wfv_done"), sem("ffn_scaled"), sem("out_ready")

        N_ITER = B + 2
        LOOP = (2, B // 2 - 1)

        def vrep_loads(b, r):
            return 16 * QUAD * (2 * index(b) + r // 2 + 1)

        def run(engine, step):
            for i in range(2 * LOOP[0]):
                step((i // 2, i % 2), True, i >= 1, i >= 2, i == 0)
            with engine.Fori(*LOOP) as k:
                for q in range(2):
                    step((k, q), True, True, True, False)
            for i in range(2 * LOOP[1], N_ITER):
                step((i // 2, i % 2), i < B, i <= B, True, False)

        block = ctx.enter_context(nc.Block())

        @block.sync
        def _(sp):
            def load_x1(b):
                if at_least(b, 2):
                    sp.wait_ge(s_ln, count(later(b, -2), 1, 1))
                sp.dma_start(x1[:, b[1]], A["x1"][index(b)]).then_inc(s_x1[b[1]], 16)

            load_x1((0, 0))
            sp.dma_start(rows[:], A["rows"]).then_inc(s_c["rows"], 16)
            sp.dma_start(maa1[:], A["maa1"]).then_inc(s_c["maa1"], 16)
            sp.dma_start(td1[:], A["td1"]).then_inc(s_c["td1"], 16)
            sp.wait_ge(s_zero, 2)
            for f in range(MAA):
                r = f % HG * MD
                sp.dma_start(maa2[r:r + MD, f], A["maa2"][f]).then_inc(s_c["maa2"], 16)
            sp.dma_start(td2[0:TD, :], A["td2"]).then_inc(s_c["td2"], 16)
            sp.dma_start(W["wr"][:], A["b_wr"]).then_inc(w_loaded["wr"], 16)
            sp.dma_start(W["wg"][:], A["b_wg"]).then_inc(w_loaded["wg"], 16)
            load_x1((0, 1))
            sp.dma_start(same_head, A["key_value"]).then_inc(s_c["key_value"], 16)
            sp.dma_start(headmean[:], A["value_value"]).then_inc(s_c["value_value"], 16)
            sp.dma_start(s0[:], A["s0"]).then_inc(s_c["s0"], 16)
            sp.dma_start(collect[:], A["collect"]).then_inc(s_c["collect"], 16)
            for name in ("wo", "wfk", "wfr", "wfv"):
                sp.dma_start(W[name][:], A["b_" + name]).then_inc(w_loaded[name], 16)

            def store_out(l):
                sp.wait_ge(s_fin, count(l, 1, 1))
                sp.dma_start(A["out"][index(l)], fin[:, l[1]]).then_inc(s_store[l[1]], 16)

            def store_value(b):
                sp.wait_ge(s_v, count(b, 1, 1))
                if at_least(b, 2):
                    sp.wait_ge(s_vrep[1], vrep_loads(later(b, -2), QUAD - 1))
                sp.dma_start(A["v"][b[1]], v[:, b[1]].rearrange("p c t -> p (c t)")).then_inc(s_vst[b[1]], 16)

            def load_values(b, r):
                for q in range(QUAD):
                    j = QUAD * r + q
                    row = 32 * q + P // S * r
                    src = A["v"][b[1], row:row + P // S].unsqueeze(1).broadcast_to([P // S, S, CT])
                    if q == 0:
                        if r >= 2 or at_least(b, 1):
                            sp.wait_ge(s_kv, count(b, S, QUAD * (r - 1)))
                        if r == 0:
                            sp.wait_ge(s_vst[b[1]], 16 * (b[0] + 1))
                    sp.dma_start(vrep[:, j % NREP], src).then_inc(s_vrep[r % 2], 16)

            def step(n, pre, scan, post, first):
                m = later(n, -1)
                if post:
                    l = later(n, -2)
                    if at_least(l, 2):
                        sp.wait_ge(s_x2, count(later(l, -2), 1, 1))
                    sp.dma_start(x1p[:, l[1]], A["x1"][index(l)]).then_inc(s_x1p[l[1]], 16)
                if pre and not first and not is_batch(n, B - 1):
                    load_x1(later(n, 1))
                if scan:
                    load_values(m, 2)
                    load_values(m, 3)
                if post and at_least(n, 3):
                    store_out(later(n, -3))
                if pre:
                    store_value(n)
                    load_values(n, 0)
                    load_values(n, 1)
                if is_batch(n, N_ITER - 1):
                    store_out(l)

            run(sp, step)
            for q in range(2):
                sp.wait_ge(s_store[q], 16 * (B // 2))

        @block.gpsimd
        def _(pool):
            pool.memset(maa2[:], 0.0).then_inc(s_zero, 1)
            pool.memset(td2[:], 0.0).then_inc(s_zero, 1)
            pool.memset(neg_half[:], -0.5)
            pool.memset(wdec[:], 0.0)
            pool.memset(th[:], 0.0)
            pool.memset(ttd[:], 0.0)
            pool.memset(ln_eps[:], EPS).then_inc(s_zero, 1)
            pool.wait_ge(s_zero, 3)
            pool.wait_ge(s_c["rows"], 16)

            def rstd1(b):
                pool.wait_ge(s_ve, count(b, 1, 1))
                pool.tensor_tensor(rs[:], ve[:], neg_half[:], ALU.pow).then_inc(s_rs, 1)

            def xa_state(b):
                if at_least(b, 1):
                    pool.wait_ge(s_xm, count(later(b, -1), MAA, MAA))
                pool.tensor_copy(xa[:, :, 0:1], rows[:, index(b), 1, :].unsqueeze(2)).then_inc(s_xa0, 1)

            def mix(b, f):
                pool.wait_ge(s_mixed, count(b, MAA, f + 1))
                if f == 2:
                    pool.wait_ge(s_td1, count(b, 1, 1))
                if f == 3:
                    pool.wait_ge(s_vmm, count(b, 1, 1))
                if f == 4:
                    pool.wait_ge(s_kmm, count(b, 1, 1))
                if f == 0 and at_least(b, 1):
                    pool.wait_ge(s_gmm, count(later(b, -1), 1, 1))
                pool.tensor_tensor(xm[:, f % 2], mixed[:, f % 2], xa[:, :, 1:T + 1], ALU.add).then_inc(s_xm, 1)

            def kv_state(m, j):
                if j >= NRING:
                    pool.wait_ge(s_st, count(m, S, j - NRING + 1))
                elif at_least(m, 1):
                    pool.wait_ge(s_st, count(later(m, -1), S, S + j - NRING + 1))
                pool.tensor_copy(kv[:, j % NRING, 0:CT].rearrange("p (c t) -> p c t", c=C)[:, :, 0:1],
                                 s0[:, index(m), :, j:j + 1]).then_inc(s_kv0, 1)

            def product(m, j):
                pool.wait_ge(s_st, count(m, S, j + 1))
                if j >= NPROD or at_least(m, 1):
                    pool.wait_ge(s_red, count(m, QUAD, (j - NPROD) // QUAD + 1))
                pool.tensor_tensor(rst[:, j % NPROD], st[:, j % NRING], rec[:, m[1]].rearrange("p c t -> p (c t)"),
                                   ALU.mult).then_inc(s_pprod, 1)

            def step(n, pre, scan, post, first):
                m, l = later(n, -1), later(n, -2)
                if first:
                    rstd1(n)
                    xa_state(n)
                if is_batch(m, 0):
                    pool.wait_ge(s_c["s0"], 16)
                if scan:
                    pool.wait_ge(s_r, count(m, 1, 1))
                    if at_least(m, 1):
                        pool.wait_ge(s_bonus, count(later(m, -1), 1, 1))
                    pool.tensor_tensor(rk[:], rec[:, m[1]], key[:, m[1]], ALU.mult).then_inc(s_rk, 1)
                for s in range(S):
                    if scan:
                        for j in ([0, 1] if s == 0 else [s + 1] if s + 1 < S else []):
                            kv_state(m, j)
                        if s >= 1 and on_pool(s - 1):
                            product(m, s - 1)
                    if pre and s in MIX_SLOT:
                        mix(n, MIX_SLOT.index(s))
                    if post and s == 7:
                        pool.wait_ge(s_gaff, count(l, 1, 1))
                        pool.wait_ge(s_g, count(l, 1, 1))
                        if at_least(l, 1):
                            pool.wait_ge(s_wo, count(later(l, -1), 1, 1))
                        pool.tensor_tensor(gated[:], sq[:], gate2[:, l[1]], ALU.mult).then_inc(s_gated, 1)
                    if post and s == 9:
                        pool.wait_ge(s_vep, count(l, 1, 1))
                        pool.tensor_tensor(rsp[:], vep[:], neg_half[:], ALU.pow).then_inc(s_rsp, 1)
                        if at_least(l, 1):
                            pool.wait_ge(s_xr2, count(later(l, -1), 1, 1))
                        pool.tensor_copy(xc[:, :, 0:1], rows[:, index(l), 0, :].unsqueeze(2)).then_inc(s_xc0, 1)
                    if pre and s == 12 and not is_batch(n, B - 1):
                        rstd1(later(n, 1))
                        xa_state(later(n, 1))

            run(pool, step)

        @block.vector
        def _(dve):
            def setup():
                dve.tensor_scalar(half_gn[:, 0], vec[:, VEC["gn_w"]], 0.5, None, ALU.mult)
                dve.tensor_scalar(half_gn[:, 1], vec[:, VEC["gn_b"]], 0.5, None, ALU.mult)
                dve.wait_ge(s_c["key_value"], 16)
                dve.wait_ge(s_c["value_value"], 16)
                dve.tensor_scalar(headmean[:], headmean[:], 1.0 / S, None, ALU.mult)
                for c in range(C):
                    last = dve.tensor_scalar(bonus_w[:, c], same_head, vec[:, VEC["u"], c:c + 1], None, ALU.mult)
                last.then_inc(s_setup, 1)

            def ln_stats(b, src, loaded, bn6, mv, ve, s_bn, s_mv, s_ve):
                dve.wait_ge(*loaded)
                dve.bn_stats(bn6[:], src).then_inc(s_bn, 1)
                dve.wait_ge(s_bn, count(b, 1, 1))
                dve.memset(ve[:], 0.0)
                dve.bn_aggr(mv[:], bn6[:]).then_inc(s_mv, 1)
                dve.wait_ge(s_mv, count(b, 1, 1))
                dve.tensor_scalar(ve[:], mv[:, 1:2], EPS, None, ALU.add).then_inc(s_ve, 1)

            def stats1(b):
                ln_stats(b, x1[:, b[1]], (s_x1[b[1]], 16 * (b[0] + 1)), bn6, mv, ve, s_bn, s_mv, s_ve)

            def apply1(b):
                dve.wait_ge(s_rs, count(b, 1, 1))
                if at_least(b, 1):
                    dve.wait_ge(s_t1, count(later(b, -1), 1, 1))
                dve.tensor_scalar(ln_tok[:], x1[:, b[1]], mv[:, 0:1], rs[:, 0:1], ALU.subtract, ALU.mult).then_inc(s_ln, 1)

            def token_shift(b):
                dve.wait_ge(s_xa, count(b, 1, 1))
                dve.wait_ge(s_xa0, count(b, 1, 1))
                if at_least(b, 1):
                    dve.wait_ge(s_w1, count(later(b, -1), 1, 1))
                dve.tensor_tensor(sx[:], xa[:, :, 0:T], xa[:, :, 1:T + 1], ALU.subtract).then_inc(s_sx, 1)
                dve.wait_ge(s_sx, count(b, 1, 1))
                for c in range(C):
                    last = dve.scalar_tensor_tensor(out=xin[:, c], in0=sx[:, c], scalar=vec[:, VEC["maa_x"], c:c + 1],
                                                    in1=xa[:, c, 1:T + 1], op0=ALU.mult, op1=ALU.add)
                last.then_inc(s_xin, 1)

            def mix(b, f):
                dve.wait_ge(s_mixmm, count(b, MAA, f + 1))
                if f >= 2 or at_least(b, 1):
                    dve.wait_ge(s_xm, count(b, MAA, max(f - 1, 0)))
                src = pre_bank[MIX_BANK[f]]
                for c in range(C):
                    last = dve.scalar_tensor_tensor(out=mixed[:, f % 2, c], in0=src[:, c * T:(c + 1) * T],
                                                    scalar=vec[:, VEC[MIXES[f]], c:c + 1], in1=sx[:, c],
                                                    op0=ALU.add, op1=ALU.mult)
                last.then_inc(s_mixed, 1)

            def gate(b):
                dve.wait_ge(s_tg, count(b, 1, 1))
                if at_least(b, 2):
                    dve.wait_ge(s_gated, count(later(b, -2), 1, 1))
                dve.scalar_tensor_tensor(out=gate2[:, b[1]].rearrange("p c t -> p (c t)"), in0=tg[:].rearrange("p c t -> p (c t)"),
                                         scalar=1.0, in1=pre_bank[USE_BANK["g"]][:, 0:CT], op0=ALU.add, op1=ALU.mult).then_inc(s_g, 1)

            def key_value(m, j):
                if j % QUAD == 0:
                    r = j // QUAD
                    dve.wait_ge(s_vrep[r % 2], vrep_loads(m, r))
                if j == 0:
                    dve.wait_ge(s_k, count(m, 1, 1))
                if j >= NRING or at_least(m, 1):
                    dve.wait_ge(s_st, count(m, S, j - NRING + 1))
                src = vrep[:, j % NREP].rearrange("p (c t) -> p c t", c=C)
                dst = kv[:, j % NRING, 0:CT].rearrange("p (c t) -> p c t", c=C)
                dve.tensor_tensor(dst[:, :, 1:T], src[:, :, 0:T - 1], key[:, m[1], :, 0:T - 1], ALU.mult).then_inc(s_kv, 1)

            def scan(m, j):
                if j == 0:
                    dve.wait_ge(s_wdec, count(m, 1, 1))
                dve.wait_ge(s_kv, count(m, S, j + 1))
                dve.wait_ge(s_kv0, count(m, S, j + 1))
                if j >= NRING or at_least(m, 1):
                    if on_pool(j):
                        dve.wait_ge(s_pprod, count(m, POOL_PRODUCTS, products(j - NRING)[0]))
                    else:
                        dve.wait_ge(s_vprod, count(m, DVE_PRODUCTS, products(j - NRING)[1]))
                dve.tensor_tensor_scan(st[:, j % NRING], wdec[:, m[1]].rearrange("p c t -> p (c t)"), kv[:, j % NRING, 0:CT], 0.0,
                                       ALU.mult, ALU.add).then_inc(s_st, 1)

            def product(m, j):
                dve.wait_ge(s_st, count(m, S, j + 1))
                if j >= NPROD or at_least(m, 1):
                    dve.wait_ge(s_red, count(m, QUAD, (j - NPROD) // QUAD + 1))
                dve.tensor_tensor(rst[:, j % NPROD], st[:, j % NRING], rec[:, m[1]].rearrange("p c t -> p (c t)"),
                                  ALU.mult).then_inc(s_vprod, 1)

            def bonus_value(m):
                dve.wait_ge(s_bonus, count(m, 1, 1))
                if at_least(m, 1):
                    dve.wait_ge(s_wkv, count(later(m, -1), 1, 1))
                dve.tensor_tensor(bv[:].rearrange("p c t -> p (c t)"), post_bank[1][:, 0:CT],
                                  v[:, m[1]].rearrange("p c t -> p (c t)"), ALU.mult).then_inc(s_bv, 1)

            def wkv_sum(m):
                dve.wait_ge(s_red, count(m, QUAD, QUAD))
                dve.wait_ge(s_bv, count(m, 1, 1))
                if at_least(m, 1):
                    dve.wait_ge(s_cen, count(later(m, -1), 1, 1))
                dve.tensor_tensor(wkv[:].rearrange("p c t -> p (c t)"), out_bank[:, 0:CT], bv[:].rearrange("p c t -> p (c t)"),
                                  ALU.add).then_inc(s_wkv, 1)

            def centre(l):
                dve.wait_ge(s_mean, count(l, 1, 1))
                if at_least(l, 1):
                    dve.wait_ge(s_gaff, count(later(l, -1), 1, 1))
                dve.tensor_tensor(cen[:].rearrange("p c t -> p (c t)"), wkv[:].rearrange("p c t -> p (c t)"),
                                  post_bank[0][:, 0:CT], ALU.subtract).then_inc(s_cen, 1)

            def group_norm(l):
                dve.wait_ge(s_grs, count(l, 1, 1))
                dve.tensor_tensor(cen[:], cen[:], sq[:], ALU.mult).then_inc(s_gnorm, 1)

            def residual(l):
                dve.wait_ge(s_wo, count(l, 1, 1))
                dve.wait_ge(s_x1p[l[1]], 16 * (l[0] + 1))
                dve.tensor_tensor(x2[:], post_bank[0][0:T, :], x1p[:, l[1]], ALU.add).then_inc(s_x2, 1)
                ln_stats(l, x2[:], (s_x2, count(l, 1, 1)), bn6p, mvp, vep, s_bnp, s_mvp, s_vep)

            def apply2(l):
                dve.wait_ge(s_rsp, count(l, 1, 1))
                dve.tensor_scalar(ln2_tok[:], x2[:], mvp[:, 0:1], rsp[:, 0:1], ALU.subtract, ALU.mult).then_inc(s_lnp, 1)

            def shift2(l):
                dve.wait_ge(s_xc, count(l, 1, 1))
                dve.wait_ge(s_xc0, count(l, 1, 1))
                dve.tensor_tensor(sx2[:], xc[:, :, 0:T], xc[:, :, 1:T + 1], ALU.subtract).then_inc(s_sx2, 1)
                dve.wait_ge(s_sx2, count(l, 1, 1))
                for dst, name, ready in ((xk2, "ffn_k", s_xk2), (xr2, "ffn_r", s_xr2)):
                    for c in range(C):
                        last = dve.scalar_tensor_tensor(out=dst[:, c], in0=sx2[:, c], scalar=vec[:, VEC[name], c:c + 1],
                                                        in1=xc[:, c, 1:T + 1], op0=ALU.mult, op1=ALU.add)
                    last.then_inc(ready, 1)

            def finish(l):
                dve.wait_ge(s_fv, count(l, 1, 1))
                dve.wait_ge(s_rr, count(l, 1, 1))
                if at_least(l, 2):
                    dve.wait_ge(s_store[l[1]], 16 * l[0])
                dve.scalar_tensor_tensor(out=fin[:, l[1]], in0=trr[:], scalar=1.0, in1=post_bank[0][0:T, :], op0=ALU.add,
                                         op1=ALU.mult).then_inc(s_ff, 1)
                dve.wait_ge(s_ff, count(l, 1, 1))
                dve.scalar_tensor_tensor(out=fin[:, l[1]], in0=fin[:, l[1]], scalar=0.5, in1=x2[:], op0=ALU.mult,
                                         op1=ALU.add).then_inc(s_fin, 1)

            def step(n, pre, scans, post, first):
                m, l = later(n, -1), later(n, -2)
                if first:
                    stats1(n)
                    apply1(n)
                    token_shift(n)
                    setup()
                if is_batch(m, 0):
                    dve.wait_ge(s_zero, 3)
                for s in range(S):
                    if scans:
                        key_value(m, s)
                        if s >= 1 and not on_pool(s - 1):
                            product(m, s - 1)
                        scan(m, s)
                    if post and s == 2:
                        wkv_sum(l)
                        if at_least(n, 3):
                            finish(later(n, -3))
                    if scans and s == 2:
                        bonus_value(m)
                    if post and s == 3:
                        centre(l)
                    if pre and s in MIX_SLOT:
                        mix(n, MIX_SLOT.index(s))
                    if post and s == 5:
                        group_norm(l)
                    if post and s == 10:
                        residual(l)
                    if post and s == 11:
                        apply2(l)
                    if post and s == 13:
                        shift2(l)
                    if pre and s == 14:
                        gate(n)
                    if pre and not is_batch(n, B - 1):
                        if s == 11:
                            stats1(later(n, 1))
                        if s == 13:
                            apply1(later(n, 1))
                        if s == 15:
                            token_shift(later(n, 1))
                if scans:
                    product(m, S - 1)
                if is_batch(l, B - 1):
                    finish(l)

            run(dve, step)

        @block.scalar
        def _(act):
            act.wait_ge(s_zero, 3)

            def affine(dst, src, scale, bias):
                for c in range(C):
                    last = act.activation(dst(c), src(c), ACT.Identity, scale=scale[:, c:c + 1], bias=bias[:, c:c + 1])
                return last

            def xa_affine(b):
                act.wait_ge(s_t1, count(b, 1, 1))
                if at_least(b, 1):
                    act.wait_ge(s_xm, count(later(b, -1), MAA, MAA))
                affine(lambda c: xa[:, c, 1:T + 1], lambda c: pre_bank[0][:, c * T:(c + 1) * T], vec[:, VEC["ln1_w"]],
                       vec[:, VEC["ln1_b"]]).then_inc(s_xa, 1)

            def tanh_maa(b):
                act.wait_ge(s_w1, count(b, 1, 1))
                if at_least(b, 1):
                    act.wait_ge(s_mixmm, count(later(b, -1), MAA, MAA))
                act.activation(th[:, 0], pre_bank[1][:, 0:T], ACT.Tanh)
                act.activation(th[0:MD, 1], pre_bank[1][0:MD, T:2 * T], ACT.Tanh).then_inc(s_th, 1)

            def tanh_td(b):
                act.wait_ge(s_td1, count(b, 1, 1))
                if at_least(b, 1):
                    act.wait_ge(s_td2, count(later(b, -1), 1, 1))
                act.activation(ttd[0:TD], pre_bank[1][0:TD, 0:T], ACT.Tanh).then_inc(s_ttd, 1)

            def decay(b):
                act.wait_ge(s_td2, count(b, 1, 1))
                if at_least(b, 1):
                    act.wait_ge(s_wdec, count(later(b, -1), 1, 1))
                for c in range(C):
                    last = act.activation(etd[:, c], pre_bank[1][:, c * T:(c + 1) * T], ACT.Exp,
                                          bias=vec[:, VEC["time_decay"], c:c + 1])
                last.then_inc(s_etd, 1)
                act.wait_ge(s_etd, count(b, 1, 1))
                if at_least(b, 2):
                    act.wait_ge(s_st, count(later(b, -2), S, S))
                act.activation(wdec[:, b[1], :, 1:T], etd[:, :, 0:T - 1], ACT.Exp, scale=-1.0).then_inc(s_wdec, 1)

            def copy_value(b):
                act.wait_ge(s_vmm, count(b, 1, 1))
                if at_least(b, 2):
                    act.wait_ge(s_bv, count(later(b, -2), 1, 1))
                    act.wait_ge(s_vst[b[1]], 16 * b[0])
                src = pre_bank[USE_BANK["v"]][:, 0:CT]
                act.copy(v[:, b[1]].rearrange("p c t -> p (c t)"), src).then_inc(s_v, 1)

            def copy_key(b):
                act.wait_ge(s_kmm, count(b, 1, 1))
                if at_least(b, 2):
                    act.wait_ge(s_kv, count(later(b, -2), S, S))
                    act.wait_ge(s_rk, count(later(b, -2), 1, 1))
                act.copy(key[:, b[1]].rearrange("p c t -> p (c t)"), pre_bank[USE_BANK["k"]][:, 0:CT]).then_inc(s_k, 1)

            def copy_rec(b):
                act.wait_ge(s_rmm, count(b, 1, 1))
                if at_least(b, 2):
                    act.wait_ge(s_pprod, count(later(b, -2), POOL_PRODUCTS, POOL_PRODUCTS))
                    act.wait_ge(s_vprod, count(later(b, -2), DVE_PRODUCTS, DVE_PRODUCTS))
                act.copy(rec[:, b[1]].rearrange("p c t -> p (c t)"), pre_bank[USE_BANK["r"]][:, 0:CT]).then_inc(s_r, 1)

            def tanh_gate(b):
                act.wait_ge(s_gmm, count(b, 1, 1))
                if at_least(b, 1):
                    act.wait_ge(s_g, count(later(b, -1), 1, 1))
                act.activation(tg[:].rearrange("p c t -> p (c t)"), pre_bank[USE_BANK["g"]][:, 0:CT], ACT.Tanh,
                               scale=0.5).then_inc(s_tg, 1)

            def square(l):
                act.wait_ge(s_cen, count(l, 1, 1))
                if at_least(l, 1):
                    act.wait_ge(s_gated, count(later(l, -1), 1, 1))
                act.activation(sq[:], cen[:], ACT.Square).then_inc(s_sq, 1)

            def gn_rstd(l):
                act.wait_ge(s_var, count(l, 1, 1))
                flat = sq[:].rearrange("p c t -> p (c t)")
                act.activation(flat, post_bank[1][:, 0:CT], ACT.Ln, bias=ln_eps[:, 0:1]).then_inc(s_ln2, 1)
                act.wait_ge(s_ln2, count(l, 1, 1))
                act.activation(flat, flat, ACT.Exp, scale=-0.5).then_inc(s_grs, 1)

            def gn_affine(l):
                act.wait_ge(s_gnorm, count(l, 1, 1))
                affine(lambda c: sq[:, c], lambda c: cen[:, c], half_gn[:, 0], half_gn[:, 1]).then_inc(s_gaff, 1)

            def xc_affine(l):
                act.wait_ge(s_t2, count(l, 1, 1))
                if at_least(l, 1):
                    act.wait_ge(s_xr2, count(later(l, -1), 1, 1))
                affine(lambda c: xc[:, c, 1:T + 1], lambda c: post_bank[1][:, c * T:(c + 1) * T], vec[:, VEC["ln2_w"]],
                       vec[:, VEC["ln2_b"]]).then_inc(s_xc, 1)

            def relu_square(l):
                act.wait_ge(s_fk, count(l, 1, 1))
                if at_least(l, 1):
                    act.wait_ge(s_fv, count(later(l, -1), 1, 1))
                flat = kk[:].rearrange("p c t -> p (c t)")
                act.activation(flat, post_bank[0][:, 0:CT], ACT.Relu).then_inc(s_relu, 1)
                act.wait_ge(s_relu, count(l, 1, 1))
                act.activation(flat, flat, ACT.Square).then_inc(s_kk, 1)

            def receptance(l):
                act.wait_ge(s_fr, count(l, 1, 1))
                if at_least(l, 1):
                    act.wait_ge(s_ff, count(later(l, -1), 1, 1))
                act.activation(trr[:], post_bank[1][0:T, :], ACT.Tanh, scale=0.5).then_inc(s_rr, 1)

            def step(n, pre, scans, post, first):
                l = later(n, -2)
                if first:
                    xa_affine(n)
                if is_batch(l, 0):
                    act.wait_ge(s_setup, 1)
                if pre:
                    tanh_maa(n)
                if post:
                    square(l)
                    gn_rstd(l)
                if pre:
                    tanh_td(n)
                if post:
                    gn_affine(l)
                if pre:
                    decay(n)
                    copy_value(n)
                    copy_key(n)
                if post:
                    xc_affine(l)
                if pre:
                    copy_rec(n)
                    tanh_gate(n)
                if pre and not is_batch(n, B - 1):
                    xa_affine(later(n, 1))
                if post:
                    relu_square(l)
                    receptance(l)

            run(act, step)

        @block.tensor
        def _(pe):
            def wait_constants(b, *names):
                if is_batch(b, 0):
                    for name in names:
                        pe.wait_ge(s_c[name], 16 * MAA if name == "maa2" else 16)

            def transposes(dst, src):
                for c in range(C):
                    last = pe.transpose(dst[:, c * T:(c + 1) * T], src[:, c * P:(c + 1) * P], ident[0:T, 0:T])
                return last

            def channel_major(dst, w, src):
                for o in range(C):
                    for c in range(C):
                        last = pe.matmul(dst[:, o * T:(o + 1) * T], w[:, c, o * P:(o + 1) * P], src[:, c], start=(c == 0),
                                         stop=(c == C - 1))
                return last

            def token_major(dst, w, src):
                for c in range(C):
                    last = pe.matmul(dst[0:T, :], src[:, c], w[:, c], start=(c == 0), stop=(c == C - 1))
                return last

            def transpose_x(b):
                pe.wait_ge(s_ln, count(b, 1, 1))
                if at_least(b, 1):
                    pe.wait_ge(s_mixed, count(later(b, -1), MAA, MAA))
                transposes(pre_bank[0], ln_tok).then_inc(s_t1, 1)

            def maa_first(b):
                wait_constants(b, "maa1")
                pe.wait_ge(s_xin, count(b, 1, 1))
                if at_least(b, 1):
                    pe.wait_ge(s_r, count(later(b, -1), 1, 1))
                for o, (a, z) in enumerate(((0, P), (P, MAA * MD))):
                    for c in range(C):
                        last = pe.matmul(pre_bank[1][0:z - a, o * T:(o + 1) * T], maa1[:, c, a:z], xin[:, c], start=(c == 0),
                                         stop=(c == C - 1))
                last.then_inc(s_w1, 1)

            def maa_second(b, f):
                if f == 0:
                    if is_batch(b, 0):
                        pe.wait_ge(s_zero, 3)
                    wait_constants(b, "maa2")
                    pe.wait_ge(s_th, count(b, 1, 1))
                    if at_least(b, 1):
                        pe.wait_ge(s_g, count(later(b, -1), 1, 1))
                elif f == 1:
                    pe.wait_ge(s_xa, count(b, 1, 1))
                elif f == 2:
                    pe.wait_ge(s_mixed, count(b, MAA, 1))
                elif f == 3:
                    pe.wait_ge(s_etd, count(b, 1, 1))
                else:
                    pe.wait_ge(s_v, count(b, 1, 1))
                dst = pre_bank[MIX_BANK[f]]
                row = MIX_ROW[f]
                for o in range(C):
                    last = pe.matmul(dst[:, o * T:(o + 1) * T], maa2[:, row, o * P:(o + 1) * P], th[:, row // HG], start=True,
                                     stop=True)
                last.then_inc(s_mixmm, 1)

            def decay_first(b):
                wait_constants(b, "td1", "td2")
                pe.wait_ge(s_xm, count(b, MAA, 1))
                pe.wait_ge(s_th, count(b, 1, 1))
                for c in range(C):
                    last = pe.matmul(pre_bank[1][0:TD, 0:T], td1[:, c], xm[:, 0, c], start=(c == 0), stop=(c == C - 1))
                last.then_inc(s_td1, 1)

            def decay_second(b):
                pe.wait_ge(s_ttd, count(b, 1, 1))
                for o in range(C):
                    last = pe.matmul(pre_bank[1][:, o * T:(o + 1) * T], td2[:, o * P:(o + 1) * P], ttd[:], start=True, stop=True)
                last.then_inc(s_td2, 1)

            def weight(b, name):
                if is_batch(b, 0):
                    pe.wait_ge(w_loaded[name], 16)
                return W[name]

            def project(b, f, w, done):
                pe.wait_ge(s_xm, count(b, MAA, f + 1))
                if f < 4:
                    pe.wait_ge(s_mixed, count(b, MAA, f + 1))
                else:
                    pe.wait_ge(s_k, count(b, 1, 1))
                channel_major(pre_bank[USE_BANK[w[1]]], weight(b, w), xm[:, f % 2]).then_inc(done, 1)

            def bonus(m):
                if is_batch(m, 0):
                    pe.wait_ge(s_setup, 1)
                pe.wait_ge(s_rk, count(m, 1, 1))
                if at_least(m, 2):
                    pe.wait_ge(s_rr, count(later(m, -2), 1, 1))
                for c in range(C):
                    last = pe.matmul(post_bank[1][:, c * T:(c + 1) * T], bonus_w[:, c], rk[:, c], start=True, stop=True)
                last.then_inc(s_bonus, 1)

            def reduce(m, r):
                if r == 0:
                    wait_constants(m, "collect")
                by_pool, by_vector = products(QUAD * r + QUAD - 1)
                pe.wait_ge(s_pprod, count(m, POOL_PRODUCTS, by_pool))
                pe.wait_ge(s_vprod, count(m, DVE_PRODUCTS, by_vector))
                if r == 0 and at_least(m, 1):
                    pe.wait_ge(s_wkv, count(later(m, -1), 1, 1))
                for q in range(QUAD):
                    j = QUAD * r + q
                    last = pe.matmul(out_bank[q * (P // QUAD):(q + 1) * (P // QUAD), 0:CT], collect[:, j], rst[:, j % NPROD],
                                     start=(r == 0), stop=(r == QUAD - 1))
                last.then_inc(s_red, 1)

            def gn_mean(l):
                pe.wait_ge(s_wkv, count(l, 1, 1))
                if at_least(l, 1):
                    pe.wait_ge(s_ff, count(later(l, -1), 1, 1))
                pe.matmul(post_bank[0][:, 0:CT], headmean[:], wkv[:].rearrange("p c t -> p (c t)"), start=True,
                          stop=True).then_inc(s_mean, 1)

            def gn_var(l, scans):
                pe.wait_ge(s_sq, count(l, 1, 1))
                if scans:
                    pe.wait_ge(s_bv, count(later(l, 1), 1, 1))
                pe.matmul(post_bank[1][:, 0:CT], headmean[:], sq[:].rearrange("p c t -> p (c t)"), start=True,
                          stop=True).then_inc(s_var, 1)

            def step(n, pre, scans, post, first):
                m, l = later(n, -1), later(n, -2)
                if first:
                    transpose_x(n)
                    maa_first(n)
                for s in range(S):
                    if scans:
                        if s == 0:
                            bonus(m)
                        if s in REDUCE_SLOT:
                            reduce(m, REDUCE_SLOT.index(s))
                    if post and s == 3:
                        gn_mean(l)
                    if pre and s in MIX_SLOT:
                        maa_second(n, MIX_SLOT.index(s))
                    if post and s == 5:
                        gn_var(l, scans)
                    if pre and s == 6:
                        decay_first(n)
                    if pre and s == 7:
                        decay_second(n)
                    if pre and s == 7:
                        project(n, 1, "wv", s_vmm)
                    if post and s == 9:
                        pe.wait_ge(s_gated, count(l, 1, 1))
                        token_major(post_bank[0], weight(l, "wo"), gated).then_inc(s_wo, 1)
                    if pre and s == 9:
                        project(n, 2, "wk", s_kmm)
                    if post and s == 12:
                        pe.wait_ge(s_lnp, count(l, 1, 1))
                        transposes(post_bank[1], ln2_tok).then_inc(s_t2, 1)
                    if pre and s == 11:
                        project(n, 3, "wr", s_rmm)
                    if pre and s == 13:
                        project(n, 4, "wg", s_gmm)
                    if pre and s == 13 and not is_batch(n, B - 1):
                        transpose_x(later(n, 1))
                    if post and s == 13:
                        pe.wait_ge(s_xk2, count(l, 1, 1))
                        channel_major(post_bank[0], weight(l, "wfk"), xk2).then_inc(s_fk, 1)
                    if post and s == 14:
                        pe.wait_ge(s_xr2, count(l, 1, 1))
                        token_major(post_bank[1], weight(l, "wfr"), xr2).then_inc(s_fr, 1)
                    if post and s == 15:
                        pe.wait_ge(s_kk, count(l, 1, 1))
                        token_major(post_bank[0], weight(l, "wfv"), kk).then_inc(s_fv, 1)
                    if pre and s == 15 and not is_batch(n, B - 1):
                        maa_first(later(n, 1))
                if scans:
                    reduce(m, QUAD - 1)

            run(pe, step)


BLOCK_WEIGHTS = {"wr": "L1_xattn_Wr", "wk": "L1_xattn_Wk", "wv": "L1_xattn_Wv", "wg": "L1_xattn_Wg", "wo": "L1_xattn_Wo",
                 "wfk": "L1_xattn_Wfk", "wfr": "L1_xattn_Wfr", "wfv": "L1_xattn_Wfv"}
EARLY = ("wv", "wk")


def program(nc, A):
    with ExitStack() as ctx:
        W = {n: ctx.enter_context(nc.sbuf_tensor(f"b_{n}", [P, C, D], F32)) for n in EARLY}
        w_loaded = {n: ctx.enter_context(nc.semaphore(f"b_{n}_loaded")) for n in BLOCK_WEIGHTS}
        ident = ctx.enter_context(nc.sbuf_tensor("ident_sb", [P, P], F32))
        vec = ctx.enter_context(nc.sbuf_tensor("vec_sb", [P, len(VECTORS), C], F32))
        cross_attention(nc, A, ident, vec, W, w_loaded)
        rwkv_block(nc, A, ident, vec, W, w_loaded)


def kernel(**inputs):
    import numpy as _np
    import concourse.bacc as _bacc
    from concourse import mybir as _mybir
    from concourse.bass_utils import run_bass_kernel_spmd as _run

    a = {name: _np.asarray(x) for name, x in inputs.items()}

    def channels(x):
        return x.reshape(C, P).T

    def weights(w):
        return w.T.reshape(C, P, -1).transpose(1, 0, 2)

    x, ctx = a["x"], a["ctx_2048"]
    maa = dict(zip(("maa_k", "maa_w", "maa_v", "maa_r", "maa_g"), a["L1_xattn_maa_stack"].reshape(MAA, D)))
    vectors = {"ln_gamma": a["L0_xattn_ln_gamma"], "ln_beta": a["L0_xattn_ln_beta"], "ffn_k": a["L1_xattn_ffn_maa_k"],
               "ffn_r": a["L1_xattn_ffn_maa_r"], "u": a["L1_xattn_u"].reshape(D)} | maa
    p = _np.arange(P)
    key_head = p // S
    value_head, value_j = p % (P // S), QUAD * (p % (P // QUAD) // (P // S)) + p // (P // QUAD)
    value_order = (_np.arange(C)[:, None] * P + S * value_head + value_j).reshape(D)
    vectors |= {n: a["L1_xattn_" + n][value_order] for n in ("gn_w", "gn_b")}
    block = {n: a[source] for n, source in BLOCK_WEIGHTS.items()}
    block |= {"wv": block["wv"][value_order], "wg": block["wg"][value_order], "wo": block["wo"][:, value_order]}
    arrays = {
        "x": x,
        "xT": x.transpose(0, 2, 1).reshape(B, C, P, T).transpose(0, 2, 1, 3),
        "ctx": ctx,
        "mask": a["mask_BxS2_bf1"].view(_np.uint8),
        "vec": _np.stack([channels(vectors.get(n, a.get("L1_xattn_" + n))) for n in VECTORS], 1),
        "gate": a["L0_xattn_gate"].reshape(1, 1),
        "ident": _np.eye(P, dtype=_np.float32),
        "headmask": (p[:, None] // HD == _np.arange(HG)[None, :]).astype(_np.float32),
        "maa1": a["L1_xattn_maa_w1"].reshape(C, P, MAA * MD).transpose(1, 0, 2),
        "maa2": a["L1_xattn_maa_w2"],
        "td1": a["L1_xattn_td_w1"].reshape(C, P, TD).transpose(1, 0, 2),
        "td2": a["L1_xattn_td_w2"],
        "key_value": (key_head[:, None] == value_head[None, :]).astype(_np.float32),
        "value_value": (value_head[:, None] == value_head[None, :]).astype(_np.float32),
        "collect": _np.stack([((key_head[:, None] == value_head[None, q]) & (value_j[None, q] == n)).astype(_np.float32)
                              for n in range(S) for q in [slice(n % QUAD * (P // QUAD), (n % QUAD + 1) * (P // QUAD))]], 1),
        "s0": ctx[:, 2:2 + S].reshape(B, C, P, S).transpose(2, 0, 1, 3),
        "rows": ctx[:, 0:2].reshape(B, 2, C, P).transpose(3, 0, 1, 2),
    }
    arrays |= {n: weights(a["L0_xattn_W" + n[1:]]) for n in ("wq", "wk", "wv", "wo")}
    arrays |= {"b_" + n: weights(w) for n, w in block.items()}

    nc = _bacc.Bacc("TRN2", target_bir_lowering=False, num_devices=1)
    fed, A = {}, {}
    for name, array in arrays.items():
        fed[f"in_{name}"] = _np.ascontiguousarray(array)
        A[name] = nc.dram_tensor(f"in_{name}", array.shape, _mybir.dt.from_np(array.dtype), kind="ExternalInput").ap()
    A["x1"] = nc.dram_tensor("x1_between_layers", (B, T, D), F32, kind="Internal").ap()
    A["v"] = nc.dram_tensor("values_of_two_batches", (2, P, C * T), F32, kind="Internal").ap()
    A["out"] = nc.dram_tensor("out_dram", (B, T, D), F32, kind="ExternalOutput").ap()
    program(nc, A)
    return _run(nc, [fed], core_ids=[0]).results[0]["out_dram"]
```
